# Optimizing a Trainium2 kernel written in Bass

```python
import numpy as np
import jax
import jax.numpy as jnp

def _softmax(x, axis=-1):
    return jax.nn.softmax(x, axis=axis)
def _gelu(x):
    return jax.nn.gelu(x, approximate=True)
def _silu(x):
    return jax.nn.silu(x)
def _sigmoid(x):
    return jax.nn.sigmoid(x)
def _layernorm(x, axis=-1, eps=1e-5):
    m = jnp.mean(x, axis=axis, keepdims=True)
    v = jnp.var(x, axis=axis, keepdims=True)
    return (x - m) / jnp.sqrt(v + eps)
def _scatter_add(tgt, idx, src, axis=0):
    return tgt.at[idx].add(src)
def _segment_sum(src, seg, n):
    return jax.ops.segment_sum(src, seg, n)

kernel_name = 'mk_adj_preln_d2_adj_64_622b4e'

def setup_inputs(seed: int = 0):
    np.random.seed(seed)
    _w = jnp.asarray
    def _rec_inputs():
        import jax
        import jax.numpy as jnp
        _gk = jax.random.key(seed)
        x = -9.806e-05 + 1 * jax.random.normal(jax.random.fold_in(_gk, 1), (3327, 64), jnp.float32)
        _a = jax.random.bernoulli(jax.random.fold_in(_gk, 2), 0.00480914, (3327, 3327))
        _a = jnp.logical_or(_a, jnp.swapaxes(_a, -1, -2))
        _a = jnp.logical_or(_a, jnp.eye(3327, dtype=bool))
        _af = _a.astype(jnp.float32)
        adj = _af
        return x, adj
    x, adj = _rec_inputs()
    def _L0_gnn_setup():
        import jax, jax.numpy as jnp
        import numpy as np
        N, D_IN, D_OUT = (8192, 64, 64)
        MAX_NEIGH = 100
        DECAY = 0.5
        key = jax.random.key(seed)
        k1, k2, k3, k4 = jax.random.split(key, 4)
        stdv = 1.0 / np.sqrt(D_OUT)
        inputs = {'input': jax.random.normal(k1, (N, D_IN), dtype=jnp.float32), 'adj': jax.random.randint(k2, (N, N), 0, 2).astype(jnp.float32), 'weight': jax.random.uniform(k3, (D_IN, D_OUT), minval=-stdv, maxval=stdv, dtype=jnp.float32), 'bias': jax.random.uniform(k4, (D_OUT,), minval=-stdv, maxval=stdv, dtype=jnp.float32)}
        return inputs
    _L0_gnn_all = _L0_gnn_setup()
    _L0_gnn_in = {k: v for k, v in _L0_gnn_all.items() if k in ('weight', 'bias', )}
    del _L0_gnn_all

    def _L1_gnn_setup():
        import jax, jax.numpy as jnp
        import numpy as np
        N = 4096
        D = 64
        NUM_LAYERS = 2
        THETA0 = 0.000244
        THETA_MAX = 0.0003
        LAM = 0.1
        TAU = 1.0
        EPS = 1e-06
        H_DENSITY = 0.005

        def _safe_norm(x, axis):
            return jnp.sqrt(jnp.maximum(jnp.sum(x * x, axis=axis), 1e-16))

        def _layer(x, H, W, Theta, Wq, bq, Wv, bv, iteration):
            scale = D ** (-0.5)
            theta_base = THETA0 + (1.0 - np.exp(-LAM * iteration)) * (THETA_MAX - THETA0)
            th_comp = theta_base
            th_edge = min(theta_base, 0.8)
            th_node = min(theta_base, 0.7)
            structural = _safe_norm(x @ W, axis=1)
            Q = x @ Wq + bq
            V = x @ Wv + bv
            edge_feat = H.T @ V
            att = Q @ edge_feat.T * scale * H
            att = jax.nn.softmax(att, axis=1)
            att_scores = att.mean(axis=0)
            importance = 0.5 * structural + 0.5 * att_scores
            comp_scores = jax.nn.softmax(importance / TAU)
            comp_mask = comp_scores >= th_comp
            x_comp = x * comp_mask[:, None]
            nrm = jnp.maximum(_safe_norm(x_comp, axis=1), 1e-08)
            xn = x_comp / nrm[:, None]
            cos = xn @ xn.T
            edge_scores = jax.nn.softmax(cos * H / TAU, axis=1)
            edge_mask = (edge_scores >= th_edge) & comp_mask[:, None]
            H_pruned = H * edge_mask
            connectivity = H_pruned.sum(axis=1)
            feat_mag = _safe_norm(x_comp, axis=1)
            node_scores = jax.nn.softmax(connectivity * feat_mag / TAU)
            connected = (H_pruned * edge_mask).sum(axis=1) > 0
            node_mask = (node_scores >= th_node) & connected
            x_final = x_comp * node_mask[:, None]
            vdeg = jnp.maximum(H_pruned.sum(axis=1), EPS)
            edeg = jnp.maximum(H_pruned.sum(axis=0), EPS)
            dv_isqrt = 1.0 / jnp.sqrt(vdeg)
            de_inv = 1.0 / edeg
            transformed = x_final @ W
            agg = H_pruned.T * dv_isqrt[None, :] @ transformed
            agg = agg * de_inv[:, None]
            msg = dv_isqrt[:, None] * (H_pruned @ agg)
            msg = msg @ Theta
            return jax.nn.relu(msg)
        key = jax.random.key(seed)
        ks = jax.random.split(key, 8)
        xav = 0.125
        X = jax.random.normal(ks[0], (N, D), jnp.float32) * 0.05
        W = jax.random.normal(ks[1], (D, D), jnp.float32) * xav
        Theta = jax.random.normal(ks[2], (D, D), jnp.float32) * xav
        Wq = jax.random.normal(ks[3], (D, D), jnp.float32) * xav
        bq = jnp.zeros((D,), jnp.float32)
        Wv = jax.random.normal(ks[4], (D, D), jnp.float32) * xav
        bv = jnp.zeros((D,), jnp.float32)
        H = (jax.random.uniform(ks[7], (N, N)) < H_DENSITY).astype(jnp.float32)
        return {'X': X, 'W': W, 'Theta': Theta, 'Wq': Wq, 'bq': bq, 'Wv': Wv, 'bv': bv, 'H': H}
    _L1_gnn_all = _L1_gnn_setup()
    _L1_gnn_in = {k: v for k, v in _L1_gnn_all.items() if k in ('W', 'Theta', 'Wq', 'bq', 'Wv', 'bv', )}
    del _L1_gnn_all

    return {
        "x": x,
        "adj": adj,
        "L0_gnn_weight": _L0_gnn_in["weight"],
        "L0_gnn_bias": _L0_gnn_in["bias"],
        "L1_gnn_W": _L1_gnn_in["W"],
        "L1_gnn_Theta": _L1_gnn_in["Theta"],
        "L1_gnn_Wq": _L1_gnn_in["Wq"],
        "L1_gnn_bq": _L1_gnn_in["bq"],
        "L1_gnn_Wv": _L1_gnn_in["Wv"],
        "L1_gnn_bv": _L1_gnn_in["bv"],
    }

def reference(x, adj, L0_gnn_weight, L0_gnn_bias, L1_gnn_W, L1_gnn_Theta, L1_gnn_Wq, L1_gnn_bq, L1_gnn_Wv, L1_gnn_bv):
    import jax
    import jax.numpy as jnp
    def _L0_gnn_ref(input, adj, weight, bias):
        import jax, jax.numpy as jnp
        import numpy as np
        N, D_IN, D_OUT = (8192, 64, 64)
        MAX_NEIGH = 100
        DECAY = 0.5
        support = input @ weight
        mask = (adj != 0).astype(support.dtype)
        rank = jnp.cumsum(mask, axis=1)
        deg = rank[:, -1:]
        k = jnp.minimum(deg, float(MAX_NEIGH))
        pos = rank - (deg - k)
        w = mask * jnp.where(pos > 0, DECAY ** (k - pos), 0.0)
        out = w @ support + bias
        return out

    def _L1_gnn_ref(X, W, Theta, Wq, bq, Wv, bv, H):
        import jax, jax.numpy as jnp
        import numpy as np
        N = 4096
        D = 64
        NUM_LAYERS = 2
        THETA0 = 0.000244
        THETA_MAX = 0.0003
        LAM = 0.1
        TAU = 1.0
        EPS = 1e-06
        H_DENSITY = 0.005

        def _safe_norm(x, axis):
            return jnp.sqrt(jnp.maximum(jnp.sum(x * x, axis=axis), 1e-16))

        def _layer(x, H, W, Theta, Wq, bq, Wv, bv, iteration):
            scale = D ** (-0.5)
            theta_base = THETA0 + (1.0 - np.exp(-LAM * iteration)) * (THETA_MAX - THETA0)
            th_comp = theta_base
            th_edge = min(theta_base, 0.8)
            th_node = min(theta_base, 0.7)
            structural = _safe_norm(x @ W, axis=1)
            Q = x @ Wq + bq
            V = x @ Wv + bv
            edge_feat = H.T @ V
            att = Q @ edge_feat.T * scale * H
            att = jax.nn.softmax(att, axis=1)
            att_scores = att.mean(axis=0)
            importance = 0.5 * structural + 0.5 * att_scores
            comp_scores = jax.nn.softmax(importance / TAU)
            comp_mask = comp_scores >= th_comp
            x_comp = x * comp_mask[:, None]
            nrm = jnp.maximum(_safe_norm(x_comp, axis=1), 1e-08)
            xn = x_comp / nrm[:, None]
            cos = xn @ xn.T
            edge_scores = jax.nn.softmax(cos * H / TAU, axis=1)
            edge_mask = (edge_scores >= th_edge) & comp_mask[:, None]
            H_pruned = H * edge_mask
            connectivity = H_pruned.sum(axis=1)
            feat_mag = _safe_norm(x_comp, axis=1)
            node_scores = jax.nn.softmax(connectivity * feat_mag / TAU)
            connected = (H_pruned * edge_mask).sum(axis=1) > 0
            node_mask = (node_scores >= th_node) & connected
            x_final = x_comp * node_mask[:, None]
            vdeg = jnp.maximum(H_pruned.sum(axis=1), EPS)
            edeg = jnp.maximum(H_pruned.sum(axis=0), EPS)
            dv_isqrt = 1.0 / jnp.sqrt(vdeg)
            de_inv = 1.0 / edeg
            transformed = x_final @ W
            agg = H_pruned.T * dv_isqrt[None, :] @ transformed
            agg = agg * de_inv[:, None]
            msg = dv_isqrt[:, None] * (H_pruned @ agg)
            msg = msg @ Theta
            return jax.nn.relu(msg)
        x = X
        for it in range(NUM_LAYERS):
            x = _layer(x, H, W, Theta, Wq, bq, Wv, bv, it)
        return x

    h = jnp.maximum(_layernorm(x, axis=-1), 0.0)
    x = x + _L0_gnn_ref(h, adj, L0_gnn_weight, L0_gnn_bias)
    h = jnp.maximum(_layernorm(x, axis=-1), 0.0)
    x = x + _L1_gnn_ref(h, L1_gnn_W, L1_gnn_Theta, L1_gnn_Wq, L1_gnn_bq, L1_gnn_Wv, L1_gnn_bv, adj)
    return x


_drawn_inputs = setup_inputs


def setup_inputs(seed=0):
    import zlib

    import numpy as np

    out = dict(_drawn_inputs(seed))
    spreads = {'L1_gnn_bq': (0.0, 0.1), 'L1_gnn_bv': (0.0, 0.1)}
    factors = {'L1_gnn_W': 8.0, 'L1_gnn_Theta': 8.0, 'L1_gnn_Wq': 8.0}
    for name, (base, spread) in spreads.items():
        noise = np.random.default_rng([zlib.crc32(name.encode()), seed]).standard_normal(out[name].shape)
        drawn = base * np.exp(spread * noise) if base else spread * noise
        out[name] = jnp.asarray(drawn.astype(out[name].dtype))
    for name, factor in factors.items():
        out[name] = (out[name] * factor).astype(out[name].dtype)
    return out
```

```python
import concourse.bass as bass
from concourse import mybir
from contextlib import ExitStack


def bass_adj_preln_gnn_hypergraph(
    nc: bass.Bass,
    x: bass.AP,
    adj: bass.AP,
    l0_weight: bass.AP,
    l0_bias: bass.AP,
    W: bass.AP,
    Theta: bass.AP,
    Wq: bass.AP,
    bq: bass.AP,
    Wv: bass.AP,
    bv: bass.AP,
    out: bass.AP,
):
    F32 = mybir.dt.float32
    BF16 = mybir.dt.bfloat16
    FP16 = mybir.dt.float16
    FP8 = mybir.dt.float8e4
    U8 = mybir.dt.uint8
    I16 = mybir.dt.int16
    ALU = mybir.AluOpType
    ACT = mybir.ActivationFunctionType
    AX = mybir.AxisListType.X
    RMAX = bass.bass_isa.ReduceOp.max
    RADD = bass.bass_isa.ReduceOp.add

    N, D = x.shape
    P = 128
    B = (N + P - 1) // P
    NP = B * P
    LAST = N - (B - 1) * P
    PADCOLS = NP - N
    assert PADCOLS == 1 and B % 2 == 0
    LAYERS = 2
    LN_EPS = 1e-5
    EPS = 1e-6
    NORM_MIN = 1e-16
    MAX_NEIGH = 100
    TH = [0.000244, 0.000244 + (1.0 - 2.718281828459045 ** (-0.1)) * (0.0003 - 0.000244)]
    FAR = 1e30

    H_BYTE = 64.0
    H_FP8 = 2.0

    STEP = 128.0
    OWN = 128.0 * STEP
    W_BIAS = MAX_NEIGH * STEP - OWN
    SUP_SCALE = 2.0 ** (127 - MAX_NEIGH)

    SG = 6
    NSG = B // SG
    TAIL = B - NSG * SG
    assert TAIL == 2
    CHUNKS = [1, 1] + [2] * ((B - 2) // 2)
    NCH = len(CHUNKS)
    RING = NCH // 2
    CHUNK_AT = [sum(CHUNKS[:c]) for c in range(NCH)]
    CHUNK_OF = {CHUNK_AT[c] + k: c for c in range(NCH) for k in range(CHUNKS[c])}

    HALF = NP // 2
    HB = B // 2
    CW = NP // 8
    PW = 2 * CW
    PAIRS = NP // PW
    GROUPS = (B + 3) // 4

    COS_SCALE = 2.0 ** 15
    COS_UNIT = COS_SCALE * COS_SCALE
    MASK_OFF = -128.0 * COS_UNIT

    def group(g):
        return range(4 * g, min(4 * g + 4, B))

    ctx = ExitStack()
    with ctx:
        def sb(name, shape, dt):
            return ctx.enter_context(nc.sbuf_tensor(name, shape, dt))

        def sem(name):
            return ctx.enter_context(nc.semaphore(name))

        H = sb("H", [P, B, NP], U8)
        X = sb("X", [P, B, D], F32)
        FEAT = sb("FEAT", [P, B, D], F32)
        PARTS = sb("PARTS", [P, B, 3 * D], BF16)
        XTb = sb("XTb", [P, NP], F32)
        ATT1 = sb("ATT1", [P, NP], F32)
        ARENA = sb("ARENA", [P, 16384], F32)

        XT = XTb[0:D, :]
        DUP = XTb[:, :].rearrange("p (b d) -> p b d", b=B)
        ROWS = XTb[:, 0:2 * CW].rearrange("p (k c) -> p k c", k=2)
        TMP1 = ATT1[:, 0:B * D].rearrange("p (b d) -> p b d", b=B)
        TMP2 = ATT1[:, B * D:2 * B * D].rearrange("p (b d) -> p b d", b=B)

        at = [0]

        def carve(words, dt=F32):
            a = ARENA[:, at[0]:at[0] + words]
            at[0] += words
            return a if dt == F32 else a.bitcast(dt)

        FST = carve(RING * SG * 2 * P).rearrange("p (r b c) -> p r b c", r=RING, b=SG)
        HS = carve(SG * NP // 4, U8).rearrange("p (b c) -> p b c", b=SG)
        assert at[0] <= 16384
        HTILE = SG // 2 * P
        HTR = XTb[:, 0:2 * HTILE].bitcast(BF16).rearrange("p (h k c) -> p h k c", h=2, k=2)
        WTR = XTb[:, 2 * HTILE:4 * HTILE].bitcast(I16).rearrange("p (h k c) -> p h k c", h=2, k=2)
        SUM0 = XTb[:, 1600:1600 + SG * D].rearrange("p (b d) -> p b d", b=SG)
        SUM1 = XTb[:, 2000:2000 + SG * D].rearrange("p (b d) -> p b d", b=SG)

        at[0] = 0
        QA = carve(NP // 2, BF16)
        QB = carve(NP // 2, BF16)
        E11 = carve(NP // 2, BF16)
        E22 = carve(NP // 2, BF16)
        E31 = carve(NP // 2, BF16)
        ATT0 = carve(NP)
        XW = carve(B * D).rearrange("p (b d) -> p b d", b=B)
        HST = carve(2 * NP // 4, U8).rearrange("p (u c) -> p u c", u=2)
        assert at[0] <= 16384
        CA, C11, C22 = QA.bitcast(FP16), E11.bitcast(FP16), E22.bitcast(FP16)
        GST = QB.bitcast(U8).rearrange("p (u c) -> p u c", u=2)
        HPST = E31.bitcast(U8).rearrange("p (u c) -> p u c", u=2)
        ATT = [ATT0, ATT1[:, :]]
        HPT = [ATT0.bitcast(BF16)[:, 0:NP], ATT1[:, 0:NP // 2].bitcast(BF16)]

        PROW = sb("PROW", [P, 2, 3 * D + 1], BF16)
        JUNK = sb("JUNK", [P, HALF], U8)
        identF = sb("identF", [P, P], F32)
        half_ident = sb("half_ident", [P, P], BF16)
        ident = sb("ident", [P, P], BF16)
        mask_ident = sb("mask_ident", [P, P], BF16)
        count_first = sb("count_first", [P, P], BF16)
        count_next = sb("count_next", [P, P], BF16)
        zeros = sb("zeros", [P, 512], BF16)
        valid = sb("valid", [P, B], F32)
        far = sb("far", [P, B], F32)
        cast_by = sb("cast_by", [P, 1], F32)
        eps = sb("eps", [P, 3], F32)
        w0 = sb("w0", [D, D], F32)
        wwv = sb("wwv", [D, 2 * D], F32)
        wqq = sb("wqq", [D, 2 * D], F32)
        wth = sb("wth", [D, D], F32)
        b0 = sb("b0", [P, D], F32)
        bvb = sb("bvb", [P, D], F32)
        bqd = sb("bqd", [2 * D, 1], F32)
        (MEAN, VAR, STD, STR, DEG, OFF, COMP, IMP, EXPN, FMAG, CONN, NMASK, DV, EDEG, T_A, T_B) = [
            sb(n, [P, B], F32) for n in ("MEAN", "VAR", "STD", "STR", "DEG", "OFF", "COMP", "IMP", "EXPN",
                                         "FMAG", "CONN", "NMASK", "DV", "EDEG", "T_A", "T_B")]
        DEGH = sb("DEGH", [P, 2, B], F32)
        ATR = sb("ATR", [B, P], F32)
        MX = sb("MX", [P, 2, PAIRS], F32)
        NEGM = sb("NEGM", [P, 2], F32)
        ZROW = sb("ZROW", [P, 2], F32)
        RZ = sb("RZ", [P, 2], F32)
        RZT = sb("RZT", [P, 1], F32)
        ZC = sb("ZC", [P, 2, PAIRS], F32)
        ZS = sb("ZS", [P, 2], F32)
        THR = sb("THR", [P, 2], F32)
        CN = sb("CN", [P, 2], F32)
        G1 = sb("G1", [P, 8], F32)

        PS = ctx.enter_context(nc.psum_tensor("PS", [P, 8, 512], F32))

        att_dram = nc.dram_tensor("att_row", [NP], F32)
        att_rows = att_dram[:].rearrange("(k q c) -> q k c", k=2, q=4)
        att_back = att_dram[:].rearrange("(b p) -> b p", p=P)
        hp_dram = nc.dram_tensor("h_pruned", [B, P, NP], U8)

        weights_loaded = sem("weights_loaded")
        x_loaded = sem("x_loaded")
        pads_zeroed = sem("pads_zeroed")
        constants_ready = sem("constants_ready")
        vec_step = sem("vec_step")
        node_to_act = sem("node_to_act")
        node_from_act = sem("node_from_act")
        node_to_pool = sem("node_to_pool")
        node_from_pool = sem("node_from_pool")
        feat_ready = sem("feat_ready")
        xt_psum = sem("xt_psum")
        xt_ready = sem("xt_ready")
        prod_psum = sem("prod_psum")
        prod_evac = sem("prod_evac")
        q_psum = sem("q_psum")
        q_evac = sem("q_evac")
        support_ready = sem("support_ready")
        adj_loaded = [sem(f"adj_loaded{r}") for r in range(RING)]
        cast_done = sem("cast_done")
        kept = sem("kept")
        cols_used = sem("cols_used")
        ht_psum = sem("ht_psum")
        ht_ready = sem("ht_ready")
        count_ready = sem("count_ready")
        w_ready = sem("w_ready")
        acc_done = sem("acc_done")
        acc_free = sem("acc_free")
        l0_sum = sem("l0_sum")
        l0_biased = sem("l0_biased")
        parts_ready = sem("parts_ready")
        e_loaded = [sem(f"e_loaded{u}") for u in range(2)]
        e_row_ready = sem("e_row_ready")
        e_used = sem("e_used")
        e_counted = sem("e_counted")
        half_done = sem("half_done")
        half_evac = sem("half_evac")
        dup_ready = sem("dup_ready")
        dup_psum = sem("dup_psum")
        dup_evac = sem("dup_evac")
        stacks_ready = sem("stacks_ready")
        a_loaded = [sem(f"a_loaded{u}") for u in range(2)]
        s_psum = sem("s_psum")
        s_masked = sem("s_masked")
        max_ready = sem("max_ready")
        z_ready = sem("z_ready")
        rz_ready = sem("rz_ready")
        col_done = sem("col_done")
        rows_ready = sem("rows_ready")
        rows_stored = sem("rows_stored")
        rows_back = sem("rows_back")
        rows_psum = sem("rows_psum")
        c_loaded = [sem(f"c_loaded{u}") for u in range(2)]
        g_ready = sem("g_ready")
        cos_psum = sem("cos_psum")
        exp_done = sem("exp_done")
        zsum_done = sem("zsum_done")
        thr_done = sem("thr_done")
        hp_ready = sem("hp_ready")
        conn_done = sem("conn_done")
        hp_stored = [sem(f"hp_stored{u}") for u in range(2)]
        g_loaded = [sem(f"g_loaded{u}") for u in range(2)]
        g_row_ready = sem("g_row_ready")
        g_used = sem("g_used")
        m_loaded = [sem(f"m_loaded{u}") for u in range(2)]
        m_psum = sem("m_psum")
        m_vec = sem("m_vec")
        m_act = sem("m_act")
        msg_done = sem("msg_done")
        msg_taken = sem("msg_taken")
        out_stored = sem("out_stored")
        held = {e: sem("held_" + e) for e in ("pe", "act", "dve", "pool", "sp")}

        block = ctx.enter_context(nc.Block())

        def hold(eng, name, s, value):
            eng.wait_ge(s, value)
            eng.sem_inc(held[name])

        @block.sync
        def _(sp):
            for dst, src in ((w0[:, :], l0_weight), (wth[:, :], Theta), (wwv[:, 0:D], W), (wwv[:, D:2 * D], Wv),
                             (wqq[:, 0:D], Wq), (wqq[:, D:2 * D], Wq),
                             (b0[:, :], l0_bias.rearrange("(o d) -> o d", o=1).to_broadcast([P, D])),
                             (bvb[:, :], bv.rearrange("(o d) -> o d", o=1).to_broadcast([P, D])),
                             (bqd[0:D, :], bq.rearrange("(d o) -> d o", o=1)),
                             (bqd[D:2 * D, :], bq.rearrange("(d o) -> d o", o=1))):
                sp.dma_start(dst, src).then_inc(weights_loaded, 16)
            sp.dma_start(X[:, 0:B - 1, :],
                         x[0:(B - 1) * P, :].rearrange("(b p) d -> p b d", p=P)).then_inc(x_loaded, 16)
            sp.wait_ge(pads_zeroed, 1)
            sp.dma_start(X[0:LAST, B - 1, :], x[(B - 1) * P:N, :]).then_inc(x_loaded, 16)

            def cols(c):
                first = B - CHUNK_AT[c] - CHUNKS[c]
                lo = first * P
                return lo, min(N, lo + CHUNKS[c] * P) - lo

            with sp.Fori(0, NSG) as sg:
                for c in range(NCH):
                    lo, w = cols(c)
                    hold(sp, "sp", cast_done, sg * NCH + (c + 1))
                    sp.dma_start(FST[:, c % RING, :, 0:w],
                                 adj[bass.ds(sg * (SG * P), SG * P), lo:lo + w]
                                 .rearrange("(b p) c -> p b c", p=P)).then_inc(adj_loaded[c % RING], 16)
            for c in range(NCH):
                lo, w = cols(c)
                r0 = NSG * SG * P
                sp.wait_ge(cast_done, NSG * NCH + c + 1)
                sp.dma_start(FST[:, c % RING, 0, 0:w], adj[r0:r0 + P, lo:lo + w]).then_inc(adj_loaded[c % RING], 16)
                r0 += P
                sp.dma_start(FST[0:112, c % RING, 1, 0:w], adj[r0:r0 + 112, lo:lo + w]).then_inc(adj_loaded[c % RING], 16)
                sp.dma_start(FST[112:LAST, c % RING, 1, 0:w], adj[r0 + 112:N, lo:lo + w]).then_inc(adj_loaded[c % RING], 16)

            for L in range(LAYERS):
                sp.wait_ge(kept, NCH + (NSG + 1) * NCH)
                if L == 0:
                    sp.wait_ge(feat_ready, 2)
                else:
                    sp.wait_ge(m_psum, PAIRS + PAIRS * B * L)
                for hf in range(2):
                    with sp.Fori(0, HB) as n:
                        for u in range(2):
                            t = n * 2 + ((2 * L + hf) * B + u)
                            sp.wait_ge(e_used, t + 1)
                            hold(sp, "sp", e_counted, t + 1)
                            sp.dma_start(HST[:, u, 0:HALF],
                                         H[:, n * 2 + u, hf * HALF:(hf + 1) * HALF]).then_inc(e_loaded[u], 16)
                sp.wait_ge(e_used, 2 + 2 * B * (L + 1))
                sp.wait_ge(e_counted, 2 + 2 * B * (L + 1))
                with sp.Fori(0, HB) as n:
                    for u in range(2):
                        t = n * 2 + (L * B + u)
                        hold(sp, "sp", max_ready, t + 1)
                        sp.dma_start(HST[:, u, :], H[:, n * 2 + u, :]).then_inc(a_loaded[u], 16)
                sp.wait_ge(rows_ready, L + 1)
                for q in range(4):
                    sp.dma_start(att_rows[q:q + 1, :, :], ROWS[32 * q:32 * q + 1, :, :]).then_inc(rows_stored, 16)
                sp.wait_ge(rows_stored, 64 * (L + 1))
                sp.dma_start(ATR[:, :], att_back).then_inc(rows_back, 16)
                def load_c(i, t, u):
                    hold(sp, "sp", g_ready, t + 1)
                    sp.dma_start(HST[:, u, :], H[:, i, :]).then_inc(c_loaded[u], 16)

                def store_c(i, t, u):
                    hold(sp, "sp", hp_ready, t + 3)
                    sp.dma_start(hp_dram[i, :, :], HPST[:, u, :]).then_inc(hp_stored[u], 16)

                load_c(0, L * B, 0)
                load_c(1, L * B + 1, 1)
                with sp.Fori(0, HB - 1) as n:
                    for u in range(2):
                        store_c(n * 2 + u, n * 2 + (L * B + u), u)
                        load_c(n * 2 + (2 + u), n * 2 + (L * B + 2 + u), u)
                for u in range(2):
                    store_c(B - 2 + u, (L + 1) * B - 2 + u, u)
                for u in range(2):
                    sp.wait_ge(hp_stored[u], 16 + 16 * HB * (L + 1))
                for hf in range(2):
                    with sp.Fori(0, HB) as n:
                        for u in range(2):
                            t = n * 2 + ((2 * L + hf) * B + u)
                            hold(sp, "sp", g_used, t + 1)
                            sp.dma_start(HST[:, u, 0:HALF],
                                         hp_dram[n * 2 + u, :, hf * HALF:(hf + 1) * HALF]).then_inc(g_loaded[u], 16)
                sp.wait_ge(g_used, 2 + 2 * B * (L + 1))
                with sp.Fori(0, HB) as n:
                    for u in range(2):
                        t = n * 2 + (L * B + u)
                        hold(sp, "sp", m_psum, t * PAIRS + PAIRS - 4 + 1)
                        sp.dma_start(HST[:, u, :], hp_dram[n * 2 + u, :, :]).then_inc(m_loaded[u], 16)
            sp.wait_ge(feat_ready, 2 + 2 * LAYERS)
            sp.dma_start(out[0:(B - 1) * P, :].rearrange("(b p) d -> p b d", p=P), X[:, 0:B - 1, :]).then_inc(out_stored, 16)
            sp.dma_start(out[(B - 1) * P:N, :], X[0:LAST, B - 1, :]).then_inc(out_stored, 16)
            sp.wait_ge(out_stored, 32)

        @block.gpsimd
        def _(pool):
            step = [0]

            def link(ins):
                step[0] += 1
                ins.then_inc(constants_ready, 1)
                pool.wait_ge(constants_ready, step[0])

            pool.sem_inc(cast_done, RING)
            pool.sem_inc(kept, NCH)
            pool.sem_inc(g_ready, 2)
            nc.gpsimd.memset(X[:, B - 1, :], 0.0).then_inc(pads_zeroed, 1)
            link(nc.gpsimd.memset(H[:, :, N:NP], 0))
            link(nc.gpsimd.memset(HS[:, :, N:NP], 0))
            link(nc.gpsimd.memset(PROW[:, :, 3 * D:3 * D + 1], 1.0))
            link(nc.gpsimd.memset(zeros[:, :], 0.0))
            link(nc.gpsimd.memset(eps[:, 0:1], LN_EPS))
            link(nc.gpsimd.memset(eps[:, 1:2], 0.0))
            link(nc.gpsimd.memset(eps[:, 2:3], W_BIAS))
            link(nc.gpsimd.memset(valid[:, :], 1.0))
            link(nc.gpsimd.affine_select(out=valid[:, :], in_=valid[:, :], compare_op=ALU.is_gt, fill=0.0, base=N,
                                         pattern=[[-P, B]], channel_multiplier=-1))
            link(nc.gpsimd.tensor_scalar(cast_by[:, :], valid[:, B - 1:B], H_BYTE, 0.0, ALU.mult, ALU.add))
            link(nc.gpsimd.tensor_scalar(far[:, :], valid[:, :], FAR, -FAR, ALU.mult, ALU.add))
            for m, rest, diag in ((identF, 0.0, 1.0), (ident, 0.0, 1.0), (half_ident, 0.0, 1.0 / H_FP8),
                                  (mask_ident, 0.0, MASK_OFF)):
                link(nc.gpsimd.memset(m[:, :], rest))
                link(nc.gpsimd.affine_select(out=m[:, :], in_=m[:, :], compare_op=ALU.not_equal, fill=diag, base=0,
                                             pattern=[[-1, P]], channel_multiplier=1))
            for m, sign, diag in ((count_first, 1, OWN), (count_next, -1, -OWN - STEP)):
                link(nc.gpsimd.memset(m[:, :], -STEP))
                link(nc.gpsimd.affine_select(out=m[:, :], in_=m[:, :], compare_op=ALU.is_gt, fill=0.0, base=0,
                                             pattern=[[-sign, P]], channel_multiplier=sign))
                link(nc.gpsimd.affine_select(out=m[:, :], in_=m[:, :], compare_op=ALU.not_equal, fill=diag, base=0,
                                             pattern=[[-1, P]], channel_multiplier=1))
            assert step[0] == CONSTANTS

            def cast(sg, c, nb):
                n = sg * NCH + (c + 1)
                lo = (B - CHUNK_AT[c] - CHUNKS[c]) * P
                w = min(N, lo + CHUNKS[c] * P) - lo
                if nb == SG:
                    pool.wait_ge(adj_loaded[c % RING], sg * 32 + 16 * (c // RING + 1))
                else:
                    pool.wait_ge(adj_loaded[c % RING], NSG * 32 + 48 * (c // RING + 1))
                pool.wait_ge(kept, n)
                hold(pool, "pool", cols_used, n)
                if nb == SG:
                    nc.gpsimd.tensor_scalar(HS[:, :, lo:lo + w], FST[:, c % RING, :, 0:w], H_BYTE, 1.0,
                                            ALU.mult, ALU.mult).then_inc(cast_done, 1)
                else:
                    nc.gpsimd.tensor_scalar(HS[:, 0, lo:lo + w], FST[:, c % RING, 0, 0:w], H_BYTE, 1.0,
                                            ALU.mult, ALU.mult)
                    nc.gpsimd.tensor_scalar(HS[:, 1, lo:lo + w], FST[:, c % RING, 1, 0:w], cast_by[:, 0:1], 1.0,
                                            ALU.mult, ALU.mult).then_inc(cast_done, 1)
                hold(pool, "pool", cast_done, n + RING)
                nc.gpsimd.tensor_copy(H[:, bass.ds(sg * SG, nb), lo:lo + w],
                                      HS[:, 0:nb, lo:lo + w]).then_inc(kept, 1)

            with pool.Fori(0, NSG) as sg:
                for c in range(NCH):
                    cast(sg, c, SG)
            for c in range(NCH):
                cast(NSG, c, TAIL)

            def rows(L, hf, loaded_by_parts, ready, used):
                with pool.Fori(0, HB) as n:
                    for u in range(2):
                        t = n * 2 + ((2 * L + hf) * B + u)
                        hold(pool, "pool", used, t + 1)
                        nc.gpsimd.tensor_copy(PROW[:, u, 0:3 * D], PARTS[:, n * 2 + u, :]).then_inc(ready, 1)

            def across(k, src, dst, op):
                pool.wait_ge(node_to_pool, k)
                nc.gpsimd.partition_all_reduce(dst, src, P, op).then_inc(node_from_pool, 1)

            for L in range(LAYERS):
                pool.wait_ge(parts_ready, 3 * L + 1)
                for hf in range(2):
                    rows(L, hf, None, e_row_ready, e_used)
                across(4 * L + 1, G1[:, 0:1], G1[:, 1:2], RMAX)
                across(4 * L + 2, G1[:, 2:3], G1[:, 3:4], RADD)
                with pool.Fori(0, HB) as n:
                    for u in range(2):
                        t = n * 2 + (L * B + u)
                        pool.wait_ge(c_loaded[u], (n + (L * HB + 1)) * 16)
                        hold(pool, "pool", hp_ready, t + 1)
                        nc.gpsimd.tensor_scalar(GST[:, u, :], HST[:, u, :], -1.0, H_BYTE,
                                                ALU.mult, ALU.add).then_inc(g_ready, 1)
                across(4 * L + 3, G1[:, 4:5], G1[:, 5:6], RMAX)
                across(4 * L + 4, G1[:, 6:7], G1[:, 7:8], RADD)
                pool.wait_ge(parts_ready, 3 * L + 2)
                for hf in range(2):
                    rows(L, hf, None, g_row_ready, g_used)

        @block.scalar
        def _(act):
            act.sem_inc(e_counted, 2)
            act.sem_inc(exp_done, PAIRS)
            act.sem_inc(m_act, 1)
            act.wait_ge(constants_ready, CONSTANTS)
            small = [0]

            def asked(o, i, func, **kw):
                small[0] += 1
                act.wait_ge(node_to_act, small[0])
                nc.scalar.activation(o, i, func, **kw).then_inc(node_from_act, 1)

            asked(STD[:, :], VAR[:, :], ACT.Sqrt, scale=1.0 / D, bias=eps[:, 0:1])

            def exponents(sg, nb):
                w = nb // 2 * P
                for s in range(B):
                    for h in range(2):
                        act.wait_ge(acc_done, sg * B + (s + 1))
                        hold(act, "act", count_ready, sg * (2 * B) + (2 * s + h + 3))
                        nc.scalar.activation(WTR[:, h, s % 2, 0:w], PS[:, 2 + h, 0:w], ACT.Relu,
                                             bias=eps[:, 2:3]).then_inc(w_ready, 1)

            with act.Fori(0, NSG) as sg:
                exponents(sg, SG)
            exponents(NSG, TAIL)

            for L in range(LAYERS):
                if L == 0:
                    asked(STD[:, :], VAR[:, :], ACT.Sqrt, scale=1.0 / D, bias=eps[:, 0:1])
                asked(STR[:, :], T_A[:, :], ACT.Sqrt)
                for hf in range(2):
                    with act.Fori(0, HB) as n:
                        for u in range(2):
                            t = n * 2 + ((2 * L + hf) * B + u)
                            act.wait_ge(e_counted, t + 2)
                            hold(act, "act", e_loaded[u], (n + ((2 * L + hf) * HB + 1)) * 16)
                            nc.scalar.activation(JUNK[:, :], HST[:, u, 0:HALF], ACT.Copy,
                                                 accum_out=DEGH[:, hf, bass.ds(n * 2 + u, 1)]).then_inc(e_counted, 1)
                with act.Fori(0, HB) as n:
                    for u in range(2):
                        t = n * 2 + (L * B + u)
                        hold(act, "act", max_ready, t + 3)
                        nc.scalar.activation(ATT[u][:, 0:N], ATT[u][:, 0:N], ACT.Exp, bias=NEGM[:, u:u + 1],
                                             accum_out=ZROW[:, u:u + 1]).then_inc(z_ready, 1)
                asked(EXPN[:, :], IMP[:, :], ACT.Exp, bias=G1[:, 1:2], accum_out=G1[:, 2:3])
                asked(FMAG[:, :], T_A[:, :], ACT.Sqrt)
                with act.Fori(0, HB) as n:
                    for u in range(2):
                        for q in range(PAIRS):
                            t = n * 2 + (L * B + u)
                            if q == 0:
                                act.wait_ge(hp_ready, t + 1)
                            hold(act, "act", cos_psum, t * PAIRS + (q + 1))
                            nc.scalar.activation(ATT[u][:, q * PW:(q + 1) * PW].rearrange("p (k c) -> p k c", k=2),
                                                 PS[:, 2 * q:2 * q + 2, 0:CW], ACT.Exp, scale=1.0 / COS_UNIT,
                                                 accum_out=ZC[:, u, q:q + 1]).then_inc(exp_done, 1)
                asked(EXPN[:, :], IMP[:, :], ACT.Exp, bias=G1[:, 5:6], accum_out=G1[:, 6:7])
                asked(DV[:, :], T_A[:, :], ACT.Sqrt)
                with act.Fori(0, HB) as n:
                    for u in range(2):
                        t = n * 2 + (L * B + u)
                        act.wait_ge(msg_done, t + 1)
                        for g in (1, 3):
                            w = min(8 * P, NP - 8 * P * g)
                            hold(act, "act", m_psum, t * PAIRS + (g + 1 + PAIRS))
                            nc.scalar.activation(HPT[u][:, 8 * P * g:8 * P * g + w],
                                                 PS[:, 2:4, :].rearrange("p k c -> p (k c)")[:, 0:w],
                                                 ACT.Copy).then_inc(m_act, 1)

        @block.vector
        def _(dve):
            chain = [0]

            def link(ins):
                chain[0] += 1
                ins.then_inc(vec_step, 1)
                dve.wait_ge(vec_step, chain[0])

            asks, sums, feats, xts, prods = [0], [0], [0], [0], [0]

            def ask(ins):
                asks[0] += 1
                ins.then_inc(node_to_act, 1)
                dve.wait_ge(node_from_act, asks[0])

            def across(ins):
                sums[0] += 1
                ins.then_inc(node_to_pool, 1)
                dve.wait_ge(node_from_pool, sums[0])

            def per_node(v):
                return v[:, :].unsqueeze(2).to_broadcast([P, B, D])

            def layernorm_relu():
                link(nc.vector.tensor_reduce(MEAN[:, :], X[:, :, :], AX, ALU.add))
                link(nc.vector.tensor_scalar(MEAN[:, :], MEAN[:, :], 1.0 / D, None, ALU.mult))
                link(nc.vector.tensor_tensor(TMP1, X[:, :, :], per_node(MEAN), ALU.subtract))
                link(nc.vector.tensor_tensor(TMP2, TMP1, TMP1, ALU.mult))
                ask(nc.vector.tensor_reduce(VAR[:, :], TMP2, AX, ALU.add))
                link(nc.vector.reciprocal(STD[:, :], STD[:, :]))
                link(nc.vector.tensor_tensor(TMP1, TMP1, per_node(STD), ALU.mult))
                nc.vector.tensor_scalar(FEAT[:, :, :], TMP1, 0.0, None, ALU.max).then_inc(feat_ready, 1)

            def features_out():
                for g in range(GROUPS):
                    w = len(group(g)) * P
                    xts[0] += 1
                    dve.wait_ge(xt_psum, xts[0])
                    nc.vector.tensor_copy(XT[:, 4 * P * g:4 * P * g + w], PS[0:D, g, 0:w]).then_inc(xt_ready, 1)

            def products():
                for g in range(GROUPS):
                    prods[0] += 1
                    dve.wait_ge(prod_psum, prods[0])
                    yield g, 4 * g, 4 * g + len(group(g))

            def split3(src, rest, parts):
                link(nc.vector.tensor_copy(parts[:, :, 0:D], src))
                link(nc.vector.tensor_tensor(rest, src, parts[:, :, 0:D], ALU.subtract))
                link(nc.vector.tensor_copy(parts[:, :, D:2 * D], rest))
                link(nc.vector.tensor_tensor(rest, rest, parts[:, :, D:2 * D], ALU.subtract))
                return nc.vector.tensor_copy(parts[:, :, 2 * D:3 * D], rest)

            def half_out(L, hf, k, width, dst, degrees):
                dve.wait_ge(half_done, k)
                for bank in range((HB + 1) // 2):
                    nb = min(2, HB - 2 * bank)
                    b = hf * HB + 2 * bank
                    src = PS[:, bank, 0:nb * width].rearrange("p (b c) -> p b c", b=nb)
                    if degrees:
                        nc.vector.tensor_copy(EDEG[:, b:b + nb], src[:, :, 3 * D])
                    last = nc.vector.tensor_reduce(dst[:, b:b + nb, 0:D],
                                                   src[:, :, 0:3 * D].rearrange("p b (t d) -> p b d t", t=3), AX, ALU.add)
                last.then_inc(half_evac, 1)

            def doubled_out(k, scale):
                for g in range(GROUPS):
                    w = len(group(g)) * P
                    dve.wait_ge(dup_psum, GROUPS * (k - 1) + g + 1)
                    nc.vector.tensor_scalar(ATT0[:, 4 * P * g:4 * P * g + w], PS[:, g, 0:w], scale, None,
                                            ALU.mult).then_inc(dup_evac, 1)
                dve.wait_ge(dup_evac, GROUPS * k)

            dve.sem_inc(ht_ready, 2)
            dve.sem_inc(acc_free, 1)
            dve.sem_inc(s_masked, 2)
            dve.sem_inc(max_ready, 2)
            dve.sem_inc(hp_ready, 2)
            dve.sem_inc(hp_stored[0], 16)
            dve.sem_inc(hp_stored[1], 16)
            dve.sem_inc(m_vec, 1)
            dve.sem_inc(msg_taken, 2)

            dve.wait_ge(x_loaded, 32)
            dve.wait_ge(constants_ready, CONSTANTS)
            dve.wait_ge(weights_loaded, 160)
            layernorm_relu()
            features_out()
            for g, lo, hi in products():
                nc.vector.tensor_scalar(TMP1[:, lo:hi, :], PS[:, g, 0:(hi - lo) * D].rearrange("p (b d) -> p b d", d=D),
                                        SUP_SCALE, None, ALU.mult).then_inc(prod_evac, 1)
            dve.wait_ge(prod_evac, prods[0])
            split3(TMP1, TMP2, PARTS[:, :, :]).then_inc(support_ready, 1)
            dve.wait_ge(support_ready, 1)

            def l0_tiles(sg, nb):
                w = nb // 2 * P
                for s in range(B):
                    for h in range(2):
                        n = sg * (2 * B) + (2 * s + h + 1)
                        dve.wait_ge(count_ready, n)
                        hold(dve, "dve", ht_psum, n)
                        nc.vector.tensor_copy(HTR[:, h, s % 2, 0:w], PS[:, h, 0:w]).then_inc(ht_ready, 1)
                hold(dve, "dve", acc_done, sg * B + (B + 2))
                for k in range(nb // 2):
                    last = nc.vector.tensor_reduce(
                        SUM0[:, 2 * k:2 * k + 2, :],
                        PS[:, 4 + k, 0:2 * 3 * D].rearrange("p (b t d) -> p b d t", b=2, t=3), AX, ALU.add)
                last.then_inc(acc_free, 1)
                hold(dve, "dve", acc_free, sg + 2)
                nc.vector.tensor_tensor(SUM1[:, 0:nb, :], SUM0[:, 0:nb, :],
                                        b0[:, :].unsqueeze(1).to_broadcast([P, nb, D]), ALU.add).then_inc(l0_biased, 1)
                hold(dve, "dve", l0_biased, sg + 1)
                rows = X[:, bass.ds(sg * SG, nb), :]
                nc.vector.tensor_tensor(rows, rows, SUM1[:, 0:nb, :], ALU.add).then_inc(l0_sum, 1)

            with dve.Fori(0, NSG) as sg:
                l0_tiles(sg, SG)
            l0_tiles(NSG, TAIL)
            dve.wait_ge(l0_sum, NSG + 1)
            dve.wait_ge(kept, NCH * (NSG + 2))

            for L in range(LAYERS):
                if L == 0:
                    layernorm_relu()
                features_out()
                for g, lo, hi in products():
                    src = PS[:, g, 0:(hi - lo) * 2 * D].rearrange("p (b c) -> p b c", c=2 * D)
                    nc.vector.tensor_copy(XW[:, lo:hi, :], src[:, :, 0:D])
                    nc.vector.tensor_tensor(TMP1[:, lo:hi, :], src[:, :, D:2 * D],
                                            bvb[:, :].unsqueeze(1).to_broadcast([P, hi - lo, D]),
                                            ALU.add).then_inc(prod_evac, 1)
                dve.wait_ge(prod_evac, prods[0])
                split3(TMP1, TMP2, PARTS[:, :, :]).then_inc(parts_ready, 1)
                dve.wait_ge(parts_ready, 3 * L + 1)
                link(nc.vector.tensor_tensor(TMP1, XW, XW, ALU.mult))
                link(nc.vector.tensor_reduce(T_A[:, :], TMP1, AX, ALU.add))
                ask(nc.vector.tensor_scalar(T_A[:, :], T_A[:, :], NORM_MIN, None, ALU.max))
                for g in range(GROUPS):
                    w = len(group(g)) * P
                    dve.wait_ge(q_psum, GROUPS * L + g + 1)
                    nc.vector.tensor_scalar(ATT0[:, 4 * P * g:4 * P * g + w], PS[:, g, 0:w], bqd[:, 0:1],
                                            D ** -0.5 / H_BYTE, ALU.add, ALU.mult).then_inc(q_evac, 1)
                dve.wait_ge(q_evac, GROUPS * (L + 1))
                REST = ATT1[:, :]
                link(nc.vector.tensor_copy(QA, ATT0))
                link(nc.vector.tensor_tensor(REST, ATT0, QA, ALU.subtract))
                link(nc.vector.tensor_copy(QB, REST))
                link(nc.vector.tensor_tensor(REST, REST, QB, ALU.subtract))
                link(nc.vector.tensor_copy(QA[D:2 * D, :], QB[D:2 * D, :]))
                link(nc.vector.tensor_copy(QB[D:2 * D, :], REST[D:2 * D, :]))
                link(nc.vector.tensor_copy(QB[0:D, :], QA[0:D, :]))

                for hf in range(2):
                    half_out(L, hf, 4 * L + hf + 1, 3 * D, DUP, False)
                dve.wait_ge(half_evac, 4 * L + 2)
                nc.vector.tensor_copy(DUP[:, :, D:2 * D], DUP[:, :, 0:D]).then_inc(dup_ready, 1)
                doubled_out(2 * L + 1, 1.0 / H_FP8)
                link(nc.vector.tensor_copy(E11, ATT0))
                link(nc.vector.tensor_tensor(REST, ATT0, E11, ALU.subtract))
                link(nc.vector.tensor_copy(E22, REST))
                link(nc.vector.tensor_tensor(REST, REST, E22, ALU.subtract))
                link(nc.vector.tensor_copy(E31[0:D, :], REST[0:D, :]))
                nc.vector.tensor_copy(E31[D:2 * D, :], E11[D:2 * D, :]).then_inc(stacks_ready, 1)
                dve.wait_ge(stacks_ready, 2 * L + 1)

                def masked(m, u, t):
                    dve.wait_ge(a_loaded[u], (m + (L * HB + 1)) * 16)
                    dve.wait_ge(col_done, t + 1)
                    for q in range(PAIRS):
                        hold(dve, "dve", s_psum, t * PAIRS + (q + 1))
                        nc.vector.tensor_tensor_reduce(
                            out=ATT[u][:, q * PW:(q + 1) * PW].rearrange("p (k c) -> p k c", k=2),
                            in0=PS[:, 2 * (q % 2):2 * (q % 2) + 2, 0:CW],
                            in1=HST[:, u, q * PW:(q + 1) * PW].rearrange("p (k c) -> p k c", k=2),
                            scale=1.0, scalar=-3e38, op0=ALU.mult, op1=ALU.max,
                            accum_out=MX[:, u, q:q + 1]).then_inc(s_masked, 1)
                    hold(dve, "dve", s_masked, t * PAIRS + (PAIRS + 2))
                    nc.vector.tensor_reduce(NEGM[:, u:u + 1], MX[:, u, :], AX, ALU.max, negate=True).then_inc(max_ready, 1)

                def weight(u, t):
                    hold(dve, "dve", z_ready, t + 1)
                    nc.vector.reciprocal(RZ[:, u:u + 1], ZROW[:, u:u + 1]).then_inc(rz_ready, 1)

                masked(0, 0, L * B)
                with dve.Fori(0, HB - 1) as n:
                    for u in range(2):
                        t = n * 2 + (L * B + u)
                        masked(n + u, 1 - u, t + 1)
                        weight(u, t)
                t = (L + 1) * B - 2
                masked(HB - 1, 1, t + 1)
                weight(0, t)
                dve.wait_ge(z_ready, t + 2)
                link(nc.vector.reciprocal(RZT[:, :], ZROW[:, 1:2]))
                nc.vector.tensor_scalar(RZ[:, 1:2], RZT[:, :], valid[:, B - 1:B], None, ALU.mult).then_inc(rz_ready, 1)
                dve.wait_ge(col_done, 2 + B * (L + 1))
                nc.vector.tensor_scalar(ROWS, PS[:, 4:6, 0:CW], 1.0 / N, None, ALU.mult).then_inc(rows_ready, 1)

                dve.wait_ge(rows_psum, L + 1)
                link(nc.vector.tensor_scalar(T_A[:, :], PS[:, 6, 0:B], 0.5, None, ALU.mult))
                link(nc.vector.tensor_scalar(IMP[:, :], STR[:, :], 0.5, None, ALU.mult))
                link(nc.vector.tensor_tensor(IMP[:, :], IMP[:, :], T_A[:, :], ALU.add))

                def node_softmax(g, dst):
                    link(nc.vector.tensor_tensor(IMP[:, :], IMP[:, :], valid[:, :], ALU.mult))
                    link(nc.vector.tensor_tensor(IMP[:, :], IMP[:, :], far[:, :], ALU.add))
                    across(nc.vector.tensor_reduce(G1[:, g:g + 1], IMP[:, :], AX, ALU.max))
                    ask(nc.vector.tensor_scalar(G1[:, g + 1:g + 2], G1[:, g + 1:g + 2], -1.0, None, ALU.mult))
                    across(nc.vector.tensor_copy(G1[:, g + 2:g + 3], G1[:, g + 2:g + 3]))
                    link(nc.vector.tensor_scalar(G1[:, g + 3:g + 4], G1[:, g + 3:g + 4], TH[L], None, ALU.mult))
                    link(nc.vector.tensor_scalar(dst, EXPN[:, :], G1[:, g + 3:g + 4], None, ALU.is_ge))

                node_softmax(0, COMP[:, :])

                link(nc.vector.tensor_tensor(TMP1, FEAT[:, :, :], per_node(COMP), ALU.mult))
                link(nc.vector.tensor_tensor(TMP2, TMP1, TMP1, ALU.mult))
                link(nc.vector.tensor_reduce(T_A[:, :], TMP2, AX, ALU.add))
                ask(nc.vector.tensor_scalar(T_A[:, :], T_A[:, :], NORM_MIN, None, ALU.max))
                link(nc.vector.tensor_scalar(T_B[:, :], FMAG[:, :], 1e-8, None, ALU.max))
                link(nc.vector.reciprocal(T_B[:, :], T_B[:, :]))
                dve.wait_ge(rows_stored, 64 * (L + 1))
                link(nc.vector.tensor_tensor(DUP[:, :, 0:D], TMP1, per_node(T_B), ALU.mult))
                nc.vector.tensor_copy(DUP[:, :, D:2 * D], DUP[:, :, 0:D]).then_inc(dup_ready, 1)
                doubled_out(2 * L + 2, COS_SCALE)
                link(nc.vector.tensor_copy(C11, ATT0))
                link(nc.vector.tensor_tensor(REST, ATT0, C11, ALU.subtract))
                link(nc.vector.tensor_copy(C22, REST))
                link(nc.vector.tensor_copy(CA[0:D, :], C11[0:D, :]))
                link(nc.vector.tensor_tensor(DEG[:, :], DEGH[:, 0, :], DEGH[:, 1, :], ALU.add))
                link(nc.vector.tensor_scalar(OFF[:, :], DEG[:, :], -TH[L] / H_BYTE, TH[L] * N, ALU.mult, ALU.add))
                link(nc.vector.tensor_scalar(T_A[:, :], COMP[:, :], -FAR, FAR, ALU.mult, ALU.add))
                link(nc.vector.tensor_tensor(OFF[:, :], OFF[:, :], T_A[:, :], ALU.add))
                nc.vector.tensor_copy(CA[D:2 * D, :], C22[D:2 * D, :]).then_inc(stacks_ready, 1)
                dve.wait_ge(stacks_ready, 2 * L + 2)

                with dve.Fori(0, HB) as n:
                    for u in range(2):
                        t = n * 2 + (L * B + u)
                        hold(dve, "dve", exp_done, t * PAIRS + 2 * PAIRS)
                        nc.vector.tensor_reduce(ZS[:, u:u + 1], ZC[:, u, :], AX, ALU.add).then_inc(zsum_done, 1)
                        hold(dve, "dve", zsum_done, t + 1)
                        nc.vector.tensor_scalar(THR[:, u:u + 1], ZS[:, u:u + 1], TH[L], OFF[:, bass.ds(n * 2 + u, 1)],
                                                ALU.mult, ALU.add).then_inc(thr_done, 1)
                        dve.wait_ge(hp_stored[u], (n + (L * HB + 1)) * 16)
                        hold(dve, "dve", thr_done, t + 1)
                        nc.vector.tensor_scalar(HPST[:, u, :].bitcast(FP8), ATT[u], THR[:, u:u + 1], None,
                                                ALU.is_ge, ALU.add, accum_out=CN[:, u:u + 1],
                                                saturate=False).then_inc(hp_ready, 1)
                        hold(dve, "dve", hp_ready, t + 3)
                        nc.vector.tensor_copy(CONN[:, bass.ds(n * 2 + u, 1)], CN[:, u:u + 1]).then_inc(conn_done, 1)
                dve.wait_ge(conn_done, B * (L + 1))

                link(nc.vector.tensor_tensor(IMP[:, :], CONN[:, :], FMAG[:, :], ALU.mult))
                node_softmax(4, NMASK[:, :])
                link(nc.vector.tensor_scalar(T_B[:, :], CONN[:, :], 0.0, None, ALU.is_gt))
                link(nc.vector.tensor_tensor(NMASK[:, :], NMASK[:, :], T_B[:, :], ALU.mult))
                link(nc.vector.tensor_tensor(NMASK[:, :], NMASK[:, :], COMP[:, :], ALU.mult))
                ask(nc.vector.tensor_scalar(T_A[:, :], CONN[:, :], EPS, None, ALU.max))
                link(nc.vector.reciprocal(DV[:, :], DV[:, :]))
                link(nc.vector.tensor_tensor(NMASK[:, :], NMASK[:, :], DV[:, :], ALU.mult))
                link(nc.vector.tensor_tensor(TMP1, XW, per_node(NMASK), ALU.mult))
                split3(TMP1, TMP2, PARTS[:, :, :]).then_inc(parts_ready, 1)
                dve.wait_ge(parts_ready, 3 * L + 2)

                for hf in range(2):
                    half_out(L, hf, 4 * L + hf + 3, 3 * D + 1, TMP1, True)
                dve.wait_ge(half_evac, 4 * L + 4)
                link(nc.vector.tensor_scalar(EDEG[:, :], EDEG[:, :], EPS, None, ALU.max))
                link(nc.vector.reciprocal(EDEG[:, :], EDEG[:, :]))
                link(nc.vector.tensor_tensor(TMP1, TMP1, per_node(EDEG), ALU.mult))
                split3(TMP1, TMP2, PARTS[:, :, :]).then_inc(parts_ready, 1)
                dve.wait_ge(parts_ready, 3 * L + 3)

                def tile_out(u, t):
                    dve.wait_ge(msg_done, t + 1)
                    for g in (0, 2):
                        hold(dve, "dve", m_psum, t * PAIRS + (g + 1 + PAIRS))
                        nc.vector.tensor_copy(HPT[u][:, 8 * P * g:8 * P * (g + 1)],
                                              PS[:, 0:2, :].rearrange("p k c -> p (k c)")).then_inc(m_vec, 1)

                def message(i, u, t):
                    hold(dve, "dve", msg_done, t + 3)
                    nc.vector.tensor_reduce(FEAT[:, bass.ds(i, 1), :],
                                            PS[:, 6 + u, 0:3 * D].rearrange("p (o t d) -> p o d t", o=1, t=3),
                                            AX, ALU.add).then_inc(msg_taken, 1)

                tile_out(0, L * B)
                with dve.Fori(0, HB - 1) as n:
                    for u in range(2):
                        t = n * 2 + (L * B + u)
                        tile_out(1 - u, t + 1)
                        message(n * 2 + u, u, t)
                tile_out(1, (L + 1) * B - 1)
                message(B - 2, 0, (L + 1) * B - 2)
                message(B - 1, 1, (L + 1) * B - 1)
                dve.wait_ge(msg_taken, 2 + B * (L + 1))
                nc.vector.tensor_tensor(FEAT[:, :, :], FEAT[:, :, :], per_node(DV), ALU.mult).then_inc(feat_ready, 1)
                features_out()
                for g, lo, hi in products():
                    nc.vector.tensor_scalar(FEAT[:, lo:hi, :], PS[:, g, 0:(hi - lo) * D].rearrange("p (b d) -> p b d", d=D),
                                            0.0, None, ALU.max).then_inc(prod_evac, 1)
                dve.wait_ge(prod_evac, prods[0])
                if L < LAYERS - 1:
                    dve.sem_inc(feat_ready)
            nc.vector.tensor_tensor(X[:, :, :], X[:, :, :], FEAT[:, :, :], ALU.add).then_inc(feat_ready, 1)

        @block.tensor
        def _(pe):
            pe.sem_inc(cols_used, NCH)
            pe.sem_inc(count_ready, 2)
            pe.sem_inc(acc_done, 2)
            pe.sem_inc(e_used, 2)
            pe.sem_inc(col_done, 2)
            pe.sem_inc(g_used, 2)
            pe.sem_inc(m_psum, PAIRS)
            pe.sem_inc(msg_done, 2)
            feats, xts, prods = [0], [0], [0]

            def features():
                feats[0] += 1
                pe.wait_ge(feat_ready, feats[0])
                for g in range(GROUPS):
                    for k, b in enumerate(group(g)):
                        last = nc.tensor.transpose(PS[0:D, g, k * P:(k + 1) * P], FEAT[:, b, :], identF[:, :])
                    last.then_inc(xt_psum, 1)

            def product(w):
                cols = w.shape[1]
                for g in range(GROUPS):
                    xts[0] += 1
                    pe.wait_ge(xt_ready, xts[0])
                    for k, b in enumerate(group(g)):
                        last = nc.tensor.matmul(PS[:, g, k * cols:(k + 1) * cols], XT[:, b * P:(b + 1) * P], w,
                                                start=True, stop=True)
                    last.then_inc(prod_psum, 1)
                prods[0] += GROUPS

            def zero_bank(bank, w):
                return nc.tensor.matmul(PS[:, bank, 0:w], zeros[:, 0:P], zeros[:, 0:w], start=True, stop=True)

            def add(o, lhsT, rhs):
                return nc.tensor.matmul(o, lhsT, rhs, start=False, stop=True, skip_group_check=True)

            pe.wait_ge(constants_ready, CONSTANTS)
            pe.wait_ge(weights_loaded, 160)
            features()
            product(w0[:, :])
            pe.wait_ge(support_ready, 1)

            def l0_group(sg, nb):
                nh = nb // 2
                w = nh * P

                def accumulate(s, inc_cols):
                    jb = B - 1 - s
                    pe.wait_ge(w_ready, sg * (2 * B) + (2 * s + 2))
                    for b in range(nb):
                        h, k = b // nh, b % nh
                        o = (b % 2) * 3 * D
                        last = add(PS[:, 4 + b // 2, o:o + 3 * D],
                                   WTR[:, h, s % 2, k * P:(k + 1) * P].bitcast(BF16), PARTS[:, jb, :])
                        if b == 0 and inc_cols:
                            last.then_inc(cols_used, 1)
                    last.then_inc(acc_done, 1)

                for s in range(B):
                    jb = B - 1 - s
                    c = CHUNK_OF[s]
                    if s == CHUNK_AT[c]:
                        pe.wait_ge(cast_done, sg * NCH + (RING + c + 1))
                    for h in range(2):
                        hold(pe, "pe", ht_ready, sg * (2 * B) + (2 * s + h + 1))
                        for k in range(nh):
                            last = nc.tensor.matmul(PS[:, h, k * P:(k + 1) * P],
                                                    HS[:, h * nh + k, jb * P:(jb + 1) * P].bitcast(FP8),
                                                    half_ident[:, :], start=True, stop=True)
                        last.then_inc(ht_psum, 1)
                    used = s + 1 == CHUNK_AT[c] + CHUNKS[c]
                    if s == 0:
                        pe.wait_ge(acc_free, sg + 1)
                        for k in range(nb // 2):
                            last = zero_bank(4 + k, 2 * 3 * D)
                        last.then_inc(cols_used, 1)
                    else:
                        accumulate(s - 1, used)
                    for h in range(2):
                        pe.wait_ge(ht_ready, sg * (2 * B) + (2 * s + h + 3))
                        tile = HTR[:, h, s % 2, 0:w]
                        if s == 0:
                            last = nc.tensor.matmul(PS[:, 2 + h, 0:w], count_first[:, :], tile, start=True, stop=True)
                        else:
                            add(PS[:, 2 + h, 0:w], count_next[:, :], HTR[:, h, (s - 1) % 2, 0:w])
                            last = add(PS[:, 2 + h, 0:w], count_first[:, :], tile)
                        last.then_inc(count_ready, 1)
                accumulate(B - 1, False)

            with pe.Fori(0, NSG) as sg:
                l0_group(sg, SG)
            l0_group(NSG, TAIL)

            def doubled(k):
                pe.wait_ge(dup_ready, k)
                for g in range(GROUPS):
                    for j, b in enumerate(group(g)):
                        last = nc.tensor.transpose(PS[:, g, j * P:(j + 1) * P], DUP[:, b, :], identF[:, :])
                    last.then_inc(dup_psum, 1)

            def over_rows(L, hf, k, width, loaded, row_ready, used):
                for bank in range((HB + 1) // 2):
                    zero_bank(bank, min(2, HB - 2 * bank) * width)
                with pe.Fori(0, HB) as n:
                    for u in range(2):
                        t = n * 2 + ((2 * L + hf) * B + u)
                        pe.wait_ge(loaded[u], (n + ((2 * L + hf) * HB + 1)) * 16)
                        hold(pe, "pe", row_ready, t + 1)
                        for j in range(HB):
                            o = (j % 2) * width
                            last = add(PS[:, j // 2, o:o + width], HST[:, u, j * P:(j + 1) * P].bitcast(FP8),
                                       PROW[:, u, 0:width])
                        last.then_inc(used, 1)
                pe.wait_ge(used, 2 + (2 * L + hf + 1) * B)
                zero_bank(7, P).then_inc(half_done, 1)

            for L in range(LAYERS):
                features()
                product(wwv[:, :])
                for g in range(GROUPS):
                    w = len(group(g)) * P
                    pe.wait_ge(prod_evac, prods[0] - GROUPS + g + 1)
                    nc.tensor.matmul(PS[:, g, 0:w], wqq[:, :], XT[:, 4 * P * g:4 * P * g + w],
                                     start=True, stop=True).then_inc(q_psum, 1)
                pe.wait_ge(q_evac, GROUPS * (L + 1))
                for hf in range(2):
                    if hf:
                        pe.wait_ge(half_evac, 4 * L + 1)
                    over_rows(L, hf, 0, 3 * D, e_loaded, e_row_ready, e_used)
                doubled(2 * L + 1)

                def scores(i, t):
                    for q in range(PAIRS):
                        pe.wait_ge(s_masked, t * PAIRS + (q + 1))
                        for lhs, rhs, first in ((QA, E11, True), (QA, E22, False), (QB, E31, False)):
                            for k in range(2):
                                c = 2 * q + k
                                o = PS[:, 2 * (q % 2) + k, 0:CW]
                                last = nc.tensor.matmul(o, lhs[:, bass.ds(i * P, P)], rhs[:, c * CW:(c + 1) * CW],
                                                        start=first, stop=rhs is E31)
                        last.then_inc(s_psum, 1)

                def column_sums(u, t):
                    pe.wait_ge(rz_ready, t + 1)
                    for c in range(8):
                        q = c % 4
                        last = add(PS[32 * q:32 * q + 1, 4 + c // 4, 0:CW], RZ[:, u:u + 1],
                                   ATT[u][:, c * CW:(c + 1) * CW])
                    last.then_inc(col_done, 1)

                pe.wait_ge(stacks_ready, 2 * L + 1)
                for bank in (4, 5):
                    zero_bank(bank, CW)
                scores(0, L * B)
                with pe.Fori(0, HB - 1) as n:
                    for u in range(2):
                        t = n * 2 + (L * B + u)
                        scores(n * 2 + (u + 1), t + 1)
                        column_sums(u, t)
                scores(B - 1, (L + 1) * B - 1)
                column_sums(0, (L + 1) * B - 2)
                column_sums(1, (L + 1) * B - 1)
                pe.wait_ge(rows_back, 16 * (L + 1))
                nc.tensor.transpose(PS[:, 6, 0:B], ATR[:, :], identF[0:B, 0:B]).then_inc(rows_psum, 1)

                doubled(2 * L + 2)
                pe.wait_ge(stacks_ready, 2 * L + 2)
                with pe.Fori(0, HB) as n:
                    for u in range(2):
                        t = n * 2 + (L * B + u)
                        i = n * 2 + u
                        for q in range(PAIRS):
                            if q == 0:
                                pe.wait_ge(g_ready, t + 3)
                            hold(pe, "pe", exp_done, t * PAIRS + (q + 1))
                            for k in range(2):
                                c = 2 * q + k
                                nc.tensor.matmul(PS[:, c, 0:CW], mask_ident[:, :],
                                                 GST[:, u, c * CW:(c + 1) * CW].bitcast(FP8), start=True, stop=False)
                            for rhs in (C11, C22):
                                for k in range(2):
                                    c = 2 * q + k
                                    last = nc.tensor.matmul(PS[:, c, 0:CW], CA[:, bass.ds(i * P, P)],
                                                            rhs[:, c * CW:(c + 1) * CW], start=False, stop=rhs is C22)
                            last.then_inc(cos_psum, 1)

                for hf in range(2):
                    if hf:
                        pe.wait_ge(half_evac, 4 * L + 3)
                    else:
                        pe.wait_ge(parts_ready, 3 * L + 2)
                    over_rows(L, hf, 0, 3 * D + 1, g_loaded, g_row_ready, g_used)

                def transposes(m, u, t):
                    for g in range(PAIRS):
                        if g == 0:
                            pe.wait_ge(m_loaded[u], (m + (L * HB + 1)) * 16)
                        hold(pe, "pe", (m_vec, m_act)[g % 2], t * 2 + (g // 2 + 1))
                        for b in range(8 * g, min(8 * g + 8, B)):
                            last = nc.tensor.matmul(PS[:, 2 * (g % 2) + (b % 8) // 4, (b % 4) * P:(b % 4 + 1) * P],
                                                    HST[:, u, b * P:(b + 1) * P].bitcast(FP8), ident[:, :],
                                                    start=True, stop=True)
                        last.then_inc(m_psum, 1)

                def messages(u, t):
                    pe.wait_ge(m_vec, t * 2 + 3)
                    pe.wait_ge(m_act, t * 2 + 3)
                    pe.wait_ge(msg_taken, t + 1)
                    for b in range(B):
                        last = nc.tensor.matmul(PS[:, 6 + u, 0:3 * D], HPT[u][:, b * P:(b + 1) * P], PARTS[:, b, :],
                                                start=b == 0, stop=b == B - 1)
                    last.then_inc(msg_done, 1)

                pe.wait_ge(parts_ready, 3 * L + 3)
                transposes(0, 0, L * B)
                with pe.Fori(0, HB - 1) as n:
                    for u in range(2):
                        t = n * 2 + (L * B + u)
                        transposes(n + u, 1 - u, t + 1)
                        messages(u, t)
                transposes(HB - 1, 1, (L + 1) * B - 1)
                messages(0, (L + 1) * B - 2)
                messages(1, (L + 1) * B - 1)
                features()
                product(wth[:, :])


CONSTANTS = 25

_INS = ["x", "adj", "L0_gnn_weight", "L0_gnn_bias", "L1_gnn_W", "L1_gnn_Theta", "L1_gnn_Wq", "L1_gnn_bq",
        "L1_gnn_Wv", "L1_gnn_bv"]
_OUTS = [((3327, 64), "float32")]


def kernel(**inputs):
    import numpy as _np
    import concourse.bacc as _bacc
    from concourse import mybir as _mybir
    from concourse.bass_utils import run_bass_kernel_spmd as _run

    nc = _bacc.Bacc("TRN2", target_bir_lowering=False, num_devices=1)
    arrays, args = {}, []
    for name in _INS:
        a = _np.ascontiguousarray(inputs[name])
        arrays[f"in_{name}_dram"] = a
        args.append(nc.dram_tensor(f"in_{name}_dram", a.shape, _mybir.dt.from_np(a.dtype), kind="ExternalInput").ap())
    for i, (shape, dtype) in enumerate(_OUTS):
        dt = _mybir.dt.from_np(_np.dtype(dtype))
        args.append(nc.dram_tensor(f"out_{i}_dram", shape, dt, kind="ExternalOutput").ap())
    bass_adj_preln_gnn_hypergraph(nc, *args)
    r = _run(nc, [arrays], core_ids=[0])
    return r.results[0]["out_0_dram"]
```

```python
import concourse.bass as bass
from concourse import mybir
from contextlib import ExitStack


def bass_adj_preln_gnn_hypergraph(
    nc: bass.Bass,
    x: bass.AP,
    adj: bass.AP,
    l0_weight: bass.AP,
    l0_bias: bass.AP,
    W: bass.AP,
    Theta: bass.AP,
    Wq: bass.AP,
    bq: bass.AP,
    Wv: bass.AP,
    bv: bass.AP,
    out: bass.AP,
):
    F32 = mybir.dt.float32
    BF16 = mybir.dt.bfloat16
    FP16 = mybir.dt.float16
    FP8 = mybir.dt.float8e4
    U8 = mybir.dt.uint8
    I16 = mybir.dt.int16
    I32 = mybir.dt.int32
    ALU = mybir.AluOpType
    ACT = mybir.ActivationFunctionType
    AX = mybir.AxisListType.X
    RMAX = bass.bass_isa.ReduceOp.max
    RADD = bass.bass_isa.ReduceOp.add

    N, D = x.shape
    P = 128
    B = (N + P - 1) // P
    NP = B * P
    LAST = N - (B - 1) * P
    PADCOLS = NP - N
    assert PADCOLS == 1 and B % 2 == 0
    LAYERS = 2
    LN_EPS = 1e-5
    EPS = 1e-6
    NORM_MIN = 1e-16
    MAX_NEIGH = 100
    TH = [0.000244, 0.000244 + (1.0 - 2.718281828459045 ** (-0.1)) * (0.0003 - 0.000244)]
    FAR = 1e30

    H_BYTE = 64.0
    H_FP8 = 2.0

    STEP = 128.0
    OWN = 128.0 * STEP
    W_BIAS = MAX_NEIGH * STEP - OWN
    SUP_SCALE = 2.0 ** (127 - MAX_NEIGH)

    SG = 6
    NSG = B // SG
    TAIL = B - NSG * SG
    assert TAIL == 2
    CHUNKS = [1, 1] + [2] * ((B - 2) // 2)
    NCH = len(CHUNKS)
    RING = NCH // 2
    CHUNK_AT = [sum(CHUNKS[:c]) for c in range(NCH)]
    CHUNK_OF = {CHUNK_AT[c] + k: c for c in range(NCH) for k in range(CHUNKS[c])}

    RS = 4
    ROUNDS = B // RS
    assert B == RS * ROUNDS + 2
    PAIR0, PAIR1 = ROUNDS + 1, ROUNDS
    HALF = NP // 2
    HB = B // 2
    EW = 2 * D + 1
    CW = NP // 8
    PW = 2 * CW
    PAIRS = NP // PW
    TILES_AT = [0, 2, 4, 7]
    SCORES_AT = [0, 2, 6, 2]
    SCORES_WAIT = [1, 4, 3, PAIRS + 2]
    GROUPS = (B + 3) // 4

    TOP = 2.0 ** 14
    TINY = 2.0 ** -100
    EXPONENT = 0x7F800000
    COS_SCALE = 2.0 ** 15
    COS_UNIT = COS_SCALE * COS_SCALE
    MASK_OFF = -128.0 * COS_UNIT

    def group(g):
        return range(4 * g, min(4 * g + 4, B))

    ctx = ExitStack()
    with ctx:
        def sb(name, shape, dt):
            return ctx.enter_context(nc.sbuf_tensor(name, shape, dt))

        def sem(name):
            return ctx.enter_context(nc.semaphore(name))

        H = sb("H", [P, B, NP], U8)
        X = sb("X", [P, B, D], F32)
        FEAT = sb("FEAT", [P, B, D], F32)
        PARTS = sb("PARTS", [P, B, 3 * D], BF16)
        XTb = sb("XTb", [P, NP], F32)
        ATT1 = sb("ATT1", [P, NP], F32)
        ARENA = sb("ARENA", [P, 16384], F32)

        XT = XTb[0:D, :]
        XT1 = XTb[0:D + 1, :]
        DUP = XTb[:, :].rearrange("p (b d) -> p b d", b=B)
        ROWS = XTb[:, 0:2 * CW].rearrange("p (k c) -> p k c", k=2)
        TMP1 = ATT1[:, 0:B * D].rearrange("p (b d) -> p b d", b=B)
        TMP2 = ATT1[:, B * D:2 * B * D].rearrange("p (b d) -> p b d", b=B)

        at = [0]

        def carve(words, dt=F32):
            a = ARENA[:, at[0]:at[0] + words]
            at[0] += words
            return a if dt == F32 else a.bitcast(dt)

        FST = carve(RING * SG * 2 * P).rearrange("p (r b c) -> p r b c", r=RING, b=SG)
        HS = carve(SG * NP // 4, U8).rearrange("p (b c) -> p b c", b=SG)
        assert at[0] <= 16384
        HTILE = SG // 2 * P
        HTR = XTb[:, 0:2 * HTILE].bitcast(BF16).rearrange("p (h k c) -> p h k c", h=2, k=2)
        WTR = XTb[:, 2 * HTILE:4 * HTILE].bitcast(I16).rearrange("p (h k c) -> p h k c", h=2, k=2)
        SUM0 = XTb[:, 1600:1600 + SG * D].rearrange("p (b d) -> p b d", b=SG)
        SUM1 = XTb[:, 2000:2000 + SG * D].rearrange("p (b d) -> p b d", b=SG)

        at[0] = 0
        QA = carve(NP // 2, FP16)
        E11 = carve(NP // 2, FP16)
        E22 = carve(NP // 2, FP16)
        ATT0 = carve(NP)
        XW = carve(B * D).rearrange("p (b d) -> p b d", b=B)
        HST = carve(RS * NP // 4, U8).rearrange("p (u c) -> p u c", u=RS)
        HPST = carve(2 * NP // 4, U8).rearrange("p (u c) -> p u c", u=2)
        assert at[0] <= 16384
        CA, C11, C22 = QA, E11, E22
        GST = XTb[:, :].bitcast(U8).rearrange("p (u c) -> p u c", u=RS)
        ATT = [ATT0, ATT1[:, :]]
        HPT = [ATT0.bitcast(BF16)[:, 0:NP], ATT1[:, 0:NP // 2].bitcast(BF16)]
        HALVES = PARTS[:, :, 0:2 * D].bitcast(FP16)

        PROW = sb("PROW", [P, RS, 2 * D + 2], FP16)
        fold = sb("fold", [P, P], F32)
        ones = sb("ones", [P, 1], F32)
        identF = sb("identF", [P, P], F32)
        half_ident = sb("half_ident", [P, P], BF16)
        ident = sb("ident", [P, P], BF16)
        mask_ident = sb("mask_ident", [P, P], BF16)
        count_first = sb("count_first", [P, P], BF16)
        count_next = sb("count_next", [P, P], BF16)
        zeros = sb("zeros", [P, 512], BF16)
        valid = sb("valid", [P, B], F32)
        far = sb("far", [P, B], F32)
        cast_by = sb("cast_by", [P, 1], F32)
        eps = sb("eps", [P, 3], F32)
        w0 = sb("w0", [D, D], F32)
        wwv = sb("wwv", [D + 1, 2 * D], F32)
        wqq = sb("wqq", [D + 1, 2 * D], F32)
        wth = sb("wth", [D, D], F32)
        b0 = sb("b0", [P, D], F32)
        (MEAN, VAR, STD, STR, DEG, OFF, COMP, IMP, EXPN, FMAG, CONN, NMASK, DV, EDEG, T_A, T_B) = [
            sb(n, [P, B], F32) for n in ("MEAN", "VAR", "STD", "STR", "DEG", "OFF", "COMP", "IMP", "EXPN",
                                         "FMAG", "CONN", "NMASK", "DV", "EDEG", "T_A", "T_B")]
        LARGEST = sb("LARGEST", [P, 8], F32)
        WARM = sb("WARM", [P, 1], F32)
        SV, SQ, SE, ST, SA = [sb(n, [P, 4], F32) for n in ("SV", "SQ", "SE", "ST", "SA")]
        UNDO = sb("UNDO", [P, 2], F32)
        ATR = sb("ATR", [B, P], F32)
        MX = sb("MX", [P, 2, PAIRS + 1], F32)
        NEGM = sb("NEGM", [P, 2], F32)
        ZROW = sb("ZROW", [P, 2], F32)
        RZ = sb("RZ", [P, 2], F32)
        RZT = sb("RZT", [P, 1], F32)
        ZC = sb("ZC", [P, 2, 2], F32)
        ZS = sb("ZS", [P, 2, 2], F32)
        THR = sb("THR", [P, 2], F32)
        CN = sb("CN", [P, RS], F32)
        G1 = sb("G1", [P, 8], F32)

        PS = ctx.enter_context(nc.psum_tensor("PS", [P, 8, 512], F32))

        att_dram = nc.dram_tensor("att_row", [NP], F32)
        att_rows = att_dram[:].rearrange("(k q c) -> q k c", k=2, q=4)
        att_back = att_dram[:].rearrange("(b p) -> b p", p=P)
        hp_dram = nc.dram_tensor("h_pruned", [B, P, NP], U8)

        weights_loaded = sem("weights_loaded")
        x_loaded = sem("x_loaded")
        pads_zeroed = sem("pads_zeroed")
        constants_ready = sem("constants_ready")
        vec_step = sem("vec_step")
        node_to_act = sem("node_to_act")
        node_from_act = sem("node_from_act")
        node_to_pool = sem("node_to_pool")
        node_from_pool = sem("node_from_pool")
        feat_ready = sem("feat_ready")
        xt_psum = sem("xt_psum")
        xt_ready = sem("xt_ready")
        prod_psum = sem("prod_psum")
        prod_evac = sem("prod_evac")
        q_psum = sem("q_psum")
        q_evac = sem("q_evac")
        support_ready = sem("support_ready")
        adj_loaded = [sem(f"adj_loaded{r}") for r in range(RING)]
        cast_done = sem("cast_done")
        kept = sem("kept")
        cols_used = sem("cols_used")
        ht_psum = sem("ht_psum")
        ht_ready = sem("ht_ready")
        count_ready = sem("count_ready")
        w_ready = sem("w_ready")
        acc_done = sem("acc_done")
        acc_free = sem("acc_free")
        l0_sum = sem("l0_sum")
        l0_biased = sem("l0_biased")
        parts_ready = sem("parts_ready")
        deg_rows = sem("deg_rows")
        deg_psum = sem("deg_psum")
        ones_row = sem("ones_row")
        scale_ready = sem("scale_ready")
        high_ready = sem("high_ready")
        v_high = sem("v_high")
        xw_evac = sem("xw_evac")
        et_evac = sem("et_evac")
        fold_psum = sem("fold_psum")
        e_high = sem("e_high")
        q_high = sem("q_high")
        c_high = sem("c_high")
        tiles_loaded = [sem(f"tiles_loaded{k}") for k in range(2)]
        e_row_ready = sem("e_row_ready")
        e_used = sem("e_used")
        half_done = sem("half_done")
        half_evac = sem("half_evac")
        dup_ready = sem("dup_ready")
        dup_psum = sem("dup_psum")
        dup_evac = sem("dup_evac")
        stacks_ready = sem("stacks_ready")
        s_psum = sem("s_psum")
        s_masked = sem("s_masked")
        max_ready = sem("max_ready")
        z_ready = sem("z_ready")
        rz_ready = sem("rz_ready")
        col_done = sem("col_done")
        rows_ready = sem("rows_ready")
        rows_stored = sem("rows_stored")
        rows_back = sem("rows_back")
        rows_psum = sem("rows_psum")
        g_ready = sem("g_ready")
        cos_psum = sem("cos_psum")
        exp_done = sem("exp_done")
        thr_done = sem("thr_done")
        hp_ready = sem("hp_ready")
        conn_done = sem("conn_done")
        hp_stored = [sem(f"hp_stored{u}") for u in range(2)]
        g_row_ready = sem("g_row_ready")
        g_used = sem("g_used")
        m_psum = sem("m_psum")
        m_vec = sem("m_vec")
        m_act = sem("m_act")
        msg_done = sem("msg_done")
        msg_taken = sem("msg_taken")
        out_stored = sem("out_stored")
        held = {e: sem("held_" + e) for e in ("pe", "act", "dve", "pool", "sp")}

        block = ctx.enter_context(nc.Block())

        def hold(eng, name, s, value):
            eng.wait_ge(s, value)
            eng.sem_inc(held[name])

        def all_tiles(eng, body):
            with eng.Fori(0, ROUNDS) as n:
                for v in range(RS):
                    body(n, n * RS + v, v)
            for v in range(2):
                body(ROUNDS, ROUNDS * RS + v, v)

        def all_tiles_ahead(eng, first, second):
            first(0, 0, 0)
            with eng.Fori(0, ROUNDS) as n:
                for v in range(RS):
                    first(n + (v + 1) // RS, n * RS + (v + 1), (v + 1) % RS)
                    second(n * RS + v, v)
            first(ROUNDS, B - 1, 1)
            second(B - 2, 0)
            second(B - 1, 1)

        PASSES = 5

        def loaded_at(L, k, n, v):
            per_pass = (PAIR0, PAIR1)[v // 2]
            return n * 16 + 16 * (per_pass * (PASSES * L + k) + 1)

        @block.sync
        def _(sp):
            for dst, src in ((w0[:, :], l0_weight), (wth[:, :], Theta), (wwv[0:D, 0:D], W), (wwv[0:D, D:2 * D], Wv),
                             (wqq[0:D, 0:D], Wq), (wqq[0:D, D:2 * D], Wq),
                             (b0[:, :], l0_bias.rearrange("(o d) -> o d", o=1).to_broadcast([P, D])),
                             (wwv[D:D + 1, D:2 * D], bv.rearrange("(o d) -> o d", o=1)),
                             (wqq[D:D + 1, 0:D], bq.rearrange("(o d) -> o d", o=1)),
                             (wqq[D:D + 1, D:2 * D], bq.rearrange("(o d) -> o d", o=1))):
                sp.dma_start(dst, src).then_inc(weights_loaded, 16)
            sp.dma_start(X[:, 0:B - 1, :],
                         x[0:(B - 1) * P, :].rearrange("(b p) d -> p b d", p=P)).then_inc(x_loaded, 16)
            sp.wait_ge(pads_zeroed, 1)
            sp.dma_start(X[0:LAST, B - 1, :], x[(B - 1) * P:N, :]).then_inc(x_loaded, 16)

            def cols(c):
                first = B - CHUNK_AT[c] - CHUNKS[c]
                lo = first * P
                return lo, min(N, lo + CHUNKS[c] * P) - lo

            with sp.Fori(0, NSG) as sg:
                for c in range(NCH):
                    lo, w = cols(c)
                    hold(sp, "sp", cast_done, sg * NCH + (c + 1))
                    sp.dma_start(FST[:, c % RING, :, 0:w],
                                 adj[bass.ds(sg * (SG * P), SG * P), lo:lo + w]
                                 .rearrange("(b p) c -> p b c", p=P)).then_inc(adj_loaded[c % RING], 16)
            for c in range(NCH):
                lo, w = cols(c)
                r0 = NSG * SG * P
                sp.wait_ge(cast_done, NSG * NCH + c + 1)
                sp.dma_start(FST[:, c % RING, 0, 0:w], adj[r0:r0 + P, lo:lo + w]).then_inc(adj_loaded[c % RING], 16)
                r0 += P
                sp.dma_start(FST[0:112, c % RING, 1, 0:w], adj[r0:r0 + 112, lo:lo + w]).then_inc(adj_loaded[c % RING], 16)
                sp.dma_start(FST[112:LAST, c % RING, 1, 0:w], adj[r0 + 112:N, lo:lo + w]).then_inc(adj_loaded[c % RING], 16)

            def load_pairs(source, used, base, per_tile=1, width=NP):
                def load(n, i, k):
                    hold(sp, "sp", used, n * (RS * per_tile) + (base + (2 * k + 2) * per_tile))
                    sp.dma_start(HST[:, 2 * k:2 * k + 2, 0:width], source(i)).then_inc(tiles_loaded[k], 16)

                with sp.Fori(0, ROUNDS) as n:
                    for k in range(2):
                        load(n, n * RS + 2 * k, k)
                load(ROUNDS, ROUNDS * RS, 0)

            def resident(i):
                return H[:, bass.ds(i, 2), :]

            def pruned(lo, hi):
                return lambda i: hp_dram[bass.ds(i, 2), :, lo:hi].rearrange("b p c -> p b c")

            for L in range(LAYERS):
                if L == 0:
                    sp.wait_ge(kept, NCH + (NSG + 1) * NCH)
                    sp.wait_ge(acc_done, 2 + B * (NSG + 1))
                else:
                    sp.wait_ge(m_psum, (RS + B * L) * PAIRS)
                load_pairs(resident, max_ready, B * L)
                sp.wait_ge(rows_ready, L + 1)
                for q in range(4):
                    sp.dma_start(att_rows[q:q + 1, :, :], ROWS[32 * q:32 * q + 1, :, :]).then_inc(rows_stored, 16)
                sp.wait_ge(rows_stored, 64 * (L + 1))
                sp.dma_start(ATR[:, :], att_back).then_inc(rows_back, 16)
                sp.wait_ge(max_ready, RS + B * (L + 1))
                def cos_load(n, i, k):
                    hold(sp, "sp", g_ready, n * RS + (B * L + 2 * k + 2))
                    sp.dma_start(HST[:, 2 * k:2 * k + 2, :], resident(i)).then_inc(tiles_loaded[k], 16)

                def store_pruned(n, i, v):
                    for u in range(2):
                        hold(sp, "sp", hp_ready, n * RS + (B * L + v + u + 3))
                        sp.dma_start(hp_dram[bass.ds(i + u, 1), :, :].rearrange("o p c -> p (o c)"),
                                     HPST[:, u, :]).then_inc(hp_stored[u], 16)

                cos_load(0, 0, 0)
                cos_load(0, 2, 1)
                with sp.Fori(0, ROUNDS - 1) as n:
                    for k in range(2):
                        cos_load(n + 1, n * RS + (RS + 2 * k), k)
                        store_pruned(n, n * RS + 2 * k, 2 * k)
                cos_load(ROUNDS, B - 2, 0)
                for k in range(3):
                    store_pruned(ROUNDS - 1, B - 6 + 2 * k, 2 * k)
                sp.wait_ge(g_ready, RS + B * (L + 1))
                for u in range(2):
                    sp.wait_ge(hp_stored[u], 16 + 16 * HB * (L + 1))
                for hf in range(2):
                    if hf:
                        sp.wait_ge(g_used, RS + B * (2 * L + 1))
                    load_pairs(pruned(hf * HALF, (hf + 1) * HALF), g_used, B * (2 * L + hf), width=HALF)
                sp.wait_ge(g_used, RS + 2 * B * (L + 1))
                load_pairs(pruned(0, NP), m_psum, B * L * PAIRS, per_tile=PAIRS)
            sp.wait_ge(feat_ready, 2 + 2 * LAYERS)
            sp.dma_start(out[0:(B - 1) * P, :].rearrange("(b p) d -> p b d", p=P), X[:, 0:B - 1, :]).then_inc(out_stored, 16)
            sp.dma_start(out[(B - 1) * P:N, :], X[0:LAST, B - 1, :]).then_inc(out_stored, 16)
            sp.wait_ge(out_stored, 32)

        @block.gpsimd
        def _(pool):
            step = [0]

            def link(ins):
                step[0] += 1
                ins.then_inc(constants_ready, 1)
                pool.wait_ge(constants_ready, step[0])

            pool.sem_inc(cast_done, RING)
            pool.sem_inc(kept, NCH)
            pool.sem_inc(g_ready, RS)
            nc.gpsimd.memset(X[:, B - 1, :], 0.0).then_inc(pads_zeroed, 1)
            link(nc.gpsimd.memset(HS[:, :, N:NP], 0))
            link(nc.gpsimd.memset(PROW[:, :, 2 * D:2 * D + 2], 1.0))
            link(nc.gpsimd.memset(wwv[D:D + 1, 0:D], 0.0))
            link(nc.gpsimd.memset(ones[:, :], 1.0))
            link(nc.gpsimd.memset(zeros[:, :], 0.0))
            link(nc.gpsimd.memset(eps[:, 0:1], LN_EPS))
            link(nc.gpsimd.memset(eps[:, 1:2], 0.0))
            link(nc.gpsimd.memset(eps[:, 2:3], W_BIAS))
            link(nc.gpsimd.memset(valid[:, :], 1.0))
            link(nc.gpsimd.affine_select(out=valid[:, :], in_=valid[:, :], compare_op=ALU.is_gt, fill=0.0, base=N,
                                         pattern=[[-P, B]], channel_multiplier=-1))
            link(nc.gpsimd.tensor_scalar(cast_by[:, :], valid[:, B - 1:B], H_BYTE, 0.0, ALU.mult, ALU.add))
            link(nc.gpsimd.tensor_scalar(far[:, :], valid[:, :], FAR, -FAR, ALU.mult, ALU.add))
            for m, rest, diag in ((identF, 0.0, 1.0), (ident, 0.0, 1.0), (half_ident, 0.0, 1.0 / H_FP8),
                                  (mask_ident, 0.0, MASK_OFF)):
                link(nc.gpsimd.memset(m[:, :], rest))
                link(nc.gpsimd.affine_select(out=m[:, :], in_=m[:, :], compare_op=ALU.not_equal, fill=diag, base=0,
                                             pattern=[[-1, P]], channel_multiplier=1))
            link(nc.gpsimd.memset(fold[:, :], 0.0))
            for off in (-D, 0, D):
                link(nc.gpsimd.affine_select(out=fold[:, :], in_=fold[:, :], compare_op=ALU.not_equal, fill=1.0, base=off,
                                             pattern=[[-1, P]], channel_multiplier=1))
            for m, sign, diag in ((count_first, 1, OWN), (count_next, -1, -OWN - STEP)):
                link(nc.gpsimd.memset(m[:, :], -STEP))
                link(nc.gpsimd.affine_select(out=m[:, :], in_=m[:, :], compare_op=ALU.is_gt, fill=0.0, base=0,
                                             pattern=[[-sign, P]], channel_multiplier=sign))
                link(nc.gpsimd.affine_select(out=m[:, :], in_=m[:, :], compare_op=ALU.not_equal, fill=diag, base=0,
                                             pattern=[[-1, P]], channel_multiplier=1))
            assert step[0] == CONSTANTS

            def cast(sg, c, nb):
                n = sg * NCH + (c + 1)
                lo = (B - CHUNK_AT[c] - CHUNKS[c]) * P
                w = min(N, lo + CHUNKS[c] * P) - lo
                if nb == SG:
                    pool.wait_ge(adj_loaded[c % RING], sg * 32 + 16 * (c // RING + 1))
                else:
                    pool.wait_ge(adj_loaded[c % RING], NSG * 32 + 48 * (c // RING + 1))
                pool.wait_ge(kept, n)
                hold(pool, "pool", cols_used, n)
                if nb == SG:
                    nc.gpsimd.tensor_scalar(HS[:, :, lo:lo + w], FST[:, c % RING, :, 0:w], H_BYTE, 1.0,
                                            ALU.mult, ALU.mult).then_inc(cast_done, 1)
                else:
                    nc.gpsimd.tensor_scalar(HS[:, 0, lo:lo + w], FST[:, c % RING, 0, 0:w], H_BYTE, 1.0,
                                            ALU.mult, ALU.mult)
                    nc.gpsimd.tensor_scalar(HS[:, 1, lo:lo + w], FST[:, c % RING, 1, 0:w], cast_by[:, 0:1], 1.0,
                                            ALU.mult, ALU.mult).then_inc(cast_done, 1)

            with pool.Fori(0, NSG) as sg:
                for c in range(NCH):
                    cast(sg, c, SG)
            for c in range(NCH):
                cast(NSG, c, TAIL)

            def rows(used, ready, base):
                def one(n, i, v):
                    hold(pool, "pool", used, n * RS + (base + v + 1))
                    nc.gpsimd.tensor_copy(PROW[:, v, 0:2 * D].bitcast(I32),
                                          HALVES[:, i, :].bitcast(I32)).then_inc(ready, 1)
                if base:
                    pool.wait_ge(used, RS + base)
                all_tiles(pool, one)

            def across(k, src, dst, op):
                pool.wait_ge(node_to_pool, k)
                nc.gpsimd.partition_all_reduce(dst, src, P, op).then_inc(node_from_pool, 1)

            sums = [0]

            def reduce_at(src, dst, op):
                sums[0] += 1
                across(sums[0], src, dst, op)

            for L in range(LAYERS):
                pool.wait_ge(feat_ready, 2 + 2 * L)
                if L == 0:
                    pool.wait_ge(l0_sum, NSG + 1)
                nc.gpsimd.memset(XTb[D:D + 1, :], 1.0).then_inc(ones_row, 1)
                reduce_at(SV[:, 0:1], SV[:, 0:1], RMAX)
                reduce_at(SQ[:, 0:1], SQ[:, 0:1], RMAX)
                pool.wait_ge(parts_ready, 3 * L + 1)
                rows(e_used, e_row_ready, B * L)
                reduce_at(SE[:, 0:1], SE[:, 0:1], RMAX)
                reduce_at(G1[:, 0:1], G1[:, 1:2], RMAX)
                reduce_at(G1[:, 2:3], G1[:, 3:4], RADD)

                def other(n, i, v):
                    pool.wait_ge(tiles_loaded[v // 2], loaded_at(L, 1, n, v))
                    hold(pool, "pool", cos_psum, n * (2 * RS) + (2 * (B * L + v) + 2))
                    nc.gpsimd.tensor_scalar(GST[:, v, :], HST[:, v, :], -1.0, H_BYTE,
                                            ALU.mult, ALU.add).then_inc(g_ready, 1)

                pool.wait_ge(stacks_ready, 2 * L + 2)
                all_tiles(pool, other)
                reduce_at(G1[:, 4:5], G1[:, 5:6], RMAX)
                reduce_at(G1[:, 6:7], G1[:, 7:8], RADD)
                reduce_at(ST[:, 0:1], ST[:, 0:1], RMAX)
                pool.wait_ge(parts_ready, 3 * L + 2)
                for hf in range(2):
                    rows(g_used, g_row_ready, B * (2 * L + hf))
                reduce_at(SA[:, 0:1], SA[:, 0:1], RMAX)

        @block.scalar
        def _(act):
            act.sem_inc(deg_rows, 1)
            act.sem_inc(exp_done, 2)
            act.sem_inc(m_act, 2)
            act.wait_ge(constants_ready, CONSTANTS)
            small = [0]

            def asked(o, i, func, **kw):
                small[0] += 1
                act.wait_ge(node_to_act, small[0])
                nc.scalar.activation(o, i, func, **kw).then_inc(node_from_act, 1)

            asked(STD[:, :], VAR[:, :], ACT.Sqrt, scale=1.0 / D, bias=eps[:, 0:1])

            def exponents(sg, nb):
                w = nb // 2 * P
                for s in range(B):
                    for h in range(2):
                        act.wait_ge(acc_done, sg * B + (s + 1))
                        hold(act, "act", count_ready, sg * (2 * B) + (2 * s + h + 3))
                        nc.scalar.activation(WTR[:, h, s % 2, 0:w], PS[:, 2 + h, 0:w], ACT.Relu,
                                             bias=eps[:, 2:3]).then_inc(w_ready, 1)
                hold(act, "act", count_ready, sg * (2 * B) + (2 * B + 2))
                for h in range(2):
                    row = FEAT[32 * h:32 * h + 1, :, :].rearrange("p b d -> p (b d)")
                    hold(act, "act", deg_psum, sg + 1)
                    last = nc.scalar.activation(row[:, bass.ds(sg * HTILE, w)], PS[32 * h:32 * h + 1, 2 + h, 0:w], ACT.Copy)
                last.then_inc(deg_rows, 1)

            with act.Fori(0, NSG) as sg:
                exponents(sg, SG)
            exponents(NSG, TAIL)

            for L in range(LAYERS):
                if L == 0:
                    asked(STD[:, :], VAR[:, :], ACT.Sqrt, scale=1.0 / D, bias=eps[:, 0:1])
                for g in range(GROUPS):
                    b = group(g)
                    act.wait_ge(prod_psum, GROUPS * (2 * L + 1) + g + 1)
                    nc.scalar.activation(XW[:, b[0]:b[-1] + 1, :],
                                         PS[:, g, 0:len(b) * 2 * D].rearrange("p (b c) -> p b c", c=2 * D)[:, :, 0:D],
                                         ACT.Copy).then_inc(xw_evac, 1)
                act.wait_ge(scale_ready, 5 * L + 1)
                for g in range(GROUPS):
                    b = group(g)
                    nc.scalar.activation(HALVES[:, b[0]:b[-1] + 1, 0:D],
                                         PS[:, g, 0:len(b) * 2 * D].rearrange("p (b c) -> p b c", c=2 * D)[:, :, D:2 * D],
                                         ACT.Copy, scale=SV[:, 2:3]).then_inc(v_high, 1)
                asked(STR[:, :], T_A[:, :], ACT.Sqrt)
                act.wait_ge(scale_ready, 5 * L + 2)
                nc.scalar.activation(QA, ATT1[:, :], ACT.Copy, scale=SQ[:, 2:3]).then_inc(q_high, 1)
                act.wait_ge(scale_ready, 5 * L + 3)
                for g in range(GROUPS):
                    w = len(group(g)) * P
                    nc.scalar.activation(E11[:, 4 * P * g:4 * P * g + w], PS[:, g, 0:w], ACT.Copy,
                                         scale=SE[:, 2:3]).then_inc(e_high, 1)
                nc.scalar.activation(WARM[:, :], eps[:, 1:2], ACT.Exp)

                def att_exp(n, i, v):
                    u = v % 2
                    hold(act, "act", max_ready, n * RS + (B * L + v + 1 + RS))
                    nc.scalar.activation(ATT[u][:, 0:N], ATT[u][:, 0:N], ACT.Exp, bias=NEGM[:, u:u + 1],
                                         accum_out=ZROW[:, u:u + 1]).then_inc(z_ready, 1)

                all_tiles(act, att_exp)
                asked(EXPN[:, :], IMP[:, :], ACT.Exp, bias=G1[:, 1:2], accum_out=G1[:, 2:3])
                asked(FMAG[:, :], T_A[:, :], ACT.Sqrt)
                for g in range(GROUPS):
                    w = len(group(g)) * P
                    act.wait_ge(dup_psum, GROUPS * L + g + 1)
                    nc.scalar.activation(C11[:, 4 * P * g:4 * P * g + w], PS[:, g, 0:w], ACT.Copy,
                                         scale=COS_SCALE).then_inc(c_high, 1)
                nc.scalar.activation(WARM[:, :], eps[:, 1:2], ACT.Exp)

                def cos_exp(n, i, v):
                    u = v % 2
                    act.wait_ge(hp_ready, n * RS + (B * L + v + 1))
                    for q in range(2):
                        hold(act, "act", cos_psum, n * (2 * RS) + (2 * (B * L + v) + q + 1 + 2 * RS))
                        nc.scalar.activation(ATT[u][:, q * HALF:(q + 1) * HALF].rearrange("p (k c) -> p k c", k=4),
                                             PS[:, 4 * q:4 * q + 4, 0:CW], ACT.Exp, scale=1.0 / COS_UNIT,
                                             accum_out=ZC[:, u, q:q + 1]).then_inc(exp_done, 1)
                    hold(act, "act", exp_done, n * (2 * RS) + (2 * (B * L + v) + 4))
                    nc.scalar.activation(ZS[:, u, :], ZC[:, u, :], ACT.Identity, scale=TH[L], bias=OFF[:, bass.ds(i, 1)],
                                         accum_out=THR[:, u:u + 1]).then_inc(thr_done, 1)

                all_tiles(act, cos_exp)
                asked(EXPN[:, :], IMP[:, :], ACT.Exp, bias=G1[:, 5:6], accum_out=G1[:, 6:7])
                asked(DV[:, :], T_A[:, :], ACT.Sqrt)
                for k in (4, 5):
                    act.wait_ge(scale_ready, 5 * L + k)
                    nc.scalar.activation(HALVES[:, :, 0:D], TMP1, ACT.Copy,
                                         scale=(ST, SA)[k - 4][:, 2:3]).then_inc(high_ready, 1)

                def tile_out(n, i, v):
                    u = v % 2
                    act.wait_ge(msg_done, n * RS + (B * L + v + 1))
                    for g in (1, 3):
                        w = min(8 * P, NP - 8 * P * g)
                        hold(act, "act", m_psum, n * (RS * PAIRS) + ((B * L + v + RS) * PAIRS + g + 1))
                        nc.scalar.activation(HPT[u][:, 8 * P * g:8 * P * g + w],
                                             PS[:, TILES_AT[g]:min(TILES_AT[g] + 2, 8), :].rearrange("p k c -> p (k c)")[:, 0:w],
                                             ACT.Copy).then_inc(m_act, 1)

                all_tiles(act, tile_out)

        @block.vector
        def _(dve):
            chain = [0]

            def link(ins):
                chain[0] += 1
                ins.then_inc(vec_step, 1)
                dve.wait_ge(vec_step, chain[0])

            asks, sums, feats, xts, prods = [0], [0], [0], [0], [0]

            def ask(ins):
                asks[0] += 1
                ins.then_inc(node_to_act, 1)
                dve.wait_ge(node_from_act, asks[0])

            def across(ins):
                sums[0] += 1
                ins.then_inc(node_to_pool, 1)
                dve.wait_ge(node_from_pool, sums[0])

            def per_node(v):
                return v[:, :].unsqueeze(2).to_broadcast([P, B, D])

            def layernorm_relu():
                link(nc.vector.tensor_reduce(MEAN[:, :], X[:, :, :], AX, ALU.add))
                link(nc.vector.tensor_scalar(MEAN[:, :], MEAN[:, :], 1.0 / D, None, ALU.mult))
                link(nc.vector.tensor_tensor(TMP1, X[:, :, :], per_node(MEAN), ALU.subtract))
                link(nc.vector.tensor_tensor(TMP2, TMP1, TMP1, ALU.mult))
                ask(nc.vector.tensor_reduce(VAR[:, :], TMP2, AX, ALU.add))
                link(nc.vector.reciprocal(STD[:, :], STD[:, :]))
                link(nc.vector.tensor_tensor(TMP1, TMP1, per_node(STD), ALU.mult))
                nc.vector.tensor_scalar(FEAT[:, :, :], TMP1, 0.0, None, ALU.max).then_inc(feat_ready, 1)

            def features_out():
                for g in range(GROUPS):
                    w = len(group(g)) * P
                    xts[0] += 1
                    dve.wait_ge(xt_psum, xts[0])
                    nc.vector.tensor_copy(XT[:, 4 * P * g:4 * P * g + w], PS[0:D, g, 0:w]).then_inc(xt_ready, 1)

            def products():
                for g in range(GROUPS):
                    prods[0] += 1
                    dve.wait_ge(prod_psum, prods[0])
                    yield g, 4 * g, 4 * g + len(group(g))

            def split3(src, rest, parts):
                link(nc.vector.tensor_copy(parts[:, :, 0:D], src))
                link(nc.vector.tensor_tensor(rest, src, parts[:, :, 0:D], ALU.subtract))
                link(nc.vector.tensor_copy(parts[:, :, D:2 * D], rest))
                link(nc.vector.tensor_tensor(rest, rest, parts[:, :, D:2 * D], ALU.subtract))
                return nc.vector.tensor_copy(parts[:, :, 2 * D:3 * D], rest)

            def scaled(s, last, scales=[0]):
                across(last)
                link(nc.vector.tensor_scalar(s[:, 0:1], s[:, 0:1], TINY, None, ALU.max))
                link(nc.vector.tensor_scalar(s[:, 1:2].bitcast(I32), s[:, 0:1].bitcast(I32), EXPONENT, None,
                                             ALU.bitwise_and))
                link(nc.vector.reciprocal(s[:, 2:3], s[:, 1:2]))
                link(nc.vector.tensor_scalar(s[:, 3:4], s[:, 1:2], 1.0 / TOP, None, ALU.mult))
                nc.vector.tensor_scalar(s[:, 2:3], s[:, 2:3], TOP, None, ALU.mult).then_inc(scale_ready, 1)
                scales[0] += 1
                dve.wait_ge(scale_ready, scales[0])

            def split2(s, k):
                scaled(s, nc.vector.tensor_reduce(s[:, 0:1], TMP1, mybir.AxisListType.XY, ALU.max, apply_absolute_value=True))
                dve.wait_ge(high_ready, k)
                return nc.vector.scalar_tensor_tensor(HALVES[:, :, D:2 * D], TMP1, s[:, 2:3], HALVES[:, :, 0:D],
                                                      ALU.mult, ALU.subtract)

            dve.sem_inc(cos_psum, 2 * RS)
            dve.sem_inc(ht_ready, 2)
            dve.sem_inc(acc_free, 1)
            dve.sem_inc(s_masked, PAIRS)
            dve.sem_inc(max_ready, RS)
            dve.sem_inc(hp_ready, 2)
            dve.sem_inc(conn_done, 1)
            dve.sem_inc(hp_stored[0], 16)
            dve.sem_inc(hp_stored[1], 16)
            dve.sem_inc(m_vec, 2)
            dve.sem_inc(msg_taken, 1)

            dve.wait_ge(x_loaded, 32)
            dve.wait_ge(constants_ready, CONSTANTS)
            dve.wait_ge(weights_loaded, 160)
            layernorm_relu()
            features_out()
            for g, lo, hi in products():
                nc.vector.tensor_scalar(TMP1[:, lo:hi, :], PS[:, g, 0:(hi - lo) * D].rearrange("p (b d) -> p b d", d=D),
                                        SUP_SCALE, None, ALU.mult).then_inc(prod_evac, 1)
            dve.wait_ge(prod_evac, prods[0])
            split3(TMP1, TMP2, PARTS[:, :, :]).then_inc(support_ready, 1)
            dve.wait_ge(support_ready, 1)

            def l0_tiles(sg, nb):
                w = nb // 2 * P
                for s in range(B):
                    for h in range(2):
                        n = sg * (2 * B) + (2 * s + h + 1)
                        dve.wait_ge(count_ready, n)
                        hold(dve, "dve", ht_psum, n)
                        nc.vector.tensor_copy(HTR[:, h, s % 2, 0:w], PS[:, h, 0:w]).then_inc(ht_ready, 1)
                    c = CHUNK_OF[s]
                    if s == CHUNK_AT[c]:
                        lo = (B - CHUNK_AT[c] - CHUNKS[c]) * P
                        hi = lo + CHUNKS[c] * P
                        hold(dve, "dve", cast_done, sg * NCH + (c + 1 + RING))
                        nc.vector.tensor_copy(H[:, bass.ds(sg * SG, nb), lo:hi].bitcast(I32),
                                              HS[:, 0:nb, lo:hi].bitcast(I32)).then_inc(kept, 1)
                hold(dve, "dve", acc_done, sg * B + (B + 2))
                for k in range(nb // 2):
                    last = nc.vector.tensor_reduce(
                        SUM0[:, 2 * k:2 * k + 2, :],
                        PS[:, 4 + k, 0:2 * 3 * D].rearrange("p (b t d) -> p b d t", b=2, t=3), AX, ALU.add)
                last.then_inc(acc_free, 1)
                hold(dve, "dve", acc_free, sg + 2)
                nc.vector.tensor_tensor(SUM1[:, 0:nb, :], SUM0[:, 0:nb, :],
                                        b0[:, :].unsqueeze(1).to_broadcast([P, nb, D]), ALU.add).then_inc(l0_biased, 1)
                hold(dve, "dve", l0_biased, sg + 1)
                rows = X[:, bass.ds(sg * SG, nb), :]
                nc.vector.tensor_tensor(rows, rows, SUM1[:, 0:nb, :], ALU.add).then_inc(l0_sum, 1)

            with dve.Fori(0, NSG) as sg:
                l0_tiles(sg, SG)
            l0_tiles(NSG, TAIL)
            dve.wait_ge(l0_sum, NSG + 1)

            for L in range(LAYERS):
                if L == 0:
                    link(nc.vector.tensor_reduce(MEAN[:, :], X[:, :, :], AX, ALU.add))
                    dve.wait_ge(deg_psum, NSG + 3)
                    for h in range(2):
                        link(nc.vector.tensor_scalar(
                            DEG[:, 0:NSG * SG].rearrange("p (s h k) -> p h s k", h=2, s=NSG)[:, h],
                            PS[:, 7 - h, 0:NSG * SG // 2].rearrange("p (s k) -> p s k", s=NSG), -1.0 / STEP, None, ALU.mult))
                        link(nc.vector.tensor_scalar(DEG[:, NSG * SG + h:NSG * SG + h + 1],
                                                     PS[:, 7 - h, NSG * SG // 2:NSG * SG // 2 + 1], -1.0 / STEP, None,
                                                     ALU.mult))
                    layernorm_relu()
                features_out()
                for g, lo, hi in products():
                    dve.wait_ge(xw_evac, GROUPS * L + g + 1)
                    link(nc.vector.tensor_reduce(LARGEST[:, g:g + 1],
                                                 PS[:, g, 0:(hi - lo) * 2 * D].rearrange("p (b c) -> p b c", c=2 * D)[:, :, D:2 * D],
                                                 mybir.AxisListType.XY, ALU.max, apply_absolute_value=True))
                scaled(SV, nc.vector.tensor_reduce(SV[:, 0:1], LARGEST[:, 0:GROUPS], AX, ALU.max))
                for g in range(GROUPS):
                    w = len(group(g)) * P
                    dve.wait_ge(q_psum, GROUPS * L + g + 1)
                    nc.vector.tensor_copy(ATT1[:, 4 * P * g:4 * P * g + w], PS[:, 7, 0:w]).then_inc(q_evac, 1)
                    b = group(g)
                    dve.wait_ge(v_high, GROUPS * L + g + 1)
                    last = nc.vector.scalar_tensor_tensor(
                        HALVES[:, b[0]:b[-1] + 1, D:2 * D],
                        PS[:, g, 0:len(b) * 2 * D].rearrange("p (b c) -> p b c", c=2 * D)[:, :, D:2 * D],
                        SV[:, 2:3], HALVES[:, b[0]:b[-1] + 1, 0:D], ALU.mult, ALU.subtract)
                last.then_inc(parts_ready, 1)
                dve.wait_ge(q_evac, GROUPS * (L + 1))
                scaled(SQ, nc.vector.tensor_reduce(SQ[:, 0:1], ATT1[:, :], AX, ALU.max, apply_absolute_value=True))
                SQUARES = ATT0[:, 0:B * D].rearrange("p (b d) -> p b d", b=B)
                link(nc.vector.tensor_tensor(SQUARES, XW, XW, ALU.mult))
                link(nc.vector.tensor_reduce(T_A[:, :], SQUARES, AX, ALU.add))
                ask(nc.vector.tensor_scalar(T_A[:, :], T_A[:, :], NORM_MIN, None, ALU.max))
                dve.wait_ge(q_high, L + 1)
                link(nc.vector.scalar_tensor_tensor(QA[D:2 * D, :], ATT1[D:2 * D, :], SQ[D:2 * D, 2:3], QA[D:2 * D, :],
                                                    ALU.mult, ALU.subtract))

                dve.wait_ge(half_done, 3 * L + 1)
                for g in range(GROUPS):
                    w = len(group(g)) * P
                    nc.vector.tensor_copy(ATT0[:, 4 * P * g:4 * P * g + w], PS[:, g, 0:w]).then_inc(et_evac, 1)
                for g in range(GROUPS):
                    w = len(group(g)) * P
                    dve.wait_ge(fold_psum, GROUPS * L + g + 1)
                    link(nc.vector.tensor_reduce(LARGEST[:, g:g + 1], PS[:, g, 0:w], AX, ALU.max,
                                                 apply_absolute_value=True))
                scaled(SE, nc.vector.tensor_reduce(SE[:, 0:1], LARGEST[:, 0:GROUPS], AX, ALU.max))
                link(nc.vector.tensor_tensor(UNDO[:, 0:1], SV[:, 3:4], SQ[:, 3:4], ALU.mult))
                link(nc.vector.tensor_tensor(UNDO[:, 0:1], UNDO[:, 0:1], SE[:, 3:4], ALU.mult))
                link(nc.vector.tensor_scalar(UNDO[:, 0:1], UNDO[:, 0:1], D ** -0.5 / H_FP8 / H_BYTE, None, ALU.mult))
                for g in range(GROUPS):
                    w = len(group(g)) * P
                    c = slice(4 * P * g, 4 * P * g + w)
                    dve.wait_ge(e_high, GROUPS * L + g + 1)
                    last = nc.vector.scalar_tensor_tensor(E22[:, c], PS[:, g, 0:w], SE[:, 2:3], E11[:, c],
                                                          ALU.mult, ALU.subtract)
                last.then_inc(stacks_ready, 1)
                dve.wait_ge(stacks_ready, 2 * L + 1)

                def weight(i, v):
                    u = v % 2
                    t = i + B * L
                    if isinstance(i, int) and i == B - 1:
                        dve.wait_ge(z_ready, t + 1)
                        link(nc.vector.reciprocal(RZT[:, :], ZROW[:, u:u + 1]))
                        nc.vector.tensor_scalar(RZ[:, u:u + 1], RZT[:, :], valid[:, B - 1:B], None,
                                                ALU.mult).then_inc(rz_ready, 1)
                    else:
                        hold(dve, "dve", z_ready, t + 1)
                        nc.vector.reciprocal(RZ[:, u:u + 1], ZROW[:, u:u + 1]).then_inc(rz_ready, 1)

                def masked(n, i, v, before=True):
                    u = v % 2
                    t = i + B * L
                    dve.wait_ge(tiles_loaded[v // 2], loaded_at(L, 0, n, v))
                    for q in range(PAIRS):
                        if q % 2 == 0:
                            dve.wait_ge(col_done, t * 2 + (q // 2 + 1))
                        hold(dve, "dve", s_psum, t * PAIRS + (q + 1))
                        for k, w in ((slice(0, 2), CW),) if q < PAIRS - 1 else ((slice(0, 1), CW), (slice(1, 2), CW - 1)):
                            nk = k.stop - k.start
                            c = q * PW + k.start * CW
                            m = q + k.start
                            last = nc.vector.tensor_tensor_reduce(
                                out=ATT[u][:, c:c + nk * w].rearrange("p (k c) -> p k c", k=nk),
                                in0=PS[:, SCORES_AT[q] + k.start:SCORES_AT[q] + k.stop, 0:w],
                                in1=HST[:, v, c:c + nk * w].rearrange("p (k c) -> p k c", k=nk),
                                scale=UNDO[:, 0:1], scalar=-3e38, op0=ALU.mult, op1=ALU.max,
                                accum_out=MX[:, u, m:m + 1])
                        last.then_inc(s_masked, 1)
                        if q == PAIRS - 2 and before:
                            weight(i - 1, (v - 1) % RS)
                    hold(dve, "dve", s_masked, t * PAIRS + 2 * PAIRS)
                    nc.vector.tensor_reduce(NEGM[:, u:u + 1], MX[:, u, :], AX, ALU.max, negate=True).then_inc(max_ready, 1)

                masked(0, 0, 0, before=False)
                with dve.Fori(0, ROUNDS) as n:
                    for v in range(RS):
                        masked(n + (v + 1) // RS, n * RS + (v + 1), (v + 1) % RS)
                masked(ROUNDS, B - 1, 1)
                weight(B - 1, 1)
                dve.wait_ge(col_done, 4 + 2 * B * (L + 1))
                nc.vector.tensor_scalar(ROWS, PS[:, 4:6, 0:CW], 1.0 / N, None, ALU.mult).then_inc(rows_ready, 1)

                dve.wait_ge(rows_psum, L + 1)
                link(nc.vector.tensor_scalar(T_A[:, :], PS[:, 6, 0:B], 0.5, None, ALU.mult))
                link(nc.vector.tensor_scalar(IMP[:, :], STR[:, :], 0.5, None, ALU.mult))
                link(nc.vector.tensor_tensor(IMP[:, :], IMP[:, :], T_A[:, :], ALU.add))

                def node_softmax(g, dst):
                    link(nc.vector.tensor_tensor(IMP[:, :], IMP[:, :], valid[:, :], ALU.mult))
                    link(nc.vector.tensor_tensor(IMP[:, :], IMP[:, :], far[:, :], ALU.add))
                    across(nc.vector.tensor_reduce(G1[:, g:g + 1], IMP[:, :], AX, ALU.max))
                    ask(nc.vector.tensor_scalar(G1[:, g + 1:g + 2], G1[:, g + 1:g + 2], -1.0, None, ALU.mult))
                    across(nc.vector.tensor_copy(G1[:, g + 2:g + 3], G1[:, g + 2:g + 3]))
                    link(nc.vector.tensor_scalar(G1[:, g + 3:g + 4], G1[:, g + 3:g + 4], TH[L], None, ALU.mult))
                    link(nc.vector.tensor_scalar(dst, EXPN[:, :], G1[:, g + 3:g + 4], None, ALU.is_ge))

                node_softmax(0, COMP[:, :])

                link(nc.vector.tensor_tensor(TMP1, FEAT[:, :, :], per_node(COMP), ALU.mult))
                link(nc.vector.tensor_tensor(TMP2, TMP1, TMP1, ALU.mult))
                link(nc.vector.tensor_reduce(T_A[:, :], TMP2, AX, ALU.add))
                ask(nc.vector.tensor_scalar(T_A[:, :], T_A[:, :], NORM_MIN, None, ALU.max))
                link(nc.vector.tensor_scalar(T_B[:, :], FMAG[:, :], 1e-8, None, ALU.max))
                link(nc.vector.reciprocal(T_B[:, :], T_B[:, :]))
                dve.wait_ge(rows_stored, 64 * (L + 1))
                link(nc.vector.tensor_tensor(DUP[:, :, 0:D], TMP1, per_node(T_B), ALU.mult))
                nc.vector.tensor_copy(DUP[:, :, D:2 * D], DUP[:, :, 0:D]).then_inc(dup_ready, 1)
                link(nc.vector.tensor_scalar(OFF[:, :], DEG[:, :], -0.5 * TH[L], 0.5 * TH[L] * N, ALU.mult, ALU.add))
                link(nc.vector.tensor_scalar(T_A[:, :], COMP[:, :], -FAR, FAR, ALU.mult, ALU.add))
                link(nc.vector.tensor_tensor(OFF[:, :], OFF[:, :], T_A[:, :], ALU.add))
                for g in range(GROUPS):
                    w = len(group(g)) * P
                    c = slice(4 * P * g, 4 * P * g + w)
                    dve.wait_ge(c_high, GROUPS * L + g + 1)
                    link(nc.vector.scalar_tensor_tensor(C22[:, c], PS[:, g, 0:w], COS_SCALE, C11[:, c],
                                                        ALU.mult, ALU.subtract))
                nc.vector.tensor_copy(CA[0:D, :], C11[0:D, :])
                nc.vector.tensor_copy(CA[D:2 * D, :], C22[D:2 * D, :]).then_inc(stacks_ready, 1)
                dve.wait_ge(stacks_ready, 2 * L + 2)

                def prune(n, i, v):
                    u = v % 2
                    t = i + B * L
                    dve.wait_ge(hp_stored[u], n * (8 * RS) + (B // 2 * L + v // 2 + 1) * 16)
                    if v == 0:
                        dve.wait_ge(conn_done, n + ((ROUNDS + 1) * L + 1))
                    hold(dve, "dve", thr_done, t + 1)
                    nc.vector.tensor_scalar(HPST[:, u, :].bitcast(FP8), ATT[u], THR[:, u:u + 1], None,
                                            ALU.is_ge, ALU.add, accum_out=CN[:, v:v + 1],
                                            saturate=False).then_inc(hp_ready, 1)
                    if v == RS - 1 or (isinstance(i, int) and i == B - 1):
                        hold(dve, "dve", hp_ready, t + 3)
                        nc.vector.tensor_copy(CONN[:, bass.ds(i - v, v + 1)], CN[:, 0:v + 1]).then_inc(conn_done, 1)

                all_tiles(dve, prune)
                dve.wait_ge(conn_done, 1 + (ROUNDS + 1) * (L + 1))

                link(nc.vector.tensor_tensor(IMP[:, :], CONN[:, :], FMAG[:, :], ALU.mult))
                node_softmax(4, NMASK[:, :])
                link(nc.vector.tensor_scalar(T_B[:, :], CONN[:, :], 0.0, None, ALU.is_gt))
                link(nc.vector.tensor_tensor(NMASK[:, :], NMASK[:, :], T_B[:, :], ALU.mult))
                link(nc.vector.tensor_tensor(NMASK[:, :], NMASK[:, :], COMP[:, :], ALU.mult))
                ask(nc.vector.tensor_scalar(T_A[:, :], CONN[:, :], EPS, None, ALU.max))
                link(nc.vector.reciprocal(DV[:, :], DV[:, :]))
                link(nc.vector.tensor_tensor(NMASK[:, :], NMASK[:, :], DV[:, :], ALU.mult))
                link(nc.vector.tensor_tensor(TMP1, XW, per_node(NMASK), ALU.mult))
                split2(ST, 2 * L + 1).then_inc(parts_ready, 1)
                dve.wait_ge(parts_ready, 3 * L + 2)

                for hf in range(2):
                    dve.wait_ge(half_done, 3 * L + hf + 2)
                    for bank in range((HB + 2) // 3):
                        nb = min(3, HB - 3 * bank)
                        b = hf * HB + 3 * bank
                        src = PS[:, bank, 0:nb * EW].rearrange("p (b c) -> p b c", b=nb)
                        nc.vector.tensor_copy(EDEG[:, b:b + nb], src[:, :, 2 * D])
                        last = nc.vector.tensor_reduce(TMP1[:, b:b + nb, :],
                                                       src[:, :, 0:2 * D].rearrange("p b (t d) -> p b d t", t=2), AX, ALU.add)
                    last.then_inc(half_evac, 1)
                dve.wait_ge(half_evac, 2 * L + 2)
                link(nc.vector.tensor_scalar(EDEG[:, :], EDEG[:, :], EPS, None, ALU.max))
                link(nc.vector.reciprocal(EDEG[:, :], EDEG[:, :]))
                link(nc.vector.tensor_tensor(TMP1, TMP1, per_node(EDEG), ALU.mult))
                split2(SA, 2 * L + 2).then_inc(parts_ready, 1)
                dve.wait_ge(parts_ready, 3 * L + 3)
                link(nc.vector.tensor_tensor(UNDO[:, 1:2], ST[:, 3:4], SA[:, 3:4], ALU.mult))
                link(nc.vector.tensor_scalar(DV[:, :], DV[:, :], UNDO[:, 1:2], None, ALU.mult))

                def tile_out(n, i, v):
                    u = v % 2
                    t = i + B * L
                    dve.wait_ge(msg_done, t + 1)
                    for g in (0, 2):
                        hold(dve, "dve", m_psum, t * PAIRS + (g + 1 + RS * PAIRS))
                        nc.vector.tensor_copy(HPT[u][:, 8 * P * g:8 * P * (g + 1)],
                                              PS[:, TILES_AT[g]:TILES_AT[g] + 2, :].rearrange("p k c -> p (k c)")).then_inc(m_vec, 1)

                def message(i, v):
                    hold(dve, "dve", msg_done, i + (B * L + 3))
                    nc.vector.tensor_reduce(FEAT[:, bass.ds(i, 1), :],
                                            PS[:, 6, 0:2 * D].rearrange("p (o t d) -> p o d t", o=1, t=2),
                                            AX, ALU.add).then_inc(msg_taken, 1)

                all_tiles_ahead(dve, tile_out, message)
                dve.wait_ge(msg_taken, 1 + B * (L + 1))
                nc.vector.tensor_tensor(FEAT[:, :, :], FEAT[:, :, :], per_node(DV), ALU.mult).then_inc(feat_ready, 1)
                features_out()
                for g, lo, hi in products():
                    nc.vector.tensor_scalar(FEAT[:, lo:hi, :], PS[:, g, 0:(hi - lo) * D].rearrange("p (b d) -> p b d", d=D),
                                            0.0, None, ALU.max).then_inc(prod_evac, 1)
                dve.wait_ge(prod_evac, GROUPS * (L + 2))
                if L < LAYERS - 1:
                    dve.sem_inc(feat_ready)
            nc.vector.tensor_tensor(X[:, :, :], X[:, :, :], FEAT[:, :, :], ALU.add).then_inc(feat_ready, 1)

        @block.tensor
        def _(pe):
            pe.sem_inc(cols_used, NCH)
            pe.sem_inc(count_ready, 2)
            pe.sem_inc(acc_done, 2)
            pe.sem_inc(e_used, RS)
            pe.sem_inc(col_done, 4)
            pe.sem_inc(g_used, RS)
            pe.sem_inc(m_psum, RS * PAIRS)
            pe.sem_inc(msg_done, 2)
            feats, xts, prods = [0], [0], [0]

            def features():
                feats[0] += 1
                pe.wait_ge(feat_ready, feats[0])
                for g in range(GROUPS):
                    for k, b in enumerate(group(g)):
                        last = nc.tensor.transpose(PS[0:D, g, k * P:(k + 1) * P], FEAT[:, b, :], identF[:, :])
                    last.then_inc(xt_psum, 1)

            def product(w, xt=XT):
                cols = w.shape[1]
                for g in range(GROUPS):
                    xts[0] += 1
                    pe.wait_ge(xt_ready, xts[0])
                    for k, b in enumerate(group(g)):
                        last = nc.tensor.matmul(PS[:, g, k * cols:(k + 1) * cols], xt[:, b * P:(b + 1) * P], w,
                                                start=True, stop=True)
                    last.then_inc(prod_psum, 1)
                prods[0] += GROUPS

            def zero_bank(bank, w):
                return nc.tensor.matmul(PS[:, bank, 0:w], zeros[:, 0:P], zeros[:, 0:w], start=True, stop=True)

            def add(o, lhsT, rhs):
                return nc.tensor.matmul(o, lhsT, rhs, start=False, stop=True, skip_group_check=True)

            pe.wait_ge(constants_ready, CONSTANTS)
            pe.wait_ge(weights_loaded, 160)
            features()
            product(w0[:, :])
            pe.wait_ge(support_ready, 1)

            def l0_group(sg, nb):
                nh = nb // 2
                w = nh * P

                def accumulate(s, inc_cols):
                    jb = B - 1 - s
                    pe.wait_ge(w_ready, sg * (2 * B) + (2 * s + 2))
                    for b in range(nb):
                        h, k = b // nh, b % nh
                        o = (b % 2) * 3 * D
                        last = add(PS[:, 4 + b // 2, o:o + 3 * D],
                                   WTR[:, h, s % 2, k * P:(k + 1) * P].bitcast(BF16), PARTS[:, jb, :])
                        if b == 0 and inc_cols:
                            last.then_inc(cols_used, 1)
                    last.then_inc(acc_done, 1)

                def transpose(s, h):
                    jb = B - 1 - s
                    c = CHUNK_OF[s]
                    if h == 0 and s == CHUNK_AT[c]:
                        pe.wait_ge(cast_done, sg * NCH + (RING + c + 1))
                    hold(pe, "pe", ht_ready, sg * (2 * B) + (2 * s + h + 1))
                    for k in range(nh):
                        last = nc.tensor.matmul(PS[:, h, k * P:(k + 1) * P],
                                                HS[:, h * nh + k, jb * P:(jb + 1) * P].bitcast(FP8),
                                                half_ident[:, :], start=True, stop=True)
                    last.then_inc(ht_psum, 1)

                def count(s, h):
                    pe.wait_ge(ht_ready, sg * (2 * B) + (2 * s + h + 3))
                    tile = HTR[:, h, s % 2, 0:w]
                    if s == 0:
                        if h == 0:
                            pe.wait_ge(deg_rows, sg + 1)
                        last = nc.tensor.matmul(PS[:, 2 + h, 0:w], count_first[:, :], tile, start=True, stop=True)
                    else:
                        pe.wait_ge(w_ready, sg * (2 * B) + (2 * s + h - 1))
                        add(PS[:, 2 + h, 0:w], count_next[:, :], HTR[:, h, (s - 1) % 2, 0:w])
                        last = add(PS[:, 2 + h, 0:w], count_first[:, :], tile)
                    last.then_inc(count_ready, 1)

                for h in range(2):
                    transpose(0, h)
                for s in range(B):
                    for h in range(2):
                        count(s, h)
                        if s + 1 < B:
                            transpose(s + 1, h)
                    if s == 0:
                        pe.wait_ge(acc_free, sg + 1)
                        for k in range(nb // 2):
                            last = zero_bank(4 + k, 2 * 3 * D)
                        last.then_inc(cols_used, 2)
                    else:
                        c = CHUNK_OF.get(s + 1)
                        accumulate(s - 1, c is not None and s + 1 == CHUNK_AT[c] + CHUNKS[c] - 1)
                accumulate(B - 1, False)
                for h in range(2):
                    last = add(PS[:, 2 + h, 0:w], count_next[:, :], HTR[:, h, (B - 1) % 2, 0:w])
                last.then_inc(deg_psum, 1)

            with pe.Fori(0, NSG) as sg:
                l0_group(sg, SG)
            l0_group(NSG, TAIL)

            def doubled(k):
                pe.wait_ge(dup_ready, k)
                for g in range(GROUPS):
                    for j, b in enumerate(group(g)):
                        last = nc.tensor.transpose(PS[:, g, j * P:(j + 1) * P], DUP[:, b, :], identF[:, :])
                    last.then_inc(dup_psum, 1)

            pe.wait_ge(deg_rows, NSG + 2)
            for h in range(2):
                row = FEAT[32 * h:32 * h + 1, :, :].rearrange("p b d -> p (b d)")
                for j in range(NSG * SG // 2 + 1):
                    last = nc.tensor.matmul(PS[:, 7 - h, j:j + 1], row[:, j * P:(j + 1) * P], ones[32 * h:32 * h + 1, :],
                                            start=True, stop=True)
                last.then_inc(deg_psum, 1)

            for L in range(LAYERS):
                features()
                pe.wait_ge(ones_row, L + 1)
                product(wwv[:, :], XT1)
                for g in range(GROUPS):
                    w = len(group(g)) * P
                    if L or g:
                        pe.wait_ge(q_evac, GROUPS * L + g)
                    nc.tensor.matmul(PS[:, 7, 0:w], wqq[:, :], XT1[:, 4 * P * g:4 * P * g + w],
                                     start=True, stop=True).then_inc(q_psum, 1)
                pe.wait_ge(parts_ready, 3 * L + 1)
                for g in range(GROUPS):
                    zero_bank(g, len(group(g)) * P)

                for i in range(B):
                    pe.wait_ge(e_row_ready, B * L + i + 1)
                    for g in range(GROUPS):
                        w = len(group(g)) * P
                        last = add(PS[:, g, 0:w], PROW[:, i % RS, 0:2 * D],
                                   H[:, i, 4 * P * g:4 * P * g + w].bitcast(FP8))
                    last.then_inc(e_used, 1)
                zero_bank(7, P).then_inc(half_done, 1)
                for g in range(GROUPS):
                    w = len(group(g)) * P
                    pe.wait_ge(et_evac, GROUPS * L + g + 1)
                    nc.tensor.matmul(PS[:, g, 0:w], fold[:, :], ATT0[:, 4 * P * g:4 * P * g + w],
                                     start=True, stop=True).then_inc(fold_psum, 1)

                def scores(i, q):
                    pe.wait_ge(s_masked, i * PAIRS + (B * L * PAIRS + SCORES_WAIT[q]))
                    for rhs in (E11, E22):
                        for k in range(2):
                            c = 2 * q + k
                            last = nc.tensor.matmul(PS[:, SCORES_AT[q] + k, 0:CW], QA[:, bass.ds(i * P, P)],
                                                    rhs[:, c * CW:(c + 1) * CW], start=rhs is E11, stop=rhs is E22)
                    last.then_inc(s_psum, 1)

                def column_sums(i, u, k):
                    if k == 0:
                        pe.wait_ge(rz_ready, i + (B * L + 1))
                    for q in range(4):
                        c = 4 * k + q
                        last = add(PS[32 * q:32 * q + 1, 4 + k, 0:CW], RZ[:, u:u + 1],
                                   ATT[u][:, c * CW:(c + 1) * CW])
                    last.then_inc(col_done, 1)

                def attention(i, u, first=False, second=False, last=False):
                    scores(i, 1)
                    scores(i, 2)
                    if not (first or second):
                        column_sums(i - 2, u, 1)
                    scores(i, 3)
                    if not last:
                        scores(i + 1, 0)
                    if not first:
                        column_sums(i - 1, 1 - u, 0)

                pe.wait_ge(stacks_ready, 2 * L + 1)
                for bank in (4, 5):
                    zero_bank(bank, CW)
                scores(0, 0)
                attention(0, 0, first=True)
                attention(1, 1, second=True)
                with pe.Fori(0, HB - 2) as n:
                    for u in range(2):
                        attention(n * 2 + (2 + u), u)
                attention(B - 2, 0)
                attention(B - 1, 1, last=True)
                column_sums(B - 2, 0, 1)
                for k in range(2):
                    column_sums(B - 1, 1, k)
                pe.wait_ge(rows_back, 16 * (L + 1))
                nc.tensor.transpose(PS[:, 6, 0:B], ATR[:, :], identF[0:B, 0:B]).then_inc(rows_psum, 1)

                doubled(L + 1)
                pe.wait_ge(stacks_ready, 2 * L + 2)

                def cosines(n, i, v):
                    pe.wait_ge(g_ready, i + (B * L + 1 + RS))
                    for q in range(2):
                        hold(pe, "pe", exp_done, i * 2 + (2 * B * L + q + 1))
                        for k in range(4):
                            c = 4 * q + k
                            nc.tensor.matmul(PS[:, c, 0:CW], mask_ident[:, :],
                                             GST[:, v, c * CW:(c + 1) * CW].bitcast(FP8), start=True, stop=False)
                        for rhs in (C11, C22):
                            for k in range(4):
                                c = 4 * q + k
                                last = nc.tensor.matmul(PS[:, c, 0:CW], CA[:, bass.ds(i * P, P)],
                                                        rhs[:, c * CW:(c + 1) * CW], start=False, stop=rhs is C22)
                        last.then_inc(cos_psum, 1)

                all_tiles(pe, cosines)

                pe.wait_ge(parts_ready, 3 * L + 2)
                for hf in range(2):
                    if hf:
                        pe.wait_ge(half_evac, 2 * L + 1)
                    for bank in range((HB + 2) // 3):
                        zero_bank(bank, min(3, HB - 3 * bank) * EW)

                    def edges(n, i, v):
                        pe.wait_ge(tiles_loaded[v // 2], loaded_at(L, 2 + hf, n, v))
                        hold(pe, "pe", g_row_ready, i + (B * (2 * L + hf) + 1))
                        for j in range(HB):
                            o = (j % 3) * EW
                            last = add(PS[:, j // 3, o:o + EW], HST[:, v, j * P:(j + 1) * P].bitcast(FP8),
                                       PROW[:, v, 0:EW])
                        last.then_inc(g_used, 1)

                    all_tiles(pe, edges)
                    zero_bank(7, P).then_inc(half_done, 1)

                def transposes(n, i, v):
                    for g in range(PAIRS):
                        if g == 0:
                            pe.wait_ge(tiles_loaded[v // 2], loaded_at(L, 4, n, v))
                        hold(pe, "pe", (m_vec, m_act)[g % 2], i * 2 + (2 * B * L + g // 2 + 1))
                        for b in range(8 * g, min(8 * g + 8, B)):
                            last = nc.tensor.matmul(PS[:, TILES_AT[g] + (b % 8) // 4, (b % 4) * P:(b % 4 + 1) * P],
                                                    HST[:, v, b * P:(b + 1) * P].bitcast(FP8), ident[:, :],
                                                    start=True, stop=True)
                        last.then_inc(m_psum, 1)

                def messages(i, v):
                    pe.wait_ge(m_vec, i * 2 + (2 * B * L + 4))
                    pe.wait_ge(m_act, i * 2 + (2 * B * L + 4))
                    pe.wait_ge(msg_taken, i + (B * L + 1))
                    for b in range(B):
                        last = nc.tensor.matmul(PS[:, 6, 0:2 * D], HPT[v % 2][:, b * P:(b + 1) * P],
                                                HALVES[:, b, :], start=b == 0, stop=b == B - 1)
                    last.then_inc(msg_done, 1)

                pe.wait_ge(parts_ready, 3 * L + 3)
                all_tiles_ahead(pe, transposes, messages)
                features()
                product(wth[:, :])


CONSTANTS = 30

_INS = ["x", "adj", "L0_gnn_weight", "L0_gnn_bias", "L1_gnn_W", "L1_gnn_Theta", "L1_gnn_Wq", "L1_gnn_bq",
        "L1_gnn_Wv", "L1_gnn_bv"]
_OUTS = [((3327, 64), "float32")]


def kernel(**inputs):
    import numpy as _np
    import concourse.bacc as _bacc
    from concourse import mybir as _mybir
    from concourse.bass_utils import run_bass_kernel_spmd as _run

    nc = _bacc.Bacc("TRN2", target_bir_lowering=False, num_devices=1)
    arrays, args = {}, []
    for name in _INS:
        a = _np.ascontiguousarray(inputs[name])
        arrays[f"in_{name}_dram"] = a
        args.append(nc.dram_tensor(f"in_{name}_dram", a.shape, _mybir.dt.from_np(a.dtype), kind="ExternalInput").ap())
    for i, (shape, dtype) in enumerate(_OUTS):
        dt = _mybir.dt.from_np(_np.dtype(dtype))
        args.append(nc.dram_tensor(f"out_{i}_dram", shape, dt, kind="ExternalOutput").ap())
    bass_adj_preln_gnn_hypergraph(nc, *args)
    r = _run(nc, [arrays], core_ids=[0])
    return r.results[0]["out_0_dram"]
```

```python
import concourse.bass as bass
from concourse import mybir
from contextlib import ExitStack


def bass_adj_preln_gnn_hypergraph(
    nc: bass.Bass,
    x: bass.AP,
    adj: bass.AP,
    l0_weight: bass.AP,
    l0_bias: bass.AP,
    W: bass.AP,
    Theta: bass.AP,
    Wq: bass.AP,
    bq: bass.AP,
    Wv: bass.AP,
    bv: bass.AP,
    out: bass.AP,
):
    F32 = mybir.dt.float32
    BF16 = mybir.dt.bfloat16
    FP16 = mybir.dt.float16
    FP8 = mybir.dt.float8e4
    U8 = mybir.dt.uint8
    I16 = mybir.dt.int16
    I32 = mybir.dt.int32
    ALU = mybir.AluOpType
    ACT = mybir.ActivationFunctionType
    AX = mybir.AxisListType.X
    RMAX = bass.bass_isa.ReduceOp.max
    RADD = bass.bass_isa.ReduceOp.add

    N, D = x.shape
    P = 128
    B = (N + P - 1) // P
    NP = B * P
    LAST = N - (B - 1) * P
    PADCOLS = NP - N
    assert PADCOLS == 1 and B % 2 == 0
    LAYERS = 2
    LN_EPS = 1e-5
    EPS = 1e-6
    NORM_MIN = 1e-16
    MAX_NEIGH = 100
    TH = [0.000244, 0.000244 + (1.0 - 2.718281828459045 ** (-0.1)) * (0.0003 - 0.000244)]
    FAR = 1e30

    H_BYTE = 64.0
    H_FP8 = 2.0

    STEP = 128.0
    OWN = 128.0 * STEP
    W_BIAS = MAX_NEIGH * STEP - OWN
    SUP_SCALE = 2.0 ** (127 - MAX_NEIGH)

    SG = 7
    NSG = B // SG
    TAIL = B - NSG * SG
    CHUNKS = [1] * 4 + [2] * ((B - 4) // 2)
    NCH = len(CHUNKS)
    RING = 5
    ROUND = NCH // RING
    assert NCH == ROUND * RING
    CHUNK_AT = [sum(CHUNKS[:c]) for c in range(NCH)]
    CHUNK_OF = {CHUNK_AT[c] + k: c for c in range(NCH) for k in range(CHUNKS[c])}

    RS = 4
    ROUNDS = B // RS
    ARS = 6
    AROUNDS = B // ARS
    assert B == ARS * AROUNDS + 2
    assert B == RS * ROUNDS + 2
    PAIR0, PAIR1 = ROUNDS + 1, ROUNDS
    HALF = NP // 2
    HRS = 2 * RS
    HROUNDS = B // HRS
    assert B == HRS * HROUNDS + 2
    HB = B // 2
    EW = 2 * D + 1
    CW = NP // 8
    PW = 2 * CW
    PAIRS = NP // PW
    HT_AT = [[0, 6], [1, 7]]
    TILES_AT = [0, 2, 4, 7]
    SCORES_AT = [0, 2, 6, 2]
    SCORES_WAIT = [1, 4, 3, PAIRS + 2]
    GROUPS = (B + 3) // 4

    TOP = 2.0 ** 14
    TINY = 2.0 ** -100
    EXPONENT = 0x7F800000
    E_SCALE = 2.0 ** -13
    COS_SCALE = 2.0 ** 15
    COS_UNIT = COS_SCALE * COS_SCALE
    MASK_OFF = -128.0 * COS_UNIT

    def halves(nb):
        return (0, (nb + 1) // 2), ((nb + 1) // 2, nb // 2)

    SPLIT = ((0, 12), (12, B))
    SPLIT_HALF = ((0, HB), (HB, B))

    def group(g):
        return range(4 * g, min(4 * g + 4, B))

    ctx = ExitStack()
    with ctx:
        def sb(name, shape, dt):
            return ctx.enter_context(nc.sbuf_tensor(name, shape, dt))

        def sem(name):
            return ctx.enter_context(nc.semaphore(name))

        H = sb("H", [P, B, NP], U8)
        X = sb("X", [P, B, D], F32)
        FEAT = sb("FEAT", [P, B, D], F32)
        HALVES = sb("HALVES", [P, B, 2 * D], FP16)
        XTb = sb("XTb", [P, NP], F32)
        ATT1 = sb("ATT1", [P, NP], F32)
        ARENA = sb("ARENA", [P, 16384], F32)

        XT = XTb[0:D, :]
        XT1 = XTb[0:D + 1, :]
        TMP1 = ATT1[:, 0:B * D].rearrange("p (b d) -> p b d", b=B)
        TMP2 = ATT1[:, B * D:2 * B * D].rearrange("p (b d) -> p b d", b=B)

        at = [0]

        def carve(words, dt=F32):
            a = ARENA[:, at[0]:at[0] + words]
            at[0] += words
            return a if dt == F32 else a.bitcast(dt)

        FST = carve(RING * SG * 2 * P).rearrange("p (r b c) -> p r b c", r=RING, b=SG)
        HS = carve(SG * NP // 4, U8).rearrange("p (b c) -> p b c", b=SG)
        assert at[0] <= 16384
        HTILE = (SG + 1) // 2 * P
        HTR = XTb[:, 0:4 * HTILE].bitcast(BF16).rearrange("p (h k c) -> p h k c", h=2, k=4)
        WTR = XTb[:, 4 * HTILE:6 * HTILE].bitcast(I16).rearrange("p (h k c) -> p h k c", h=2, k=2)
        DEG_ROWS = ATT1[:, 0:(NSG + 1) * HTILE]
        SUM0 = ATT1[:, (NSG + 1) * HTILE:(NSG + 1) * HTILE + SG * D].rearrange("p (b d) -> p b d", b=SG)
        SUM1 = ATT1[:, (NSG + 1) * HTILE + SG * D:(NSG + 1) * HTILE + 2 * SG * D].rearrange("p (b d) -> p b d", b=SG)

        at[0] = 0
        QA = carve(NP // 2, FP16)
        E11 = carve(NP // 2, FP16)
        E22 = carve(NP // 2, FP16)
        ATT0 = carve(NP)
        XW = carve(B * D).rearrange("p (b d) -> p b d", b=B)
        HST = carve(RS * NP // 4, U8).rearrange("p (u c) -> p u c", u=RS)
        HSTH = HST.rearrange("p u c -> p (u c)").rearrange("p (u c) -> p u c", u=HRS)
        HPST = carve(2 * NP // 4, U8).rearrange("p (u c) -> p u c", u=2)
        AHST = ARENA[:, at[0] - ARS * NP // 4:at[0]].bitcast(U8).rearrange("p (u c) -> p u c", u=ARS)
        assert at[0] <= 16384
        CA, C11, C22 = QA, E11, E22
        ROWS = HPST.rearrange("p u c -> p (u c)").bitcast(F32)[:, 0:2 * CW].rearrange("p (k c) -> p k c", k=2)
        DUP = ATT1[:, :].rearrange("p (b d) -> p b d", b=B)
        SQUARES = ATT0[:, 0:B * D].rearrange("p (b d) -> p b d", b=B)
        XN = ATT0[:, B * D:2 * B * D].rearrange("p (b d) -> p b d", b=B)
        AHALVES = ATT0[:, NP // 2:NP].bitcast(FP16).rearrange("p (b d) -> p b d", b=B)
        GST = XTb[:, :].bitcast(U8).rearrange("p (u c) -> p u c", u=RS)
        ATT = [ATT0, ATT1[:, :]]
        SCORES = [ATT0, ATT1[:, :], XTb[:, :]]
        HPT = [ATT0.bitcast(BF16)[:, 0:NP], ATT1[:, 0:NP // 2].bitcast(BF16)]

        PROW = sb("PROW", [P, RS, 2 * D + 2], FP16)
        fold = sb("fold", [P, P], F32)
        ones = sb("ones", [P, 1], F32)
        identF = sb("identF", [P, P], F32)
        half_ident = sb("half_ident", [P, P], BF16)
        ident = sb("ident", [P, P], BF16)
        mask_ident = sb("mask_ident", [P, P], BF16)
        count_first = sb("count_first", [P, P], BF16)
        count_next = sb("count_next", [P, P], BF16)
        zeros = sb("zeros", [P, 512], BF16)
        valid = sb("valid", [P, B], F32)
        far = sb("far", [P, B], F32)
        cast_by = sb("cast_by", [P, 1], F32)
        eps = sb("eps", [P, 3], F32)
        w0 = sb("w0", [D, D], F32)
        wwv = sb("wwv", [D + 1, 2 * D], F32)
        wqq = sb("wqq", [D + 1, 2 * D], F32)
        wth = sb("wth", [D, D], F32)
        b0 = sb("b0", [P, D], F32)
        (MEAN, VAR, STD, STR, DEG, OFF, COMP, IMP, EXPN, FMAG, CONN, NMASK, DV, EDEG, T_A, T_B) = [
            sb(n, [P, B], F32) for n in ("MEAN", "VAR", "STD", "STR", "DEG", "OFF", "COMP", "IMP", "EXPN",
                                         "FMAG", "CONN", "NMASK", "DV", "EDEG", "T_A", "T_B")]
        LARGEST = sb("LARGEST", [P, 8], F32)
        WARM = sb("WARM", [P, 1], F32)
        S0, SV, SQ, ST = [sb(n, [P, 4], F32) for n in ("S0", "SV", "SQ", "ST")]
        UNDO = sb("UNDO", [P, 2], F32)
        ATR = sb("ATR", [B, P], F32)
        MX = sb("MX", [P, 2, PAIRS + 1], F32)
        NEGM = sb("NEGM", [P, 2], F32)
        ZROW = sb("ZROW", [P, 2], F32)
        RZ = sb("RZ", [P, 2], F32)
        RZT = sb("RZT", [P, 1], F32)
        ZC = sb("ZC", [P, 2, 2], F32)
        ZS = sb("ZS", [P, 2, 2], F32)
        THR = sb("THR", [P, 2], F32)
        CN = sb("CN", [P, RS], F32)
        G1 = sb("G1", [P, 8], F32)

        PS = ctx.enter_context(nc.psum_tensor("PS", [P, 8, 512], F32))

        att_dram = nc.dram_tensor("att_row", [NP], F32)
        att_rows = att_dram[:].rearrange("(k q c) -> q k c", k=2, q=4)
        att_back = att_dram[:].rearrange("(b p) -> b p", p=P)
        hp_dram = nc.dram_tensor("h_pruned", [B, P, NP], U8)

        w0_loaded = sem("w0_loaded")
        weights_loaded = sem("weights_loaded")
        x_loaded = sem("x_loaded")
        pads_zeroed = sem("pads_zeroed")
        constants_ready = sem("constants_ready")
        vec_step = sem("vec_step")
        node_to_act = sem("node_to_act")
        node_from_act = sem("node_from_act")
        node_to_pool = sem("node_to_pool")
        node_from_pool = sem("node_from_pool")
        feat_ready = sem("feat_ready")
        xt_psum = sem("xt_psum")
        xt_ready = sem("xt_ready")
        prod_psum = sem("prod_psum")
        prod_evac = sem("prod_evac")
        q_psum = sem("q_psum")
        q_evac = sem("q_evac")
        support_ready = sem("support_ready")
        adj_loaded = [sem(f"adj_loaded{r}") for r in range(RING)]
        cast_done = sem("cast_done")
        kept = sem("kept")
        cols_used = sem("cols_used")
        ht_psum = sem("ht_psum")
        ht_ready = sem("ht_ready")
        count_ready = sem("count_ready")
        w_ready = sem("w_ready")
        acc_done = sem("acc_done")
        acc_free = sem("acc_free")
        l0_sum = sem("l0_sum")
        l0_biased = sem("l0_biased")
        parts_ready = sem("parts_ready")
        deg_rows = sem("deg_rows")
        deg_psum = sem("deg_psum")
        deg_taken = sem("deg_taken")
        ones_row = sem("ones_row")
        xt_ready_act = sem("xt_ready_act")
        centred = sem("centred")
        squared = sem("squared")
        l0_high = sem("l0_high")
        et_evac_act = sem("et_evac_act")
        c_low = sem("c_low")
        off_ready = sem("off_ready")
        t_ready = sem("t_ready")
        scale_ready = sem("scale_ready")
        high_ready = sem("high_ready")
        v_high = sem("v_high")
        xw_evac = sem("xw_evac")
        et_evac = sem("et_evac")
        fold_psum = sem("fold_psum")
        e_high = sem("e_high")
        q_high = sem("q_high")
        c_high = sem("c_high")
        tiles_loaded = [sem(f"tiles_loaded{k}") for k in range(4)]
        e_row_ready = sem("e_row_ready")
        e_used = sem("e_used")
        half_evac = sem("half_evac")
        dup_first = sem("dup_first")
        dup_ready = sem("dup_ready")
        dup_psum = sem("dup_psum")
        stacks_ready = sem("stacks_ready")
        s_psum = sem("s_psum")
        s_masked = sem("s_masked")
        max_ready = sem("max_ready")
        z_ready = sem("z_ready")
        rz_ready = sem("rz_ready")
        col_done = sem("col_done")
        rows_ready = sem("rows_ready")
        rows_stored = sem("rows_stored")
        rows_back = sem("rows_back")
        rows_psum = sem("rows_psum")
        g_ready = sem("g_ready")
        cos_psum = sem("cos_psum")
        exp_done = sem("exp_done")
        thr_done = sem("thr_done")
        hp_ready = sem("hp_ready")
        conn_done = sem("conn_done")
        hp_stored = [sem(f"hp_stored{u}") for u in range(2)]
        g_row_ready = sem("g_row_ready")
        g_used = sem("g_used")
        m_psum = sem("m_psum")
        m_vec = sem("m_vec")
        m_act = sem("m_act")
        msg_done = sem("msg_done")
        msg_taken = sem("msg_taken")
        out_stored = sem("out_stored")
        held = {e: sem("held_" + e) for e in ("pe", "act", "dve", "pool", "sp")}

        block = ctx.enter_context(nc.Block())

        def hold(eng, name, s, value):
            eng.wait_ge(s, value)
            eng.sem_inc(held[name])

        def all_tiles(eng, body, size=RS):
            with eng.Fori(0, B // size) as n:
                for v in range(size):
                    body(n, n * size + v, v)
            for v in range(2):
                body(B // size, B // size * size + v, v)

        def all_tiles_ahead(eng, first, second):
            first(0, 0, 0)
            with eng.Fori(0, ROUNDS) as n:
                for v in range(RS):
                    first(n + (v + 1) // RS, n * RS + (v + 1), (v + 1) % RS)
                    second(n * RS + v, v)
            first(ROUNDS, B - 1, 1)
            second(B - 2, 0)
            second(B - 1, 1)

        HLOADS = [tuple(HROUNDS + (k == hf) for k in range(4)) for hf in range(2)]
        ALOADS = (AROUNDS + 1, AROUNDS, AROUNDS, 0)
        LOADS = (ALOADS, (PAIR0, PAIR1, 0, 0), HLOADS[0], HLOADS[1], (PAIR0, PAIR1, 0, 0))

        def loaded_at(L, step, n, k):
            before = L * sum(c[k] for c in LOADS) + sum(c[k] for c in LOADS[:step])
            return n * 16 + 16 * (before + 1)

        @block.sync
        def _(sp):
            sp.dma_start(X[:, 0:B - 1, :],
                         x[0:(B - 1) * P, :].rearrange("(b p) d -> p b d", p=P)).then_inc(x_loaded, 16)
            sp.wait_ge(pads_zeroed, 1)
            sp.dma_start(X[0:LAST, B - 1, :], x[(B - 1) * P:N, :]).then_inc(x_loaded, 16)

            def cols(c):
                first = B - CHUNK_AT[c] - CHUNKS[c]
                lo = first * P
                return lo, min(N, lo + CHUNKS[c] * P) - lo

            with sp.Fori(0, NSG) as sg:
                for c in range(NCH):
                    lo, w = cols(c)
                    hold(sp, "sp", cast_done, sg * NCH + (c + 1))
                    sp.dma_start(FST[:, c % RING, :, 0:w],
                                 adj[bass.ds(sg * (SG * P), SG * P), lo:lo + w]
                                 .rearrange("(b p) c -> p b c", p=P)).then_inc(adj_loaded[c % RING], 16)
            for c in range(NCH):
                lo, w = cols(c)
                r0 = NSG * SG * P
                sp.wait_ge(cast_done, NSG * NCH + c + 1)
                sp.dma_start(FST[:, c % RING, 0:TAIL - 1, 0:w],
                             adj[r0:r0 + (TAIL - 1) * P, lo:lo + w]
                             .rearrange("(b p) c -> p b c", p=P)).then_inc(adj_loaded[c % RING], 16)
                r0 += (TAIL - 1) * P
                sp.dma_start(FST[0:112, c % RING, TAIL - 1, 0:w], adj[r0:r0 + 112, lo:lo + w]).then_inc(adj_loaded[c % RING], 16)
                sp.dma_start(FST[112:LAST, c % RING, TAIL - 1, 0:w], adj[r0 + 112:N, lo:lo + w]).then_inc(adj_loaded[c % RING], 16)

            def load_pairs(source, used, base, per_tile=1):
                def load(n, i, k):
                    hold(sp, "sp", used, n * (RS * per_tile) + (base + (2 * k + 2) * per_tile))
                    sp.dma_start(HST[:, 2 * k:2 * k + 2, :], source(i)).then_inc(tiles_loaded[k], 16)

                with sp.Fori(0, ROUNDS) as n:
                    for k in range(2):
                        load(n, n * RS + 2 * k, k)
                load(ROUNDS, ROUNDS * RS, 0)

            def load_halves(hf, base):
                def load(i, k):
                    sp.dma_start(HSTH[:, 2 * k:2 * k + 2, :],
                                 hp_dram[bass.ds(i, 2), :, hf * HALF:(hf + 1) * HALF]
                                 .rearrange("b p c -> p b c")).then_inc(tiles_loaded[k], 16)

                place = [(k + hf) % 4 for k in range(4)]
                for k in range(4):
                    if hf:
                        sp.wait_ge(g_used, base - B + HRS * (HROUNDS - 1) + 2 * k + 4)
                    load(2 * k, place[k])
                with sp.Fori(0, HROUNDS - 1) as n:
                    for k in range(4):
                        hold(sp, "sp", g_used, n * HRS + (base + 2 * k + 2))
                        load(n * HRS + (HRS + 2 * k), place[k])
                hold(sp, "sp", g_used, base + HRS * (HROUNDS - 1) + 2)
                load(B - 2, place[0])

            def resident(i):
                return H[:, bass.ds(i, 2), :]

            def pruned(i):
                return hp_dram[bass.ds(i, 2), :, :].rearrange("b p c -> p b c")

            for L in range(LAYERS):
                if L == 0:
                    sp.wait_ge(kept, NCH + (NSG + 1) * NCH)
                    sp.wait_ge(acc_done, 2 + B * (NSG + 1))
                else:
                    sp.wait_ge(m_psum, (RS + B * L) * PAIRS)
                def att_load(i, k):
                    sp.dma_start(AHST[:, 2 * k:2 * k + 2, :], resident(i)).then_inc(tiles_loaded[k], 16)

                for k in range(3):
                    att_load(2 * k, k)
                with sp.Fori(0, AROUNDS - 1) as n:
                    for k in range(3):
                        hold(sp, "sp", max_ready, n * ARS + (RS + B * L + 2 * k + 2))
                        att_load(n * ARS + (ARS + 2 * k), k)
                sp.wait_ge(max_ready, RS + B * L + (AROUNDS - 1) * ARS + 2)
                att_load(B - 2, 0)
                def cos_load(n, i, k):
                    hold(sp, "sp", g_ready, n * RS + (B * L + 2 * k + 2))
                    sp.dma_start(HST[:, 2 * k:2 * k + 2, :], resident(i)).then_inc(tiles_loaded[k], 16)

                def store_pruned(n, i, v):
                    for u in range(2):
                        hold(sp, "sp", hp_ready, n * RS + (B * L + v + u + 3))
                        sp.dma_start(hp_dram[bass.ds(i + u, 1), :, :].rearrange("o p c -> p (o c)"),
                                     HPST[:, u, :]).then_inc(hp_stored[u], 16)

                sp.wait_ge(max_ready, RS + B * (L + 1))
                cos_load(0, 0, 0)
                cos_load(0, 2, 1)
                sp.wait_ge(rows_ready, L + 1)
                sp.dma_start(att_rows, ROWS[0:97:32, :, :]).then_inc(rows_stored, 16)
                sp.wait_ge(rows_stored, 16 * (L + 1))
                sp.dma_start(ATR[:, :], att_back).then_inc(rows_back, 16)
                with sp.Fori(0, ROUNDS - 1) as n:
                    for k in range(2):
                        cos_load(n + 1, n * RS + (RS + 2 * k), k)
                        store_pruned(n, n * RS + 2 * k, 2 * k)
                cos_load(ROUNDS, B - 2, 0)
                for k in range(3):
                    store_pruned(ROUNDS - 1, B - 6 + 2 * k, 2 * k)
                sp.wait_ge(g_ready, RS + B * (L + 1))
                for u in range(2):
                    sp.wait_ge(hp_stored[u], 16 + 16 * HB * (L + 1))
                for hf in range(2):
                    load_halves(hf, RS + B * (2 * L + hf))
                sp.wait_ge(g_used, RS + 2 * B * (L + 1))
                load_pairs(pruned, m_psum, B * L * PAIRS, per_tile=PAIRS)
            sp.wait_ge(feat_ready, 4 + LAYERS)
            sp.dma_start(out[0:(B - 1) * P, :].rearrange("(b p) d -> p b d", p=P), X[:, 0:B - 1, :]).then_inc(out_stored, 16)
            sp.dma_start(out[(B - 1) * P:N, :], X[0:LAST, B - 1, :]).then_inc(out_stored, 16)
            sp.wait_ge(out_stored, 32)

        @block.gpsimd
        def _(pool):
            step = [0]

            def link(ins):
                step[0] += 1
                ins.then_inc(constants_ready, 1)
                pool.wait_ge(constants_ready, step[0])

            pool.sem_inc(cast_done, RING)
            pool.sem_inc(kept, NCH)
            pool.sem_inc(g_ready, RS)
            nc.gpsimd.memset(X[:, B - 1, :], 0.0).then_inc(pads_zeroed, 1)
            nc.gpsimd.memset(S0[:, :], 0.0).then_inc(pads_zeroed, 1)
            link(nc.gpsimd.memset(HS[:, :, N:NP], 0))
            link(nc.gpsimd.memset(PROW[:, :, 2 * D:2 * D + 2], 1.0))
            link(nc.gpsimd.memset(wwv[D:D + 1, 0:D], 0.0))
            link(nc.gpsimd.memset(XTb[:, NP - PADCOLS:NP], 0.0))
            link(nc.gpsimd.memset(ones[:, :], 1.0))
            link(nc.gpsimd.memset(zeros[:, :], 0.0))
            link(nc.gpsimd.memset(eps[:, 0:1], LN_EPS))
            link(nc.gpsimd.memset(eps[:, 1:2], 0.0))
            link(nc.gpsimd.memset(eps[:, 2:3], W_BIAS))
            link(nc.gpsimd.memset(valid[:, :], 1.0))
            link(nc.gpsimd.affine_select(out=valid[:, :], in_=valid[:, :], compare_op=ALU.is_gt, fill=0.0, base=N,
                                         pattern=[[-P, B]], channel_multiplier=-1))
            link(nc.gpsimd.tensor_scalar(cast_by[:, :], valid[:, B - 1:B], H_BYTE, 0.0, ALU.mult, ALU.add))
            link(nc.gpsimd.tensor_scalar(far[:, :], valid[:, :], FAR, -FAR, ALU.mult, ALU.add))
            for m, rest, diag in ((identF, 0.0, 1.0), (ident, 0.0, 1.0), (half_ident, 0.0, 1.0 / H_FP8),
                                  (mask_ident, 0.0, MASK_OFF)):
                link(nc.gpsimd.memset(m[:, :], rest))
                link(nc.gpsimd.affine_select(out=m[:, :], in_=m[:, :], compare_op=ALU.not_equal, fill=diag, base=0,
                                             pattern=[[-1, P]], channel_multiplier=1))
            link(nc.gpsimd.memset(fold[:, :], 0.0))
            for off in (-D, 0, D):
                link(nc.gpsimd.affine_select(out=fold[:, :], in_=fold[:, :], compare_op=ALU.not_equal, fill=1.0, base=off,
                                             pattern=[[-1, P]], channel_multiplier=1))
            for m, sign, diag in ((count_first, 1, OWN), (count_next, -1, -OWN - STEP)):
                link(nc.gpsimd.memset(m[:, :], -STEP))
                link(nc.gpsimd.affine_select(out=m[:, :], in_=m[:, :], compare_op=ALU.is_gt, fill=0.0, base=0,
                                             pattern=[[-sign, P]], channel_multiplier=sign))
                link(nc.gpsimd.affine_select(out=m[:, :], in_=m[:, :], compare_op=ALU.not_equal, fill=diag, base=0,
                                             pattern=[[-1, P]], channel_multiplier=1))
            assert step[0] == CONSTANTS

            def across(k, src, dst, op):
                pool.wait_ge(node_to_pool, k)
                nc.gpsimd.partition_all_reduce(dst, src, P, op).then_inc(node_from_pool, 1)

            sums = [0]

            def reduce_at(src, dst, op):
                sums[0] += 1
                across(sums[0], src, dst, op)

            reduce_at(S0[:, 0:1], S0[:, 0:1], RMAX)

            def cast(sg, c, nb):
                n = sg * NCH + (c + 1)
                lo = (B - CHUNK_AT[c] - CHUNKS[c]) * P
                w = min(N, lo + CHUNKS[c] * P) - lo
                if nb == SG:
                    pool.wait_ge(adj_loaded[c % RING], sg * (16 * ROUND) + 16 * (c // RING + 1))
                else:
                    pool.wait_ge(adj_loaded[c % RING], NSG * 16 * ROUND + 48 * (c // RING + 1))
                pool.wait_ge(kept, n)
                hold(pool, "pool", cols_used, n)
                if nb == SG:
                    nc.gpsimd.tensor_scalar(HS[:, :, lo:lo + w], FST[:, c % RING, :, 0:w], H_BYTE, 1.0,
                                            ALU.mult, ALU.mult).then_inc(cast_done, 1)
                else:
                    nc.gpsimd.tensor_scalar(HS[:, 0:nb - 1, lo:lo + w], FST[:, c % RING, 0:nb - 1, 0:w], H_BYTE, 1.0,
                                            ALU.mult, ALU.mult)
                    nc.gpsimd.tensor_scalar(HS[:, nb - 1, lo:lo + w], FST[:, c % RING, nb - 1, 0:w], cast_by[:, 0:1], 1.0,
                                            ALU.mult, ALU.mult).then_inc(cast_done, 1)

            with pool.Fori(0, NSG) as sg:
                for c in range(NCH):
                    cast(sg, c, SG)
            for c in range(NCH):
                cast(NSG, c, TAIL)

            def rows(used, ready, base, in_between=None, shift=0):
                def one(n, i, v):
                    hold(pool, "pool", used, n * RS + (base + v + 1))
                    nc.gpsimd.tensor_copy(PROW[:, (v + shift) % RS, 0:2 * D].bitcast(I32),
                                          HALVES[:, i, :].bitcast(I32)).then_inc(ready, 1)
                if base and not shift:
                    pool.wait_ge(used, RS + base)
                if in_between is None:
                    all_tiles(pool, one)
                    return
                with pool.Fori(0, ROUNDS - 2) as n:
                    for v in range(RS):
                        one(n, n * RS + v, v)
                in_between()
                for i in range((ROUNDS - 2) * RS, B):
                    one(i // RS, i, i % RS)

            for L in range(LAYERS):
                pool.wait_ge(feat_ready, 4 + L)
                if L == 0:
                    pool.wait_ge(l0_sum, NSG + 1)
                nc.gpsimd.memset(XTb[D:D + 1, :], 1.0).then_inc(ones_row, 1)
                reduce_at(SV[:, 0:1], SV[:, 0:1], RMAX)
                pool.wait_ge(parts_ready, 3 * L + 1)
                def in_between():
                    reduce_at(SQ[:, 0:1], SQ[:, 0:1], RMAX)
                    reduce_at(ST[:, 0:1], ST[:, 0:1], RMAX)

                rows(e_used, e_row_ready, B * L, in_between)

                def other(n, i, v):
                    pool.wait_ge(tiles_loaded[v // 2], loaded_at(L, 1, n, v // 2))
                    hold(pool, "pool", cos_psum, n * (2 * RS) + (2 * (B * L + v) + 2))
                    nc.gpsimd.tensor_scalar(GST[:, v, :], HST[:, v, :], -1.0, H_BYTE,
                                            ALU.mult, ALU.add).then_inc(g_ready, 1)

                pool.wait_ge(col_done, 6 + 2 * B * (L + 1))
                for v in range(2):
                    other(0, v, v)
                reduce_at(G1[:, 0:1], G1[:, 1:2], RMAX)
                reduce_at(G1[:, 2:3], G1[:, 3:4], RADD)
                with pool.Fori(0, ROUNDS) as n:
                    for v in range(RS):
                        other(n + (v + 2) // RS, n * RS + (v + 2), (v + 2) % RS)
                reduce_at(G1[:, 4:5], G1[:, 5:6], RMAX)
                reduce_at(G1[:, 6:7], G1[:, 7:8], RADD)
                pool.wait_ge(parts_ready, 3 * L + 2)
                for hf in range(2):
                    rows(g_used, g_row_ready, B * (2 * L + hf), shift=2 * hf)

        @block.scalar
        def _(act):
            act.sem_inc(deg_rows, 1)
            act.sem_inc(exp_done, 2)
            act.sem_inc(m_act, 2)
            act.dma_start(w0[:, :], l0_weight).then_inc(w0_loaded, 16)
            for dst, src in ((b0[:, :], l0_bias.rearrange("(o d) -> o d", o=1).to_broadcast([P, D])),
                             (wwv[0:D, 0:D], W), (wwv[0:D, D:2 * D], Wv), (wqq[0:D, 0:D], Wq), (wqq[0:D, D:2 * D], Wq),
                             (wth[:, :], Theta),
                             (wwv[D:D + 1, D:2 * D], bv.rearrange("(o d) -> o d", o=1)),
                             (wqq[D:D + 1, 0:D], bq.rearrange("(o d) -> o d", o=1)),
                             (wqq[D:D + 1, D:2 * D], bq.rearrange("(o d) -> o d", o=1))):
                act.dma_start(dst, src).then_inc(weights_loaded, 16)
            small, squares, xts = [0], [0], [0]

            def squared_features(squares_at, centred_at):
                for lo, hi in SPLIT:
                    squares[0] += 1
                    act.wait_ge(centred, squares[0])
                    nc.scalar.activation(squares_at[:, lo:hi, :], centred_at[:, lo:hi, :], ACT.Square).then_inc(squared, 1)

            def features_out():
                for g in range(GROUPS):
                    xts[0] += 1
                    if g % 2:
                        w = len(group(g)) * P
                        act.wait_ge(xt_psum, xts[0])
                        nc.scalar.activation(XT[:, 4 * P * g:4 * P * g + w], PS[0:D, g, 0:w],
                                             ACT.Copy).then_inc(xt_ready_act, 1)

            def asked(o, i, func, **kw):
                small[0] += 1
                act.wait_ge(node_to_act, small[0])
                nc.scalar.activation(o, i, func, **kw).then_inc(node_from_act, 1)

            squared_features(TMP2, TMP1)
            act.wait_ge(constants_ready, CONSTANTS)
            asked(STD[:, :], VAR[:, :], ACT.Sqrt, scale=1.0 / D, bias=eps[:, 0:1])
            features_out()
            act.wait_ge(scale_ready, 1)
            for g in range(GROUPS):
                lo, hi = 4 * g, 4 * g + len(group(g))
                act.wait_ge(prod_psum, g + 1)
                nc.scalar.activation(HALVES[:, lo:hi, 0:D], PS[:, g, 0:(hi - lo) * D].rearrange("p (b d) -> p b d", d=D),
                                     ACT.Copy, scale=S0[:, 2:3]).then_inc(l0_high, 1)

            def exponents(sg, nb):
                for s in range(B):
                    for h in range(2):
                        w = halves(nb)[h][1] * P
                        act.wait_ge(acc_done, sg * B + (s + 1))
                        hold(act, "act", count_ready, sg * (2 * B) + (2 * s + h + 3))
                        nc.scalar.activation(WTR[:, h, s % 2, 0:w], PS[:, 2 + h, 0:w], ACT.Relu,
                                             bias=eps[:, 2:3]).then_inc(w_ready, 1)
                hold(act, "act", count_ready, sg * (2 * B) + (2 * B + 2))
                for h in range(2):
                    w = halves(nb)[h][1] * P
                    hold(act, "act", deg_psum, sg + 1)
                    last = nc.scalar.activation(DEG_ROWS[32 * h:32 * h + 1, bass.ds(sg * (halves(SG)[h][1] * P), w)], PS[32 * h:32 * h + 1, 2 + h, 0:w], ACT.Copy)
                last.then_inc(deg_rows, 1)

            with act.Fori(0, NSG) as sg:
                exponents(sg, SG)
            exponents(NSG, TAIL)

            for L in range(LAYERS):
                if L == 0:
                    squared_features(SQUARES, XN)
                    asked(STD[:, :], VAR[:, :], ACT.Sqrt, scale=1.0 / D, bias=eps[:, 0:1])
                features_out()
                for g in range(GROUPS):
                    b = group(g)
                    act.wait_ge(prod_psum, GROUPS * (2 * L + 1) + g + 1)
                    nc.scalar.activation(XW[:, b[0]:b[-1] + 1, :],
                                         PS[:, g, 0:len(b) * 2 * D].rearrange("p (b c) -> p b c", c=2 * D)[:, :, 0:D],
                                         ACT.Copy).then_inc(xw_evac, 1)
                act.wait_ge(scale_ready, 3 * L + 2)
                for g in range(GROUPS):
                    b = group(g)
                    nc.scalar.activation(HALVES[:, b[0]:b[-1] + 1, 0:D],
                                         PS[:, g, 0:len(b) * 2 * D].rearrange("p (b c) -> p b c", c=2 * D)[:, :, D:2 * D],
                                         ACT.Copy, scale=SV[:, 2:3]).then_inc(v_high, 1)
                asked(STR[:, :], T_A[:, :], ACT.Sqrt)
                asked(FMAG[:, :], T_A[:, :], ACT.Sqrt)
                act.wait_ge(scale_ready, 3 * L + 3)
                nc.scalar.activation(QA, ATT1[:, :], ACT.Copy, scale=SQ[:, 2:3]).then_inc(q_high, 1)
                act.wait_ge(e_used, RS + B * (L + 1))
                for g in range(1, GROUPS, 2):
                    w = len(group(g)) * P
                    nc.scalar.activation(ATT0[:, 4 * P * g:4 * P * g + w], PS[:, g, 0:w],
                                         ACT.Copy).then_inc(et_evac_act, 1)
                for g in range(GROUPS):
                    w = len(group(g)) * P
                    act.wait_ge(fold_psum, GROUPS * L + g + 1)
                    nc.scalar.activation(E11[:, 4 * P * g:4 * P * g + w], PS[:, g, 0:w], ACT.Copy,
                                         scale=E_SCALE).then_inc(e_high, 1)
                nc.scalar.activation(WARM[:, :], eps[:, 1:2], ACT.Exp)

                def att_exp(n, i, v):
                    u, w = v % 2, v % 3
                    hold(act, "act", max_ready, i + (B * L + 1 + RS))
                    nc.scalar.activation(SCORES[w][:, 0:N], SCORES[w][:, 0:N], ACT.Exp, bias=NEGM[:, u:u + 1],
                                         accum_out=ZROW[:, u:u + 1]).then_inc(z_ready, 1)

                all_tiles(act, att_exp, ARS)
                asked(EXPN[:, :], IMP[:, :], ACT.Exp, bias=G1[:, 1:2], accum_out=G1[:, 2:3])
                for g in range(GROUPS):
                    lo, hi = 4 * g, 4 * g + len(group(g))
                    act.wait_ge(dup_first, GROUPS * L + g + 1)
                    nc.scalar.activation(DUP[:, lo:hi, D:2 * D], DUP[:, lo:hi, 0:D], ACT.Copy).then_inc(dup_ready, 1)
                for g in range(GROUPS):
                    w = len(group(g)) * P
                    act.wait_ge(dup_psum, GROUPS * L + g + 1)
                    nc.scalar.activation(C11[:, 4 * P * g:4 * P * g + w], PS[:, g, 0:w], ACT.Copy, scale=COS_SCALE)
                    nc.scalar.activation(CA[0:D, 4 * P * g:4 * P * g + w], PS[0:D, g, 0:w], ACT.Copy,
                                         scale=COS_SCALE).then_inc(c_high, 1)
                act.wait_ge(off_ready, L + 1)

                def cos_exp(n, i, v):
                    u = v % 2
                    act.wait_ge(hp_ready, n * RS + (B * L + v + 1))
                    for q in range(2):
                        hold(act, "act", cos_psum, n * (2 * RS) + (2 * (B * L + v) + q + 1 + 2 * RS))
                        nc.scalar.activation(ATT[u][:, q * HALF:(q + 1) * HALF].rearrange("p (k c) -> p k c", k=4),
                                             PS[:, 4 * q:4 * q + 4, 0:CW], ACT.Exp, scale=1.0 / COS_UNIT,
                                             accum_out=ZC[:, u, q:q + 1]).then_inc(exp_done, 1)
                    hold(act, "act", exp_done, n * (2 * RS) + (2 * (B * L + v) + 4))
                    nc.scalar.activation(ZS[:, u, :], ZC[:, u, :], ACT.Identity, scale=TH[L], bias=OFF[:, bass.ds(i, 1)],
                                         accum_out=THR[:, u:u + 1]).then_inc(thr_done, 1)

                all_tiles(act, cos_exp)
                asked(EXPN[:, :], IMP[:, :], ACT.Exp, bias=G1[:, 5:6], accum_out=G1[:, 6:7])
                asked(DV[:, :], T_A[:, :], ACT.Sqrt)
                for k, (lo, hi) in enumerate(SPLIT_HALF):
                    act.wait_ge(t_ready, 4 * L + k + 1)
                    nc.scalar.activation(HALVES[:, lo:hi, 0:D], TMP1[:, lo:hi, :], ACT.Copy,
                                         scale=ST[:, 2:3]).then_inc(high_ready, 1)
                for k, (lo, hi) in enumerate(SPLIT_HALF):
                    act.wait_ge(t_ready, 4 * L + k + 3)
                    nc.scalar.activation(AHALVES[:, lo:hi, 0:D], TMP1[:, lo:hi, :], ACT.Copy).then_inc(high_ready, 1)

                def tile_out(n, i, v):
                    u = v % 2
                    act.wait_ge(msg_done, n * RS + (B * L + v + 1))
                    for g in (1, 3):
                        w = min(8 * P, NP - 8 * P * g)
                        hold(act, "act", m_psum, n * (RS * PAIRS) + ((B * L + v + RS) * PAIRS + g + 1))
                        nc.scalar.activation(HPT[u][:, 8 * P * g:8 * P * g + w],
                                             PS[:, TILES_AT[g]:min(TILES_AT[g] + 2, 8), :].rearrange("p k c -> p (k c)")[:, 0:w],
                                             ACT.Copy).then_inc(m_act, 1)

                all_tiles(act, tile_out)
                features_out()

        @block.vector
        def _(dve):
            chain = [0]

            def link(ins):
                chain[0] += 1
                ins.then_inc(vec_step, 1)
                dve.wait_ge(vec_step, chain[0])

            asks, sums, squares, xts, prods = [0], [0], [0], [0], [0]

            def ask(ins):
                asks[0] += 1
                ins.then_inc(node_to_act, 1)
                dve.wait_ge(node_from_act, asks[0])

            def across(ins):
                sums[0] += 1
                ins.then_inc(node_to_pool, 1)
                dve.wait_ge(node_from_pool, sums[0])

            def per_node(v):
                return v[:, :].unsqueeze(2).to_broadcast([P, B, D])

            def layernorm_relu(squares_at, centred_at):
                link(nc.vector.tensor_reduce(MEAN[:, :], X[:, :, :], AX, ALU.add))
                link(nc.vector.tensor_scalar(MEAN[:, :], MEAN[:, :], 1.0 / D, None, ALU.mult))
                for lo, hi in SPLIT:
                    nc.vector.tensor_tensor(centred_at[:, lo:hi, :], X[:, lo:hi, :], per_node(MEAN)[:, lo:hi, :],
                                            ALU.subtract).then_inc(centred, 1)
                for k, (lo, hi) in enumerate(SPLIT):
                    squares[0] += 1
                    dve.wait_ge(squared, squares[0])
                    last = nc.vector.tensor_reduce(VAR[:, lo:hi], squares_at[:, lo:hi, :], AX, ALU.add)
                    if k == 0:
                        link(last)
                ask(last)
                link(nc.vector.reciprocal(STD[:, :], STD[:, :]))
                for lo, hi in SPLIT:
                    nc.vector.scalar_tensor_tensor(FEAT[:, lo:hi, :], centred_at[:, lo:hi, :], 0.0,
                                                   per_node(STD)[:, lo:hi, :], ALU.max, ALU.mult).then_inc(feat_ready, 1)

            def features_out():
                for g in range(GROUPS):
                    w = len(group(g)) * P
                    xts[0] += 1
                    if g % 2 == 0:
                        dve.wait_ge(xt_psum, xts[0])
                        nc.vector.tensor_copy(XT[:, 4 * P * g:4 * P * g + w], PS[0:D, g, 0:w]).then_inc(xt_ready, 1)

            def products():
                for g in range(GROUPS):
                    prods[0] += 1
                    dve.wait_ge(prod_psum, prods[0])
                    yield g, 4 * g, 4 * g + len(group(g))

            def scaled(s, last):
                across(last)
                powers(s)

            def powers(s, scales=[0]):
                link(nc.vector.tensor_scalar(s[:, 0:1], s[:, 0:1], TINY, None, ALU.max))
                link(nc.vector.tensor_scalar(s[:, 1:2].bitcast(I32), s[:, 0:1].bitcast(I32), EXPONENT, None,
                                             ALU.bitwise_and))
                link(nc.vector.reciprocal(s[:, 2:3], s[:, 1:2]))
                link(nc.vector.tensor_scalar(s[:, 3:4], s[:, 1:2], 1.0 / TOP, None, ALU.mult))
                nc.vector.tensor_scalar(s[:, 2:3], s[:, 2:3], TOP, None, ALU.mult).then_inc(scale_ready, 1)
                scales[0] += 1
                dve.wait_ge(scale_ready, scales[0])

            dve.sem_inc(cos_psum, 2 * RS)
            dve.sem_inc(ht_ready, 4)
            dve.sem_inc(acc_free, 1)
            dve.sem_inc(s_masked, PAIRS)
            dve.sem_inc(max_ready, RS)
            dve.sem_inc(hp_ready, 2)
            dve.sem_inc(conn_done, 1)
            dve.sem_inc(hp_stored[0], 16)
            dve.sem_inc(hp_stored[1], 16)
            dve.sem_inc(m_vec, 2)
            dve.sem_inc(msg_taken, 1)

            dve.wait_ge(pads_zeroed, 2)
            dve.wait_ge(w0_loaded, 16)
            sums[0] += 1
            nc.vector.tensor_reduce(S0[0:D, 0:1], w0[:, :], AX, ALU.max, apply_absolute_value=True).then_inc(node_to_pool, 1)
            dve.wait_ge(x_loaded, 32)
            layernorm_relu(TMP2, TMP1)
            dve.wait_ge(constants_ready, CONSTANTS)
            dve.wait_ge(node_from_pool, 1)
            link(nc.vector.tensor_scalar(S0[:, 0:1], S0[:, 0:1], float(D), None, ALU.mult))
            powers(S0)
            link(nc.vector.tensor_scalar(UNDO[:, 0:1], S0[:, 3:4], SUP_SCALE, None, ALU.mult))
            features_out()
            prods[0] += GROUPS
            for g in range(GROUPS):
                lo, hi = 4 * g, 4 * g + len(group(g))
                dve.wait_ge(l0_high, g + 1)
                nc.vector.scalar_tensor_tensor(HALVES[:, lo:hi, D:2 * D],
                                               PS[:, g, 0:(hi - lo) * D].rearrange("p (b d) -> p b d", d=D), S0[:, 2:3],
                                               HALVES[:, lo:hi, 0:D], ALU.mult, ALU.subtract).then_inc(support_ready, 1)
            dve.wait_ge(support_ready, GROUPS)

            def copies(sg, s, nb):
                for h in range(2):
                    w = halves(nb)[h][1] * P
                    dve.wait_ge(count_ready, sg * (2 * B) + (2 * s + h + (1 if s < 2 else -3)))
                    hold(dve, "dve", ht_psum, sg * (2 * B) + (2 * s + h + 1))
                    nc.vector.tensor_copy(HTR[:, h, s % 4, 0:w], PS[:, HT_AT[h][s % 2], 0:w]).then_inc(ht_ready, 1)

            def steps(sg, nb):
                for s in range(3, B):
                    copies(sg, s, nb)
                    for c in range(NCH):
                        if s != max(CHUNK_AT[c], 3):
                            continue
                        lo = (B - CHUNK_AT[c] - CHUNKS[c]) * P
                        hi = lo + CHUNKS[c] * P
                        hold(dve, "dve", cast_done, sg * NCH + (c + 1 + RING))
                        nc.vector.tensor_copy(H[:, bass.ds(sg * SG, nb), lo:hi].bitcast(I32),
                                              HS[:, 0:nb, lo:hi].bitcast(I32)).then_inc(kept, 1)

            def sums_out(sg, nb):
                hold(dve, "dve", acc_done, sg * B + (B + 2))
                for k in range((nb + 3) // 4):
                    m = min(4, nb - 4 * k)
                    last = nc.vector.tensor_reduce(
                        SUM0[:, 4 * k:4 * k + m, :],
                        PS[:, 4 + k, 0:m * 2 * D].rearrange("p (b t d) -> p b d t", b=m, t=2), AX, ALU.add)
                last.then_inc(acc_free, 1)

            def add_to_x(sg, nb):
                hold(dve, "dve", acc_free, sg + 2)
                nc.vector.scalar_tensor_tensor(SUM1[:, 0:nb, :], SUM0[:, 0:nb, :], UNDO[:, 0:1],
                                               b0[:, :].unsqueeze(1).to_broadcast([P, nb, D]),
                                               ALU.mult, ALU.add).then_inc(l0_biased, 1)
                hold(dve, "dve", l0_biased, sg + 1)
                rows = X[:, bass.ds(sg * SG, nb), :]
                nc.vector.tensor_tensor(rows, rows, SUM1[:, 0:nb, :], ALU.add).then_inc(l0_sum, 1)

            dve.wait_ge(weights_loaded, 144)
            for s in range(3):
                copies(0, s, SG)
            with dve.Fori(0, NSG) as sg:
                steps(sg, SG)
                for s in range(2):
                    copies(sg + 1, s, SG)
                sums_out(sg, SG)
                copies(sg + 1, 2, SG)
                add_to_x(sg, SG)
            steps(NSG, TAIL)
            sums_out(NSG, TAIL)
            add_to_x(NSG, TAIL)
            dve.wait_ge(l0_sum, NSG + 1)

            for L in range(LAYERS):
                if L == 0:
                    def degrees():
                        dve.wait_ge(deg_psum, NSG + 3)
                        for h, (b, nb) in enumerate(halves(SG)):
                            link(nc.vector.tensor_scalar(
                                DEG[:, 0:NSG * SG].rearrange("p (s b) -> p s b", s=NSG)[:, :, b:b + nb],
                                PS[:, 7 - h, 0:NSG * nb].rearrange("p (s b) -> p s b", s=NSG), -1.0 / STEP, None,
                                ALU.mult))
                            first, rest = halves(TAIL)[h]
                            nc.vector.tensor_scalar(DEG[:, NSG * SG + first:NSG * SG + first + rest],
                                                    PS[:, 7 - h, NSG * nb:NSG * nb + rest], -1.0 / STEP, None,
                                                    ALU.mult).then_inc(deg_taken, 1)

                    layernorm_relu(SQUARES, XN)
                    degrees()
                features_out()
                for g, lo, hi in products():
                    dve.wait_ge(xw_evac, GROUPS * L + g + 1)
                    link(nc.vector.tensor_reduce(LARGEST[:, g:g + 1],
                                                 PS[:, g, 0:(hi - lo) * 2 * D].rearrange("p (b c) -> p b c", c=2 * D)[:, :, D:2 * D],
                                                 mybir.AxisListType.XY, ALU.max, apply_absolute_value=True))
                scaled(SV, nc.vector.tensor_reduce(SV[:, 0:1], LARGEST[:, 0:GROUPS], AX, ALU.max))
                for g in range(GROUPS):
                    b = group(g)
                    dve.wait_ge(v_high, GROUPS * L + g + 1)
                    last = nc.vector.scalar_tensor_tensor(
                        HALVES[:, b[0]:b[-1] + 1, D:2 * D],
                        PS[:, g, 0:len(b) * 2 * D].rearrange("p (b c) -> p b c", c=2 * D)[:, :, D:2 * D],
                        SV[:, 2:3], HALVES[:, b[0]:b[-1] + 1, 0:D], ALU.mult, ALU.subtract)
                last.then_inc(parts_ready, 1)
                link(nc.vector.tensor_tensor(SQUARES, XW, XW, ALU.mult))
                link(nc.vector.tensor_reduce(T_A[:, :], SQUARES, AX, ALU.add))
                ask(nc.vector.tensor_scalar(T_A[:, :], T_A[:, :], NORM_MIN, None, ALU.max))
                link(nc.vector.tensor_tensor(SQUARES, FEAT[:, :, :], FEAT[:, :, :], ALU.mult))
                link(nc.vector.tensor_reduce(T_A[:, :], SQUARES, AX, ALU.add))
                ask(nc.vector.tensor_scalar(T_A[:, :], T_A[:, :], NORM_MIN, None, ALU.max))
                link(nc.vector.tensor_scalar(T_B[:, :], FMAG[:, :], 1e-8, None, ALU.max))
                link(nc.vector.reciprocal(T_B[:, :], T_B[:, :]))
                link(nc.vector.tensor_reduce(ST[:, 1:2], XW, mybir.AxisListType.XY, ALU.max, apply_absolute_value=True))
                for g in range(GROUPS):
                    w = len(group(g)) * P
                    dve.wait_ge(q_psum, GROUPS * L + g + 1)
                    link(nc.vector.tensor_reduce(LARGEST[:, g:g + 1], PS[:, 7, 0:w], AX, ALU.max,
                                                 apply_absolute_value=True))
                    nc.vector.tensor_copy(ATT1[:, 4 * P * g:4 * P * g + w], PS[:, 7, 0:w]).then_inc(q_evac, 1)
                dve.wait_ge(q_evac, GROUPS * (L + 1))
                scaled(SQ, nc.vector.tensor_reduce(SQ[:, 0:1], LARGEST[:, 0:GROUPS], AX, ALU.max))
                scaled(ST, nc.vector.tensor_copy(ST[:, 0:1], ST[:, 1:2]))
                dve.wait_ge(q_high, L + 1)
                link(nc.vector.scalar_tensor_tensor(QA[D:2 * D, :], ATT1[D:2 * D, :], SQ[D:2 * D, 2:3], QA[D:2 * D, :],
                                                    ALU.mult, ALU.subtract))
                link(nc.vector.tensor_tensor(UNDO[:, 0:1], SV[:, 3:4], SQ[:, 3:4], ALU.mult))
                link(nc.vector.tensor_scalar(UNDO[:, 0:1], UNDO[:, 0:1], D ** -0.5 / H_FP8 / H_BYTE / E_SCALE, None,
                                             ALU.mult))

                dve.wait_ge(e_used, RS + B * (L + 1))
                for g in range(0, GROUPS, 2):
                    w = len(group(g)) * P
                    nc.vector.tensor_copy(ATT0[:, 4 * P * g:4 * P * g + w], PS[:, g, 0:w]).then_inc(et_evac, 1)
                for g in range(GROUPS):
                    w = len(group(g)) * P
                    c = slice(4 * P * g, 4 * P * g + w)
                    dve.wait_ge(e_high, GROUPS * L + g + 1)
                    last = nc.vector.scalar_tensor_tensor(E22[:, c], PS[:, g, 0:w], E_SCALE, E11[:, c],
                                                          ALU.mult, ALU.subtract)
                last.then_inc(stacks_ready, 1)
                dve.wait_ge(stacks_ready, 2 * L + 1)

                def weight(i, u):
                    t = i + B * L
                    if isinstance(i, int) and i == B - 1:
                        dve.wait_ge(z_ready, t + 1)
                        link(nc.vector.reciprocal(RZT[:, :], ZROW[:, u:u + 1]))
                        nc.vector.tensor_scalar(RZ[:, u:u + 1], RZT[:, :], valid[:, B - 1:B], None,
                                                ALU.mult).then_inc(rz_ready, 1)
                    else:
                        hold(dve, "dve", z_ready, t + 1)
                        nc.vector.reciprocal(RZ[:, u:u + 1], ZROW[:, u:u + 1]).then_inc(rz_ready, 1)

                def maximum(i, u):
                    hold(dve, "dve", s_masked, (i + B * L) * PAIRS + 2 * PAIRS)
                    nc.vector.tensor_reduce(NEGM[:, u:u + 1], MX[:, u, :], AX, ALU.max, negate=True).then_inc(max_ready, 1)

                def masked(n, i, v, behind=2):
                    u = v % 2
                    t = i + B * L
                    dve.wait_ge(tiles_loaded[v // 2], loaded_at(L, 0, n, v // 2))
                    for q in range(PAIRS):
                        if q % 2 == 0:
                            dve.wait_ge(col_done, t * 2 + (q // 2 + 1))
                        hold(dve, "dve", s_psum, t * PAIRS + (q + 1))
                        for k, w in ((slice(0, 2), CW),) if q < PAIRS - 1 else ((slice(0, 1), CW), (slice(1, 2), CW - 1)):
                            nk = k.stop - k.start
                            c = q * PW + k.start * CW
                            m = q + k.start
                            last = nc.vector.tensor_tensor_reduce(
                                out=SCORES[v % 3][:, c:c + nk * w].rearrange("p (k c) -> p k c", k=nk),
                                in0=PS[:, SCORES_AT[q] + k.start:SCORES_AT[q] + k.stop, 0:w],
                                in1=AHST[:, v, c:c + nk * w].rearrange("p (k c) -> p k c", k=nk),
                                scale=UNDO[:, 0:1], scalar=-3e38, op0=ALU.mult, op1=ALU.max,
                                accum_out=MX[:, u, m:m + 1])
                        last.then_inc(s_masked, 1)
                        if q == 0 and behind:
                            maximum(i - 1, 1 - u)
                        if q == 0 and behind > 1:
                            weight(i - 2, u)

                masked(0, 0, 0, behind=0)
                masked(0, 1, 1, behind=1)
                with dve.Fori(0, AROUNDS) as n:
                    for v in range(2, ARS + 2):
                        masked(n + v // ARS, n * ARS + v, v % ARS)
                maximum(B - 1, 1)
                weight(B - 2, 0)
                dve.wait_ge(col_done, 6 + 2 * (B * L + B - 2))
                weight(B - 1, 1)
                dve.wait_ge(col_done, 6 + 2 * B * (L + 1))
                nc.vector.tensor_scalar(ROWS, PS[:, 4:6, 0:CW], 1.0 / N, None, ALU.mult).then_inc(rows_ready, 1)

                link(nc.vector.tensor_tensor(XN, FEAT[:, :, :], per_node(T_B), ALU.mult))

                dve.wait_ge(rows_psum, L + 1)
                link(nc.vector.tensor_scalar(T_A[:, :], PS[:, 6, 0:B], 0.5, None, ALU.mult))
                link(nc.vector.tensor_scalar(IMP[:, :], STR[:, :], 0.5, None, ALU.mult))
                link(nc.vector.tensor_tensor(IMP[:, :], IMP[:, :], T_A[:, :], ALU.add))

                def node_softmax(g, dst):
                    link(nc.vector.tensor_tensor(IMP[:, :], IMP[:, :], valid[:, :], ALU.mult))
                    link(nc.vector.tensor_tensor(IMP[:, :], IMP[:, :], far[:, :], ALU.add))
                    across(nc.vector.tensor_reduce(G1[:, g:g + 1], IMP[:, :], AX, ALU.max))
                    ask(nc.vector.tensor_scalar(G1[:, g + 1:g + 2], G1[:, g + 1:g + 2], -1.0, None, ALU.mult))
                    across(nc.vector.tensor_copy(G1[:, g + 2:g + 3], G1[:, g + 2:g + 3]))
                    link(nc.vector.tensor_scalar(G1[:, g + 3:g + 4], G1[:, g + 3:g + 4], TH[L], None, ALU.mult))
                    link(nc.vector.tensor_scalar(dst, EXPN[:, :], G1[:, g + 3:g + 4], None, ALU.is_ge))

                node_softmax(0, COMP[:, :])

                for g in range(GROUPS):
                    lo, hi = 4 * g, 4 * g + len(group(g))
                    nc.vector.tensor_tensor(DUP[:, lo:hi, 0:D], XN[:, lo:hi, :], per_node(COMP)[:, lo:hi, :],
                                            ALU.mult).then_inc(dup_first, 1)
                def stack(g):
                    c = slice(4 * P * g, 4 * P * g + len(group(g)) * P)
                    dve.wait_ge(c_low, GROUPS * L + g + 1)
                    return nc.vector.tensor_copy(CA[D:2 * D, c], C22[D:2 * D, c])

                for g in range(GROUPS):
                    w = len(group(g)) * P
                    c = slice(4 * P * g, 4 * P * g + w)
                    dve.wait_ge(c_high, GROUPS * L + g + 1)
                    nc.vector.scalar_tensor_tensor(C22[:, c], PS[:, g, 0:w], COS_SCALE, C11[:, c],
                                                   ALU.mult, ALU.subtract).then_inc(c_low, 1)
                    if g:
                        stack(g - 1)
                stack(GROUPS - 1).then_inc(stacks_ready, 1)
                link(nc.vector.tensor_scalar(OFF[:, :], DEG[:, :], -0.5 * TH[L], 0.5 * TH[L] * N, ALU.mult, ALU.add))
                link(nc.vector.tensor_scalar(T_A[:, :], COMP[:, :], -FAR, FAR, ALU.mult, ALU.add))
                nc.vector.tensor_tensor(OFF[:, :], OFF[:, :], T_A[:, :], ALU.add).then_inc(off_ready, 1)
                dve.wait_ge(off_ready, L + 1)
                link(nc.vector.tensor_tensor(FMAG[:, :], FMAG[:, :], COMP[:, :], ALU.mult))
                link(nc.vector.tensor_scalar(FMAG[:, :], FMAG[:, :], NORM_MIN ** 0.5, None, ALU.max))

                def prune(n, i, v):
                    u = v % 2
                    t = i + B * L
                    dve.wait_ge(hp_stored[u], n * (8 * RS) + (B // 2 * L + v // 2 + 1) * 16)
                    if v == 0:
                        dve.wait_ge(conn_done, n + ((ROUNDS + 1) * L + 1))
                    hold(dve, "dve", thr_done, t + 1)
                    nc.vector.tensor_scalar(HPST[:, u, :].bitcast(FP8), ATT[u], THR[:, u:u + 1], None,
                                            ALU.is_ge, ALU.add, accum_out=CN[:, v:v + 1],
                                            saturate=False).then_inc(hp_ready, 1)
                    if v == RS - 1 or (isinstance(i, int) and i == B - 1):
                        hold(dve, "dve", hp_ready, t + 3)
                        nc.vector.tensor_copy(CONN[:, bass.ds(i - v, v + 1)], CN[:, 0:v + 1]).then_inc(conn_done, 1)

                all_tiles(dve, prune)
                dve.wait_ge(conn_done, 1 + (ROUNDS + 1) * (L + 1))

                link(nc.vector.tensor_tensor(IMP[:, :], CONN[:, :], FMAG[:, :], ALU.mult))
                node_softmax(4, NMASK[:, :])
                link(nc.vector.tensor_scalar(T_B[:, :], CONN[:, :], 0.0, None, ALU.is_gt))
                link(nc.vector.tensor_tensor(NMASK[:, :], NMASK[:, :], T_B[:, :], ALU.mult))
                link(nc.vector.tensor_tensor(NMASK[:, :], NMASK[:, :], COMP[:, :], ALU.mult))
                ask(nc.vector.tensor_scalar(T_A[:, :], CONN[:, :], EPS, None, ALU.max))
                link(nc.vector.reciprocal(DV[:, :], DV[:, :]))
                link(nc.vector.tensor_tensor(NMASK[:, :], NMASK[:, :], DV[:, :], ALU.mult))
                for lo, hi in SPLIT_HALF:
                    nc.vector.tensor_tensor(TMP1[:, lo:hi, :], XW[:, lo:hi, :], per_node(NMASK)[:, lo:hi, :],
                                            ALU.mult).then_inc(t_ready, 1)
                for k, (lo, hi) in enumerate(SPLIT_HALF):
                    dve.wait_ge(high_ready, 4 * L + k + 1)
                    last = nc.vector.scalar_tensor_tensor(HALVES[:, lo:hi, D:2 * D], TMP1[:, lo:hi, :], ST[:, 2:3],
                                                          HALVES[:, lo:hi, 0:D], ALU.mult, ALU.subtract)
                last.then_inc(parts_ready, 1)
                dve.wait_ge(parts_ready, 3 * L + 2)
                link(nc.vector.tensor_scalar(DV[:, :], DV[:, :], ST[:, 3:4], None, ALU.mult))

                for hf, (lo, hi) in enumerate(SPLIT_HALF):
                    dve.wait_ge(g_used, RS + B * (2 * L + hf + 1))
                    for bank in range((HB + 2) // 3):
                        nb = min(3, HB - 3 * bank)
                        b = lo + 3 * bank
                        src = PS[:, (bank + 5 * hf) % 8, 0:nb * EW].rearrange("p (b c) -> p b c", b=nb)
                        nc.vector.tensor_copy(EDEG[:, b:b + nb], src[:, :, 2 * D])
                        nc.vector.tensor_reduce(TMP1[:, b:b + nb, :],
                                                       src[:, :, 0:2 * D].rearrange("p b (t d) -> p b d t", t=2), AX,
                                                       ALU.add).then_inc(half_evac, 1)
                    dve.wait_ge(half_evac, 5 * (2 * L + hf + 1))
                    link(nc.vector.tensor_scalar(EDEG[:, lo:hi], EDEG[:, lo:hi], EPS, None, ALU.max))
                    link(nc.vector.reciprocal(EDEG[:, lo:hi], EDEG[:, lo:hi]))
                    nc.vector.tensor_tensor(TMP1[:, lo:hi, :], TMP1[:, lo:hi, :], per_node(EDEG)[:, lo:hi, :],
                                            ALU.mult).then_inc(t_ready, 1)
                    dve.wait_ge(high_ready, 4 * L + hf + 3)
                    last = nc.vector.tensor_tensor(AHALVES[:, lo:hi, D:2 * D], TMP1[:, lo:hi, :],
                                                   AHALVES[:, lo:hi, 0:D], ALU.subtract)
                last.then_inc(parts_ready, 1)
                dve.wait_ge(parts_ready, 3 * L + 3)

                def tile_out(n, i, v):
                    u = v % 2
                    t = i + B * L
                    dve.wait_ge(msg_done, t + 1)
                    for g in (0, 2):
                        hold(dve, "dve", m_psum, t * PAIRS + (g + 1 + RS * PAIRS))
                        nc.vector.tensor_copy(HPT[u][:, 8 * P * g:8 * P * (g + 1)],
                                              PS[:, TILES_AT[g]:TILES_AT[g] + 2, :].rearrange("p k c -> p (k c)")).then_inc(m_vec, 1)

                def message(i, v):
                    hold(dve, "dve", msg_done, i + (B * L + 3))
                    nc.vector.tensor_reduce(FEAT[:, bass.ds(i, 1), :],
                                            PS[:, 6, 0:2 * D].rearrange("p (o t d) -> p o d t", o=1, t=2),
                                            AX, ALU.add).then_inc(msg_taken, 1)

                all_tiles_ahead(dve, tile_out, message)
                dve.wait_ge(msg_taken, 1 + B * (L + 1))
                features_out()
                def add_out(g):
                    lo, hi = 4 * g, 4 * g + len(group(g))
                    dve.wait_ge(prod_evac, GROUPS * L + g + 1)
                    return nc.vector.tensor_tensor(X[:, lo:hi, :], X[:, lo:hi, :], FEAT[:, lo:hi, :], ALU.add)

                for g, lo, hi in products():
                    nc.vector.scalar_tensor_tensor(FEAT[:, lo:hi, :],
                                                   PS[:, g, 0:(hi - lo) * D].rearrange("p (b d) -> p b d", d=D), 0.0,
                                                   per_node(DV)[:, lo:hi, :], ALU.max, ALU.mult).then_inc(prod_evac, 1)
                    if L == LAYERS - 1 and g:
                        add_out(g - 1)
                if L == LAYERS - 1:
                    add_out(GROUPS - 1).then_inc(feat_ready, 1)
                else:
                    dve.wait_ge(prod_evac, GROUPS * (L + 1))
                    dve.sem_inc(feat_ready)

        @block.tensor
        def _(pe):
            pe.sem_inc(cols_used, NCH)
            pe.sem_inc(count_ready, 2)
            pe.sem_inc(acc_done, 2)
            pe.sem_inc(e_used, RS)
            pe.sem_inc(col_done, 6)
            pe.sem_inc(g_used, RS)
            pe.sem_inc(m_psum, RS * PAIRS)
            pe.sem_inc(msg_done, 2)
            xts = [0]

            def features(ready):
                for g in range(GROUPS):
                    ready(g)
                    for k, b in enumerate(group(g)):
                        last = nc.tensor.transpose(PS[0:D, g, k * P:(k + 1) * P], FEAT[:, b, :], identF[:, :])
                    last.then_inc(xt_psum, 1)

            def normalised(n):
                def ready(g):
                    if n and g == GROUPS - 1:
                        pe.wait_ge(deg_taken, 2)
                    for k, (lo, hi) in enumerate(SPLIT):
                        if 4 * g == lo:
                            pe.wait_ge(feat_ready, n + k + 1)
                return ready

            def product(w, xt=XT):
                cols = w.shape[1]
                for g in range(GROUPS):
                    if g % 2 == 0:
                        pe.wait_ge(xt_ready, xts[0] * ((GROUPS + 1) // 2) + g // 2 + 1)
                    else:
                        pe.wait_ge(xt_ready_act, xts[0] * (GROUPS // 2) + g // 2 + 1)
                    for k, b in enumerate(group(g)):
                        last = nc.tensor.matmul(PS[:, g, k * cols:(k + 1) * cols], xt[:, b * P:(b + 1) * P], w,
                                                start=True, stop=True)
                    last.then_inc(prod_psum, 1)
                xts[0] += 1

            def zero_bank(bank, w):
                return nc.tensor.matmul(PS[:, bank, 0:w], zeros[:, 0:P], zeros[:, 0:w], start=True, stop=True)

            def add(o, lhsT, rhs):
                return nc.tensor.matmul(o, lhsT, rhs, start=False, stop=True, skip_group_check=True)

            pe.wait_ge(constants_ready, CONSTANTS)
            features(normalised(0))
            pe.wait_ge(w0_loaded, 16)
            product(w0[:, :])
            pe.wait_ge(support_ready, GROUPS)

            def l0_group(sg, nb):
                def accumulate(s, inc_cols):
                    jb = B - 1 - s
                    pe.wait_ge(w_ready, sg * (2 * B) + (2 * s + 2))
                    for b in range(nb):
                        h = int(b >= halves(nb)[1][0])
                        k = b - halves(nb)[h][0]
                        o = (b % 4) * 2 * D
                        last = add(PS[:, 4 + b // 4, o:o + 2 * D],
                                   WTR[:, h, s % 2, k * P:(k + 1) * P].bitcast(BF16), HALVES[:, jb, :])
                        if b == 0 and inc_cols:
                            last.then_inc(cols_used, 1)
                    last.then_inc(acc_done, 1)

                def transpose(s, h):
                    jb = B - 1 - s
                    c = CHUNK_OF[s]
                    if h == 0 and s == CHUNK_AT[c]:
                        pe.wait_ge(cast_done, sg * NCH + (RING + c + 1))
                    hold(pe, "pe", ht_ready, sg * (2 * B) + (2 * s + h + 1))
                    b0, nh = halves(nb)[h]
                    for k in range(nh):
                        last = nc.tensor.matmul(PS[:, HT_AT[h][s % 2], k * P:(k + 1) * P],
                                                HS[:, b0 + k, jb * P:(jb + 1) * P].bitcast(FP8),
                                                half_ident[:, :], start=True, stop=True)
                    last.then_inc(ht_psum, 1)

                def count(s, h):
                    pe.wait_ge(ht_ready, sg * (2 * B) + (2 * s + h + 5))
                    w = halves(nb)[h][1] * P
                    tile = HTR[:, h, s % 4, 0:w]
                    if s == 0:
                        if h == 0:
                            pe.wait_ge(deg_rows, sg + 1)
                        last = nc.tensor.matmul(PS[:, 2 + h, 0:w], count_first[:, :], tile, start=True, stop=True)
                    else:
                        pe.wait_ge(w_ready, sg * (2 * B) + (2 * s + h - 1))
                        add(PS[:, 2 + h, 0:w], count_next[:, :], HTR[:, h, (s - 1) % 4, 0:w])
                        last = add(PS[:, 2 + h, 0:w], count_first[:, :], tile)
                    last.then_inc(count_ready, 1)

                for s in range(2):
                    for h in range(2):
                        transpose(s, h)
                for s in range(B):
                    for h in range(2):
                        count(s, h)
                        if s + 2 < B:
                            transpose(s + 2, h)
                    if s == 1:
                        pe.wait_ge(acc_free, sg + 1)
                        for k in range((nb + 3) // 4):
                            last = zero_bank(4 + k, 4 * 2 * D)
                        last.then_inc(cols_used, 3)
                    if s:
                        accumulate(s - 1, s + 3 in CHUNK_AT or s + 3 == B)
                accumulate(B - 1, False)
                for h in range(2):
                    w = halves(nb)[h][1] * P
                    last = add(PS[:, 2 + h, 0:w], count_next[:, :], HTR[:, h, (B - 1) % 4, 0:w])
                last.then_inc(deg_psum, 1)

            with pe.Fori(0, NSG) as sg:
                l0_group(sg, SG)
            l0_group(NSG, TAIL)

            def doubled(L):
                for g in range(GROUPS):
                    pe.wait_ge(dup_ready, GROUPS * L + g + 1)
                    for j, b in enumerate(group(g)):
                        last = nc.tensor.transpose(PS[:, g, j * P:(j + 1) * P], DUP[:, b, :], identF[:, :])
                    last.then_inc(dup_psum, 1)

            pe.wait_ge(weights_loaded, 144)
            pe.wait_ge(deg_rows, NSG + 2)
            pe.wait_ge(acc_free, NSG + 2)
            for h in range(2):
                for j in range(NSG * halves(SG)[h][1] + halves(TAIL)[h][1]):
                    last = nc.tensor.matmul(PS[:, 7 - h, j:j + 1], DEG_ROWS[32 * h:32 * h + 1, j * P:(j + 1) * P],
                                            ones[32 * h:32 * h + 1, :], start=True, stop=True)
                last.then_inc(deg_psum, 1)

            for L in range(LAYERS):
                features(normalised(2) if L == 0 else lambda g: g or pe.wait_ge(feat_ready, 5))
                pe.wait_ge(ones_row, L + 1)
                product(wwv[:, :], XT1)
                pe.wait_ge(parts_ready, 3 * L + 1)
                for g in range(GROUPS):
                    zero_bank(g, len(group(g)) * P)

                for i in range(B):
                    pe.wait_ge(e_row_ready, B * L + i + 1)
                    for g in range(GROUPS):
                        w = len(group(g)) * P
                        last = add(PS[:, g, 0:w], PROW[:, i % RS, 0:2 * D],
                                   H[:, i, 4 * P * g:4 * P * g + w].bitcast(FP8))
                    last.then_inc(e_used, 1)
                    if i % 2 == 0 and i // 2 < GROUPS:
                        g = i // 2
                        w = len(group(g)) * P
                        if L or g:
                            pe.wait_ge(q_evac, GROUPS * L + g)
                        nc.tensor.matmul(PS[:, 7, 0:w], wqq[:, :], XT1[:, 4 * P * g:4 * P * g + w],
                                         start=True, stop=True).then_inc(q_psum, 1)
                pe.wait_ge(q_evac, GROUPS * (L + 1))
                for g in range(GROUPS):
                    w = len(group(g)) * P
                    if g % 2 == 0:
                        pe.wait_ge(et_evac, (GROUPS + 1) // 2 * L + g // 2 + 1)
                    else:
                        pe.wait_ge(et_evac_act, GROUPS // 2 * L + g // 2 + 1)
                    nc.tensor.matmul(PS[:, g, 0:w], fold[:, :], ATT0[:, 4 * P * g:4 * P * g + w],
                                     start=True, stop=True).then_inc(fold_psum, 1)

                def scores(i, q):
                    pe.wait_ge(s_masked, i * PAIRS + (B * L * PAIRS + SCORES_WAIT[q]))
                    for rhs in (E11, E22):
                        for k in range(2):
                            c = 2 * q + k
                            last = nc.tensor.matmul(PS[:, SCORES_AT[q] + k, 0:CW], QA[:, bass.ds(i * P, P)],
                                                    rhs[:, c * CW:(c + 1) * CW], start=rhs is E11, stop=rhs is E22)
                    last.then_inc(s_psum, 1)

                def column_sums(i, v, k):
                    if k == 0:
                        pe.wait_ge(rz_ready, i + (B * L + 1))
                    for q in range(4):
                        c = 4 * k + q
                        last = add(PS[32 * q:32 * q + 1, 4 + k, 0:CW], RZ[:, v % 2:v % 2 + 1],
                                   SCORES[v % 3][:, c * CW:(c + 1) * CW])
                    last.then_inc(col_done, 1)

                def attention(i, v, sums=True, last=False):
                    scores(i, 1)
                    scores(i, 2)
                    if sums:
                        column_sums(i - 2, (v - 2) % ARS, 0)
                    scores(i, 3)
                    if not last:
                        scores(i + 1, 0)
                    if sums:
                        column_sums(i - 2, (v - 2) % ARS, 1)

                pe.wait_ge(stacks_ready, 2 * L + 1)
                for bank in (4, 5):
                    zero_bank(bank, CW)
                scores(0, 0)
                for i in range(2):
                    attention(i, i, sums=False)
                with pe.Fori(0, AROUNDS - 1) as n:
                    for v in range(2, ARS + 2):
                        attention(n * ARS + v, v % ARS)
                for i in range(B - ARS, B):
                    attention(i, i % ARS, last=i == B - 1)
                for i in range(B - 2, B):
                    for k in range(2):
                        column_sums(i, i % ARS, k)
                pe.wait_ge(rows_back, 16 * (L + 1))
                nc.tensor.transpose(PS[:, 6, 0:B], ATR[:, :], identF[0:B, 0:B]).then_inc(rows_psum, 1)

                doubled(L)
                pe.wait_ge(stacks_ready, 2 * L + 2)

                def cosines(n, i, v):
                    pe.wait_ge(g_ready, i + (B * L + 1 + RS))
                    for q in range(2):
                        hold(pe, "pe", exp_done, i * 2 + (2 * B * L + q + 1))
                        for k in range(4):
                            c = 4 * q + k
                            nc.tensor.matmul(PS[:, c, 0:CW], mask_ident[:, :],
                                             GST[:, v, c * CW:(c + 1) * CW].bitcast(FP8), start=True, stop=False)
                        for rhs in (C11, C22):
                            for k in range(4):
                                c = 4 * q + k
                                last = nc.tensor.matmul(PS[:, c, 0:CW], CA[:, bass.ds(i * P, P)],
                                                        rhs[:, c * CW:(c + 1) * CW], start=False, stop=rhs is C22)
                        last.then_inc(cos_psum, 1)

                all_tiles(pe, cosines)

                pe.wait_ge(parts_ready, 3 * L + 2)
                for hf in range(2):
                    for k in range((HB + 2) // 3):
                        bank = (k + 5 * hf) % 8
                        if hf and bank < 5:
                            pe.wait_ge(half_evac, 10 * L + bank + 1)
                        zero_bank(bank, min(3, HB - 3 * k) * EW)

                    def edges(n, i, v):
                        k = (v // 2 + hf) % 4
                        u = 2 * k + v % 2
                        pe.wait_ge(tiles_loaded[k], loaded_at(L, 2 + hf, n, k))
                        hold(pe, "pe", g_row_ready, i + (B * (2 * L + hf) + 1))
                        for j in range(HB):
                            o = (j % 3) * EW
                            last = add(PS[:, (j // 3 + 5 * hf) % 8, o:o + EW], HSTH[:, u, j * P:(j + 1) * P].bitcast(FP8),
                                       PROW[:, (v + 2 * hf) % RS, 0:EW])
                        last.then_inc(g_used, 1)

                    all_tiles(pe, edges, HRS)

                def transposes(n, i, v):
                    for g in range(PAIRS):
                        if g == 0:
                            pe.wait_ge(tiles_loaded[v // 2], loaded_at(L, 4, n, v // 2))
                        hold(pe, "pe", (m_vec, m_act)[g % 2], i * 2 + (2 * B * L + g // 2 + 1))
                        for b in range(8 * g, min(8 * g + 8, B)):
                            last = nc.tensor.matmul(PS[:, TILES_AT[g] + (b % 8) // 4, (b % 4) * P:(b % 4 + 1) * P],
                                                    HST[:, v, b * P:(b + 1) * P].bitcast(FP8), ident[:, :],
                                                    start=True, stop=True)
                        last.then_inc(m_psum, 1)

                def messages(i, v):
                    pe.wait_ge(m_vec, i * 2 + (2 * B * L + 4))
                    pe.wait_ge(m_act, i * 2 + (2 * B * L + 4))
                    pe.wait_ge(msg_taken, i + (B * L + 1))
                    for b in range(B):
                        last = nc.tensor.matmul(PS[:, 6, 0:2 * D], HPT[v % 2][:, b * P:(b + 1) * P],
                                                AHALVES[:, b, :], start=b == 0, stop=b == B - 1)
                    last.then_inc(msg_done, 1)

                pe.wait_ge(parts_ready, 3 * L + 3)
                all_tiles_ahead(pe, transposes, messages)
                features(lambda g: pe.wait_ge(msg_taken, 1 + B * L + 4 * g + len(group(g))))
                product(wth[:, :])


CONSTANTS = 31

_INS = ["x", "adj", "L0_gnn_weight", "L0_gnn_bias", "L1_gnn_W", "L1_gnn_Theta", "L1_gnn_Wq", "L1_gnn_bq",
        "L1_gnn_Wv", "L1_gnn_bv"]
_OUTS = [((3327, 64), "float32")]


def kernel(**inputs):
    import numpy as _np
    import concourse.bacc as _bacc
    from concourse import mybir as _mybir
    from concourse.bass_utils import run_bass_kernel_spmd as _run

    nc = _bacc.Bacc("TRN2", target_bir_lowering=False, num_devices=1)
    arrays, args = {}, []
    for name in _INS:
        a = _np.ascontiguousarray(inputs[name])
        arrays[f"in_{name}_dram"] = a
        args.append(nc.dram_tensor(f"in_{name}_dram", a.shape, _mybir.dt.from_np(a.dtype), kind="ExternalInput").ap())
    for i, (shape, dtype) in enumerate(_OUTS):
        dt = _mybir.dt.from_np(_np.dtype(dtype))
        args.append(nc.dram_tensor(f"out_{i}_dram", shape, dt, kind="ExternalOutput").ap())
    bass_adj_preln_gnn_hypergraph(nc, *args)
    r = _run(nc, [arrays], core_ids=[0])
    return r.results[0]["out_0_dram"]
```
